# Optimizing a Trainium2 kernel written in Bass

```python
import numpy as np
import jax
import jax.numpy as jnp

def _softmax(x, axis=-1):
    return jax.nn.softmax(x, axis=axis)

def _gelu(x):
    return jax.nn.gelu(x, approximate=True)

def _silu(x):
    return jax.nn.silu(x)

def _sigmoid(x):
    return jax.nn.sigmoid(x)

def _layernorm(x, axis=-1, eps=1e-05):
    m = jnp.mean(x, axis=axis, keepdims=True)
    v = jnp.var(x, axis=axis, keepdims=True)
    return (x - m) / jnp.sqrt(v + eps)

def _scatter_add(tgt, idx, src, axis=0):
    return tgt.at[idx].add(src)

def _segment_sum(src, seg, n):
    return jax.ops.segment_sum(src, seg, n)
kernel_name = 'mk_gnn_preln_d2_gnn_r32_6ebe54'

def setup_inputs(seed: int=0):
    np.random.seed(seed)
    _w = jnp.asarray

    def _rec_inputs():
        import jax
        import jax.numpy as jnp
        _gk = jax.random.key(seed)
        x = -0.0005121 + 1.001 * jax.random.normal(jax.random.fold_in(_gk, 1), (3125, 32), jnp.float32)
        _s = jax.random.randint(jax.random.fold_in(_gk, 2), (50000,), 0, 3125, jnp.int32)
        _d = jax.random.randint(jax.random.fold_in(_gk, 3), (50000,), 0, 3125, jnp.int32)
        _loop = jnp.arange(3125, dtype=jnp.int32)
        src = jnp.concatenate([_s, _d, _loop])
        dst = jnp.concatenate([_d, _s, _loop])
        _o = jnp.argsort(dst, stable=True)
        src = src[_o]
        dst = dst[_o]
        edge_attr_32 = 0.000196303 + 1.00016 * jax.random.normal(jax.random.fold_in(_gk, 11), (103125, 32), jnp.float32)
        return (x, src, dst, edge_attr_32)
    x, src, dst, edge_attr_32 = _rec_inputs()

    def _L0_gnn_setup():
        import jax, jax.numpy as jnp
        import numpy as np
        N_NODES = 3125
        N_EDGES = 50000
        D = 32
        H = 2 * D
        EPS = 1e-07

        def _edge_softmax(logits, dst, num_nodes):
            m = jax.ops.segment_max(logits, dst, num_segments=num_nodes)
            e = jnp.exp(logits - m[dst])
            s = jax.ops.segment_sum(e, dst, num_segments=num_nodes)
            return e / s[dst]
        key = jax.random.key(seed)
        ks = jax.random.split(key, 6)
        x = jax.random.normal(ks[0], (N_NODES, D), dtype=jnp.float32)
        edge_index = jax.random.randint(ks[1], (2, N_EDGES), 0, N_NODES, dtype=jnp.int64)
        beta = jnp.ones((1,), dtype=jnp.float32)
        W1 = jax.random.normal(ks[2], (D, H), dtype=jnp.float32) * (1.0 / np.sqrt(D))
        b1 = jnp.zeros((H,), dtype=jnp.float32)
        W2 = jax.random.normal(ks[3], (H, D), dtype=jnp.float32) * (1.0 / np.sqrt(H))
        b2 = jnp.zeros((D,), dtype=jnp.float32)
        return {'x': x, 'edge_index': edge_index, 'beta': beta, 'W1': W1, 'b1': b1, 'W2': W2, 'b2': b2}
    _L0_gnn_all = _L0_gnn_setup()
    _L0_gnn_in = {k: v for k, v in _L0_gnn_all.items() if k in ('beta', 'W1', 'b1', 'W2', 'b2')}
    del _L0_gnn_all

    def _L1_gnn_setup():
        import jax, jax.numpy as jnp
        import numpy as np
        N_NODES = 50000
        N_EDGES = 25000
        X_DIM = 32
        E_DIM = 32
        HID = 64
        OUT = 32
        key = jax.random.key(seed)
        ks = jax.random.split(key, 6)
        x = jax.random.normal(ks[0], (N_NODES, X_DIM), dtype=jnp.float32)
        edge_index = jax.random.randint(ks[1], (2, N_EDGES), 0, N_NODES, dtype=jnp.int64)
        edge_attr = jax.random.normal(ks[2], (N_EDGES, E_DIM), dtype=jnp.float32)
        in_dim = 2 * X_DIM + E_DIM
        W1 = jax.random.normal(ks[3], (in_dim, HID), dtype=jnp.float32) * (1.0 / np.sqrt(in_dim))
        b1 = jnp.zeros((HID,), dtype=jnp.float32)
        W2 = jax.random.normal(ks[4], (HID, OUT), dtype=jnp.float32) * (1.0 / np.sqrt(HID))
        b2 = jnp.zeros((OUT,), dtype=jnp.float32)
        return {'x': x, 'edge_index': edge_index, 'edge_attr': edge_attr, 'W1': W1, 'b1': b1, 'W2': W2, 'b2': b2}
    _L1_gnn_all = _L1_gnn_setup()
    _L1_gnn_in = {k: v for k, v in _L1_gnn_all.items() if k in ('W1', 'b1', 'W2', 'b2')}
    del _L1_gnn_all
    return {'x': x, 'src': src, 'dst': dst, 'edge_attr_32': edge_attr_32, 'L0_gnn_beta': _L0_gnn_in['beta'], 'L0_gnn_W1': _L0_gnn_in['W1'], 'L0_gnn_b1': _L0_gnn_in['b1'], 'L0_gnn_W2': _L0_gnn_in['W2'], 'L0_gnn_b2': _L0_gnn_in['b2'], 'L1_gnn_W1': _L1_gnn_in['W1'], 'L1_gnn_b1': _L1_gnn_in['b1'], 'L1_gnn_W2': _L1_gnn_in['W2'], 'L1_gnn_b2': _L1_gnn_in['b2']}

def reference(x, src, dst, edge_attr_32, L0_gnn_beta, L0_gnn_W1, L0_gnn_b1, L0_gnn_W2, L0_gnn_b2, L1_gnn_W1, L1_gnn_b1, L1_gnn_W2, L1_gnn_b2):
    import jax
    import jax.numpy as jnp

    def _L0_gnn_ref(x, edge_index, beta, W1, b1, W2, b2):
        import jax, jax.numpy as jnp
        import numpy as np
        N_NODES = 3125
        N_EDGES = 50000
        D = 32
        H = 2 * D
        EPS = 1e-07

        def _edge_softmax(logits, dst, num_nodes):
            m = jax.ops.segment_max(logits, dst, num_segments=num_nodes)
            e = jnp.exp(logits - m[dst])
            s = jax.ops.segment_sum(e, dst, num_segments=num_nodes)
            return e / s[dst]
        n = x.shape[0]
        dst = edge_index[0]
        src = edge_index[1]
        edge_msg = jax.nn.relu(x[src]) + EPS
        alpha = _edge_softmax(beta * edge_msg, dst, n)
        h = jax.ops.segment_sum(edge_msg * alpha, dst, num_segments=n)
        h = jax.nn.relu(h @ W1 + b1) @ W2 + b2
        return h

    def _L1_gnn_ref(x, edge_index, edge_attr, W1, b1, W2, b2):
        import jax, jax.numpy as jnp
        import numpy as np
        N_NODES = 50000
        N_EDGES = 25000
        X_DIM = 32
        E_DIM = 32
        HID = 64
        OUT = 32
        num_nodes = x.shape[0]
        rol, col = (edge_index[0], edge_index[1])
        e_feat = jnp.concatenate([x[rol], x[col], edge_attr], axis=-1)
        h = jax.nn.relu(e_feat @ W1 + b1)
        v = h @ W2 + b2
        x_cand = jax.ops.segment_max(v, col, num_segments=num_nodes)
        return jnp.maximum(x_cand, x[:, -v.shape[-1]:])
    edge_index = jnp.stack([src, dst])
    h = jnp.maximum(_layernorm(x, axis=-1), 0.0)
    x = x + _L0_gnn_ref(h, edge_index, L0_gnn_beta, L0_gnn_W1, L0_gnn_b1, L0_gnn_W2, L0_gnn_b2)
    h = jnp.maximum(_layernorm(x, axis=-1), 0.0)
    x = x + _L1_gnn_ref(h, edge_index, edge_attr_32, L1_gnn_W1, L1_gnn_b1, L1_gnn_W2, L1_gnn_b2)
    return x

_drawn_inputs = setup_inputs


def setup_inputs(seed=0):
    import zlib

    import numpy as np

    out = dict(_drawn_inputs(seed))
    spreads = {'L0_gnn_b1': (0.0, 0.1),
     'L0_gnn_b2': (0.0, 0.1),
     'L1_gnn_b1': (0.0, 0.302),
     'L1_gnn_b2': (0.0, 0.1)}
    factors = {}
    for name, (base, spread) in spreads.items():
        noise = np.random.default_rng([zlib.crc32(name.encode()), seed]).standard_normal(out[name].shape)
        drawn = base * np.exp(spread * noise) if base else spread * noise
        out[name] = jnp.asarray(drawn.astype(out[name].dtype))
    for name, factor in factors.items():
        out[name] = (out[name] * factor).astype(out[name].dtype)
    return out
```

```python
from contextlib import ExitStack

import concourse.bass as bass
from concourse import mybir

P = 128
N, D, H, E = 3125, 32, 64, 103125
NB = (N + P - 1) // P
NP = NB * P
MSG_EPS, LN_EPS = 1e-7, 1e-5

HI = 8
LO = (N + HI - 1) // HI
TILES = (E + P - 1) // P
GT = 3
W0 = P // HI
GROUPS = (TILES + GT - 1) // GT
ATILES = GT * GROUPS
CHUNK = P // W0
CHUNKS = (GROUPS + CHUNK - 1) // CHUNK
CT = GT * CHUNK
TAIL_GROUPS = GROUPS - CHUNK * (CHUNKS - 1)
PAIRS = CHUNKS // 2 - 1
Q = TILES * 32
HALF = (16, 15)
STEP = sum(HALF)
STEPS = TILES // STEP
W1 = 32
HALVES = 2 * STEPS
EPAD = 4 * Q
NO_DST = 8191
BIG = 3.0e38
RANGE = 60.0
NOT_FOUND = 1 << 20
COUNT_MAX = 256
GE = 125
GCHUNKS = E // GE
assert E % GE == 0
RING = 8
SIGN_PAIRS = STEPS // 2
assert TILES % STEP == 0 and CHUNKS % 2 == 0 and 2 * SIGN_PAIRS == STEPS and SIGN_PAIRS <= PAIRS


def build(nc, xb, src0, dst0, srcq, dstq, eat, base0, base0c, last0, base1, last1, next1, slast, dstp, src, dst, ea,
          beta, w01, b01, w02, b02, w11, b11, w12, b12, out):
    f32, f16, bf16, i32 = mybir.dt.float32, mybir.dt.float16, mybir.dt.bfloat16, mybir.dt.int32
    ALU, ACT, AX = mybir.AluOpType, mybir.ActivationFunctionType, mybir.AxisListType.X
    ds = bass.ds
    ctx = ExitStack()
    with ctx:
        def sb(name, shape, dt):
            return ctx.enter_context(nc.sbuf_tensor(name, shape, dt))

        def sem(name):
            return ctx.enter_context(nc.semaphore(name))

        g_dram = nc.dram_tensor("g_dram", (NP + 1, 3 * H), bf16).ap()
        h_dram = nc.dram_tensor("h_dram", (NP, D), f32).ap()
        v_dram = nc.dram_tensor("v_dram", (P * TILES, D), f32).ap()
        end_dram = nc.dram_tensor("end_dram", (NP, 1), i32).ap()

        ident = sb("ident", [P, P], f32)
        diff_i = sb("diff_i", [P, P], f32)
        lo_iota = sb("lo_iota", [P, LO + 1], f16)
        part = sb("part", [P, 1], i32)
        part16 = sb("part16", [P, 1], i32)
        part32 = sb("part32", [P, 1], i32)
        part32f = sb("part32f", [P, 1], f32)
        part16f = sb("part16f", [P, 1], f32)
        node_id = sb("node_id", [P, NB], f32)
        ones = sb("ones", [P, P], f32)
        zero_b = sb("zero_b", [P, 512], bf16)
        w01d = sb("w01d", [P, 2, P], f32)
        w02d = sb("w02d", [P, 2, P], f32)
        w1sd = sb("w1sd", [P, 2, P], f32)
        w1dd = sb("w1dd", [P, 2, P], f32)
        w1ed = sb("w1ed", [P, 2, P], f32)
        w12d = sb("w12d", [P, 2, P], f32)
        b01c = sb("b01c", [P, 1], f32)
        b11c = sb("b11c", [P, 1], f32)
        b02r = sb("b02r", [P, D], f32)
        b12r = sb("b12r", [P, D], f32)
        betac = sb("betac", [P, 1], f32)
        x = sb("x", [P, NB, D], f32)
        xc = sb("xc", [P, NB, D], f32)
        sq = sb("sq", [P, NB, D], f32)
        stat = sb("stat", [P, 4, NB], f32)
        h = sb("h", [P, NB, D], f32)
        logit = sb("logit", [P, NB, D], f32)
        g = sb("g", [P, NB, 2, D], f32)
        gs = sb("gs", [P, NB, 3, H], bf16)
        ext = sb("ext", [P, 2, D], f32)
        top = sb("top", [H, 1], f32)
        topd = sb("topd", [H, H], f32)
        topb = sb("topb", [P, 2, D], f32)
        hT = sb("hT", [P, NB * D], f32)
        mT = sb("mT", [P, 2, NB * D], f32)
        x1 = sb("x1", [P, NB, D], f32)
        scan_bufs = sb("scan_bufs", [P, 8 * 512], f32)
        src_i, dst_i = (scan_bufs[:, ATILES * n:ATILES * n + ATILES].bitcast(i32) for n in range(2))
        keys = sb("keys", [P, 5, ATILES], f32)
        srcf, hif, key_win, key_lo = keys[:, 0, :], keys[:, 1:3, :], keys[:, 3, :], keys[:, 4, :]
        base0_i = sb("base0_i", [P, GROUPS], i32)
        gidx_b = sb("gidx_b", [P, CHUNKS], i32)
        gidx = sb("gidx", [P, CHUNKS], i32)
        grow = sb("grow", [P, CHUNKS, 3 * H], bf16)
        oh_win = sb("oh_win", [P, RING, P], f16)
        oh_lo = sb("oh_lo", [P, RING, LO + 1], f16)
        cg = sb("cg", [P, CHUNK, LO + 1], bf16)
        cnt = sb("cnt", [P, 2, NP], bf16)
        base1_i = sb("base1_i", [P, HALVES], i32)
        next1_i = sb("next1_i", [P, HALVES], i32)
        win_id = sb("win_id", [P, HALVES], f32)
        bias_le = sb("bias_le", [P, HALVES], f32)
        bias_lt = sb("bias_lt", [P, HALVES], f32)
        ends_in = sb("ends_in", [P, HALVES], f32)
        pos_off = sb("pos_off", [P, HALVES], f32)
        dcount = sb("dcount", [P, 2, 512], i32)
        ssum = sb("ssum", [P, 2, 2], f32)
        pc = sb("pc", [P, 8, 2], f32)
        pos_i = sb("pos_i", [P, 2], i32)
        pidx_i = sb("pidx_i", [P, 2], i32)
        end_i = sb("end_i", [P, NB], i32)
        end_t = sb("end_t", [P, 3, NB], i32)
        end_f = sb("end_f", [P, 4, NB], f32)
        end_idx = sb("end_idx", [P, NB], i32)
        srcq_i = sb("srcq_i", [P, TILES + STEP], i32)
        base1r = sb("base1r", [1, 4 * HALVES], i32)
        base1c = sb("base1c", [1, 4 * HALVES], i32)
        idx_st = [sb(f"idx_st{i}", [P, HALF[i]], i32) for i in range(2)]
        rows = [sb(f"rows{i}", [P, HALF[i], D], f32) for i in range(2)]
        sgn = [rows[i][:, :, :].rearrange("p t c -> p (t c)").bitcast(bf16) for i in range(2)]
        hsT = [sb(f"hsT{i}", [P, 32 * HALF[i]], f32) for i in range(2)]
        eab = [sb(f"eab{i}", [P, 32 * HALF[i]], f32) for i in range(2)]
        dstb = [sb(f"dstb{i}", [P, 32 * HALF[i] + 1], i32) for i in range(2)]
        same, lim, ohd, hdT = ([scan_bufs[:, 1024 * n + 512 * i:1024 * n + 512 * i + 32 * HALF[i]] for i in range(2)] for n in range(4))
        win = [sb(f"win{i}", [P, P], f32) for i in range(2)]
        hid = [sb(f"hid{i}", [P, 2, 32 * HALF[i]], f32) for i in range(2)]
        run = [sb(f"run{i}", [P, 32 * HALF[i]], f32) for i in range(2)]
        vrow = [sb(f"vrow{i}", [P, 32 * HALF[i]], f32) for i in range(2)]
        cand = sb("cand", [P, NB, D], f32)
        edge_v = sb("edge_v", [P, 3, D], f32)
        edge_n = sb("edge_n", [P, 3], i32)
        edge_nf = sb("edge_nf", [P, 3], f32)
        edge_p = sb("edge_p", [P, 3, NB], f32)
        tmp = sb("tmp", [P, 3, NB, D], f32)
        res = sb("res", [P, NB, D], f32)
        last0_i = sb("last0_i", [1, GROUPS], i32)
        base0_r = sb("base0_r", [1, GROUPS], i32)
        last1_i = sb("last1_i", [1, 4 * HALVES], i32)
        n_order = (E - 1) // 127
        order_i = tmp[:, :, :, :].rearrange("p a k c -> p (a k c)").bitcast(i32)[0:127, 0:2 * n_order].rearrange("p (a n) -> p a n", a=2)
        n_far = (EPAD - COUNT_MAX) // P
        assert EPAD - E < COUNT_MAX and (EPAD - COUNT_MAX) % P == 0
        far_i = scan_bufs[:, 2 * ATILES:2 * ATILES + 2 * n_far].bitcast(i32).rearrange("p (a n) -> p a n", a=2)
        far_f = key_win[:, 0:n_far]
        order_f = g[:, :, :, :].rearrange("p k a c -> p (k a c)")[0:127, :]
        wide0 = sb("wide0", [1, GROUPS], f32)
        wide1 = sb("wide1", [1, 4 * HALVES], f32)
        wide2 = sb("wide2", [1, D], f32)
        broken = sb("broken", [P, 5], f32)
        flag_f = sb("flag_f", [1, 1], f32)
        flag = sb("flag", [1, 1], i32)
        feat = grow[:, :, :].rearrange("p a b -> p (a b)").bitcast(f32)[0:D, 0:NP]
        peak = cnt[:, :, :].rearrange("p a b -> p (a b)").bitcast(f32)[0:D, 0:NP]
        total = keys[:, :, :].rearrange("p a b -> p (a b)")[0:D, 0:NP]
        wsum = scan_bufs[0:D, 0:NP]
        w11f = sb("w11f", [3 * D, H], f32)
        g_src = sb("g_src", [1, GE], i32)
        g_dst = sb("g_dst", [1, GE], i32)
        g_ea = sb("g_ea", [GE, D], f32)
        g_diff = sb("g_diff", [D, GE], f32)
        g_exp = sb("g_exp", [D, GE], f32)
        g_in = sb("g_in", [3 * D, GE], f32)
        g_hid = sb("g_hid", [P, GE], f32)

        ps = [ctx.enter_context(nc.psum_tensor(f"ps{i}", [P, 4, 512], f32)) for i in range(2)]
        ps_cnt = ps[0]
        ps_sum = ps[1][:, :, :].rearrange("p a b -> p (a b)")[:, 0:NB * H].rearrange("p (k c) -> p k c", c=H)

        s_const = sem("s_const")
        s_zero = sem("s_zero")
        s_x = sem("s_x")
        s_edges = sem("s_edges")
        s_win = sem("s_win")
        s_weights = sem("s_weights")
        s_dve = sem("s_dve")
        s_pool = sem("s_pool")
        s_sqrt_in = sem("s_sqrt_in")
        s_sqrt = sem("s_sqrt")
        s_ext = sem("s_ext")
        s_extT = sem("s_extT")
        s_topd = sem("s_topd")
        s_topb = sem("s_topb")
        s_shift = sem("s_shift")
        s_exp = sem("s_exp")
        s_gsplit = sem("s_gsplit")
        s_gtab = sem("s_gtab")
        s_gidx = sem("s_gidx")
        s_grow = sem("s_grow")
        s_onehot = sem("s_onehot")
        s_tile = sem("s_tile")
        s_evac = sem("s_evac")
        s_shuf = [sem(f"s_shuf{i}") for i in range(CHUNK)]
        s_chunk = sem("s_chunk")
        s_dcl = [sem(f"s_dcl{i}") for i in range(2)]
        s_sgn = sem("s_sgn")
        s_used = sem("s_used")
        s_endp = sem("s_endp")
        s_turn = sem("s_turn")
        s_winprep = sem("s_winprep")
        s_endinit = sem("s_endinit")
        s_scat = sem("s_scat")
        s_endld = sem("s_endld")
        s_endidx = sem("s_endidx")
        s_h0T = sem("s_h0T")
        s_m1 = sem("s_m1")
        s_m1r = sem("s_m1r")
        s_m2 = sem("s_m2")
        s_h1 = sem("s_h1")
        s_htab = sem("s_htab")
        s_idx = [sem(f"s_idx{i}") for i in range(2)]
        s_rows = [sem(f"s_rows{i}") for i in range(2)]
        s_ea = [sem(f"s_ea{i}") for i in range(2)]
        s_dst = [sem(f"s_dst{i}") for i in range(2)]
        s_wrow = [sem(f"s_wrow{i}") for i in range(2)]
        s_srcq = sem("s_srcq")
        s_ohd = [sem(f"s_ohd{i}") for i in range(2)]
        s_same = [sem(f"s_same{i}") for i in range(2)]
        s_lim = [sem(f"s_lim{i}") for i in range(2)]
        s_hd = [sem(f"s_hd{i}") for i in range(2)]
        s_hdc = [sem(f"s_hdc{i}") for i in range(2)]
        s_pre = [sem(f"s_pre{i}") for i in range(2)]
        s_hid = [sem(f"s_hid{i}") for i in range(2)]
        s_v = [sem(f"s_v{i}") for i in range(2)]
        s_run = [sem(f"s_run{i}") for i in range(2)]
        s_vrow = [sem(f"s_vrow{i}") for i in range(2)]
        s_vout = [sem(f"s_vout{i}") for i in range(2)]
        s_base1c = sem("s_base1c")
        s_candf = sem("s_candf")
        s_cand = sem("s_cand")
        s_edgev = sem("s_edgev")
        s_res = sem("s_res")
        s_out = sem("s_out")
        s_bounds = sem("s_bounds")
        s_broken = sem("s_broken")
        s_count = sem("s_count")
        s_flag = sem("s_flag")
        s_gidx3 = [sem(f"s_gidx3_{i}") for i in range(3)]
        s_gused = sem("s_gused")
        s_gea = sem("s_gea")
        s_gdiff = sem("s_gdiff")
        s_gexp = sem("s_gexp")
        s_geaT = sem("s_geaT")
        s_gin = sem("s_gin")
        s_gpre = sem("s_gpre")
        s_ghid = sem("s_ghid")
        s_gv = sem("s_gv")
        s_gturn = sem("s_gturn")

        block = ctx.enter_context(nc.Block())

        def windowed(rows_of_streams, w):
            return rows_of_streams.rearrange("q (o c) -> q o c", o=1).to_broadcast([4, W1, w])

        def if_general(eng):
            eng.wait_ge(s_flag, 1)
            eng.wait_ge(s_out, 16)
            return eng.If(eng.value_load(flag[0:1, 0:1], min_val=0, max_val=4 * E) > 0)

        @block.sync
        def _(sp):
            sp.dma_start(x[:, :, :].rearrange("p k c -> p (k c)"), xb).then_inc(s_x, 16)
            sp.dma_start(betac[:, :], beta.rearrange("(o a) -> o a", o=1).to_broadcast([P, 1])).then_inc(s_x, 16)
            sp.dma_start(src_i, src0).then_inc(s_edges, 16)
            sp.dma_start(dst_i, dst0).then_inc(s_edges, 16)
            sp.dma_start(base0_i[:, :], base0.rearrange("(o a) -> o a", o=1).to_broadcast([P, GROUPS])).then_inc(s_edges, 16)
            for r in range(CHUNK):
                sp.dma_start(gidx_b[W0 * r:W0 * r + W0, :], base0c[r:r + 1, :].to_broadcast([W0, CHUNKS])).then_inc(s_win, 16)
            for q in range(4):
                sp.dma_start(base1_i[32 * q:32 * q + 32, :], base1[q:q + 1, :].to_broadcast([32, HALVES])).then_inc(s_win, 16)
                sp.dma_start(next1_i[32 * q:32 * q + 32, :], next1[q:q + 1, :].to_broadcast([32, HALVES])).then_inc(s_win, 16)
            sp.dma_start(base1r[:, :], base1.rearrange("(o q) n -> o (q n)", o=1)).then_inc(s_win, 16)
            sp.dma_start(srcq_i[:, 0:TILES], srcq).then_inc(s_srcq, 16)
            sp.dma_start(last0_i[:, :], last0.rearrange("(o a) -> o a", o=1)).then_inc(s_bounds, 16)
            sp.dma_start(base0_r[:, :], base0.rearrange("(o a) -> o a", o=1)).then_inc(s_bounds, 16)
            sp.dma_start(last1_i[:, :], last1.rearrange("(o q) n -> o (q n)", o=1)).then_inc(s_bounds, 16)
            for i in range(2):
                sp.dma_start(order_i[:, i, :], dst[i:i + E - 1].rearrange("(p n) -> p n", p=127)).then_inc(s_bounds, 16)
            for i in range(2):
                sp.dma_start(far_i[:, i, :], dstp[COUNT_MAX * i:COUNT_MAX * i + P * n_far].rearrange("(p n) -> p n", p=P)).then_inc(s_bounds, 16)
            sp.wait_ge(s_zero, 2)
            sp.dma_start(end_dram.rearrange("(p k) o -> p (k o)", p=P), end_i[:, :]).then_inc(s_endinit, 16)
            sp.dma_start(edge_n[:, :], slast.rearrange("(o a) -> o a", o=1).to_broadcast([P, 3])).then_inc(s_srcq, 16)
            sp.wait_ge(s_gsplit, 1)
            sp.dma_start(g_dram[NP:NP + 1, :], zero_b[0:1, 0:3 * H]).then_inc(s_gtab, 16)
            sp.dma_start(g_dram[0:NP, :].rearrange("(k p) c -> p k c", p=P), gs[:, :, :, :].rearrange("p k s c -> p k (s c)")).then_inc(s_gtab, 16)

            sp.wait_ge(s_zero, 1)
            for q in range(4):
                rq, s, c = slice(32 * q, 32 * q + 32), q // 2, 64 * (q % 2)
                for m, wt in ((w01d, w01[:, :]), (w1sd, w11[0:D, :]), (w1dd, w11[D:2 * D, :]), (w1ed, w11[2 * D:3 * D, :])):
                    sp.dma_start(m[rq, s, c:c + H], wt).then_inc(s_weights, 16)
                for m, wt in ((w02d, w02), (w12d, w12)):
                    sp.dma_start(m[64 * (q % 2):64 * (q % 2) + 64, s, 32 * q:32 * q + 32], wt).then_inc(s_weights, 16)
            for m, b in ((b01c, b01), (b11c, b11)):
                for i in range(2):
                    sp.dma_start(m[64 * i:64 * i + 64, :], b.rearrange("(a o) -> a o", o=1)).then_inc(s_weights, 16)
            for m, b in ((b02r, b02), (b12r, b12)):
                sp.dma_start(m[:, :], b.rearrange("(o a) -> o a", o=1).to_broadcast([P, D])).then_inc(s_weights, 16)
            sp.dma_start(w11f[:, :], w11).then_inc(s_weights, 16)
            def shuffle(c0, k, groups, first):
                for j in range(groups):
                    grp = CHUNK * (c0 + k) + j
                    if j == 0 and not first:
                        sp.wait_ge(s_chunk, c0 + k - 1)
                    sp.wait_ge(s_evac, grp + 1)
                    sp.dma_start(cnt[W0 * j:W0 * j + W0, k % 2, 0:HI * LO].rearrange("n (a b) -> n a b", a=HI),
                                 cg[:, j, 0:LO]).then_inc(s_shuf[j], 16)

            shuffle(0, 0, CHUNK, True)
            shuffle(0, 1, CHUNK, True)
            with sp.Fori(1, PAIRS) as it:
                shuffle(2 * it, 0, CHUNK, False)
                shuffle(2 * it, 1, CHUNK, False)
            shuffle(2 * PAIRS, 0, CHUNK, False)
            shuffle(2 * PAIRS, 1, TAIL_GROUPS, False)

            sp.wait_ge(s_h1, 1)
            sp.dma_start(h_dram.rearrange("(k p) c -> p k c", p=P), h[:, :, :]).then_inc(s_htab, 16)
            sp.wait_ge(s_scat, 16 * HALVES)
            sp.dma_start(end_i[:, :], end_dram.rearrange("(k p) o -> p (k o)", p=P), allow_slow_non_contiguous=True).then_inc(s_endld, 16)
            sp.wait_ge(s_htab, 16)
            sp.wait_ge(s_base1c, 1)

            def load_half(it, i, first):
                w = 32 * HALF[i]
                c0 = it * (32 * STEP) + 32 * HALF[0] * i
                if not first:
                    sp.wait_ge(s_lim[i], it)
                sp.dma_start(dstb[i][:, :], windowed(dstq[:, ds(c0, w + 1)], w + 1)).then_inc(s_dst[i], 16)
                if not first:
                    sp.wait_ge(s_hd[i], it)
                for q in range(4):
                    first_node = sp.value_load(base1c[0:1, ds(2 * it + i + q * HALVES, 1)], min_val=0, max_val=N - W1)
                    sp.dma_start(win[i][32 * q:32 * q + 32, 32 * q:32 * q + 32], h_dram[ds(first_node, W1), :]).then_inc(s_wrow[i], 16)
                if not first:
                    sp.wait_ge(s_pre[i], it)
                sp.dma_start(eab[i][:, :], eat[:, ds(c0, w)]).then_inc(s_ea[i], 16)

            def store_half(it, i):
                w = HALF[i]
                sp.wait_ge(s_vrow[i], it + 1)
                sp.dma_start(v_dram.rearrange("(p t) c -> p t c", p=P)[:, ds(it * STEP + HALF[0] * i, w), :],
                             vrow[i][:, :].rearrange("p (t c) -> p t c", c=D)).then_inc(s_vout[i], 16)

            load_half(0, 0, True)
            load_half(0, 1, True)
            with sp.Fori(1, STEPS) as it:
                load_half(it, 0, False)
                store_half(it - 1, 0)
                load_half(it, 1, False)
                store_half(it - 1, 1)
            store_half(STEPS - 1, 0)
            store_half(STEPS - 1, 1)
            sp.wait_ge(s_vout[0], 16 * STEPS)
            sp.wait_ge(s_vout[1], 16 * STEPS)
            for q in range(3):
                sp.dma_start(edge_v[:, q, :], v_dram[(32 * q + 32) * TILES - 1:(32 * q + 32) * TILES, :].to_broadcast([P, D])).then_inc(s_edgev, 16)
            sp.wait_ge(s_res, 1)
            sp.dma_start(out, res[:, :, :].rearrange("p k c -> p (k c)")).then_inc(s_out, 16)
            sp.wait_ge(s_out, 16)

            def load_edges(c, at, features):
                sp.wait_ge(s_gused, c + (at + 1))
                sp.dma_start(g_src[:, :], src[ds(c * GE, GE)].rearrange("(o a) -> o a", o=1)).then_inc(s_gidx3[at // GCHUNKS], 16)
                sp.dma_start(g_dst[:, :], dst[ds(c * GE, GE)].rearrange("(o a) -> o a", o=1)).then_inc(s_gidx3[at // GCHUNKS], 16)
                if features:
                    sp.dma_start(g_ea[:, :], ea[ds(c * GE, GE), :]).then_inc(s_gea, 16)

            with if_general(sp):
                for n in range(3):
                    with sp.Fori(0, GCHUNKS) as c:
                        load_edges(c, n * GCHUNKS, n == 2)
                sp.wait_ge(s_res, 2)
                sp.dma_start(out, res[:, :, :].rearrange("p k c -> p (k c)")).then_inc(s_out, 16)
                sp.wait_ge(s_out, 32)

        @block.gpsimd
        def _(gp):
            done = [0]

            def step(ins):
                done[0] += 1
                ins.then_inc(s_pool, 1)
                gp.wait_ge(s_pool, done[0])

            gp.iota(diff_i[:, :], [[1, P]], base=0, channel_multiplier=-1, allow_small_or_imprecise_dtypes=True)
            gp.iota(lo_iota[:, :], [[1, LO + 1]], base=0, channel_multiplier=0, allow_small_or_imprecise_dtypes=True)
            gp.iota(node_id[:, :], [[P, NB]], base=0, channel_multiplier=1, allow_small_or_imprecise_dtypes=True)
            for i in range(2):
                gp.iota(pos_off[:, :].rearrange("p (s i) -> p s i", i=2)[:, :, i], [[32 * STEP, STEPS]],
                        base=32 * HALF[0] * i - 1 + 16 * HALF[i], channel_multiplier=0, allow_small_or_imprecise_dtypes=True)
            gp.iota(part[:, :], [[0, 1]], base=0, channel_multiplier=1).then_inc(s_const, 1)
            for m in (w01d, w1sd, w1dd, w1ed, w02d):
                gp.memset(m[:, :, :], 0.0)
            gp.memset(w12d[:, :, :], 0.0).then_inc(s_zero, 1)
            gp.memset(end_i[:, :], NOT_FOUND).then_inc(s_zero, 1)
            gp.memset(srcq_i[:, TILES:], 0)
            gp.memset(cand[:, :, :], -BIG).then_inc(s_candf, 1)
            gp.memset(cnt[:, :, HI * LO:], 0.0)
            gp.memset(run[1][:, :], -BIG)
            gp.memset(win[0][:, :], 0.0)
            gp.memset(win[1][:, :], 0.0).then_inc(s_zero, 1)
            gp.wait_ge(s_gidx, 1)
            gp.wait_ge(s_gtab, 32)
            for c in range(CHUNKS):
                gp.indirect_dma_start(grow[:, c, :], None, g_dram[:, :], bass.IndirectOffsetOnAxis(gidx[:, c:c + 1], 0)).then_inc(s_grow, 16)

            gp.wait_ge(s_winprep, 1)
            gp.wait_ge(s_endinit, 16)

            def load_count_dst(it, first):
                for i in range(2):
                    c0 = it * (32 * STEP) + 32 * HALF[0] * i
                    w = 32 * HALF[i]
                    gp.dma_start(dcount[:, i, 0:w], windowed(dstq[:, ds(c0 + 1, w)], w)).then_inc(s_dcl[i], 16)

            def ends(it, first):
                at = [0]

                def link(ins):
                    at[0] += 1
                    ins.then_inc(s_endp, 1)
                    gp.wait_ge(s_endp, it * LINKS + at[0])
                    gp.sem_inc(s_turn, 1)

                for k, m in ((0, pos_off), (1, win_id), (2, ends_in)):
                    gp.tensor_copy(pc[:, k, :], m[:, ds(2 * it, 2)])
                gp.wait_ge(s_sgn, it + 1)
                gp.sem_inc(s_turn, 1)
                link(gp.tensor_scalar(pc[:, 3, :], ssum[:, 0, :], -0.5, None, ALU.mult))
                link(gp.tensor_tensor(pc[:, 4, :], ssum[:, 1, :], ssum[:, 0, :], ALU.subtract))
                link(gp.tensor_scalar(pc[:, 4, :], pc[:, 4, :], 0.5, None, ALU.is_gt))
                link(gp.tensor_tensor(pc[:, 5, :], pc[:, 4, :], pc[:, 2, :], ALU.mult))
                link(gp.tensor_tensor(pc[:, 3, :], pc[:, 3, :], pc[:, 0, :], ALU.add))
                link(gp.tensor_scalar(pc[:, 6, :], pc[:, 5, :], -float(NOT_FOUND), float(NOT_FOUND), ALU.mult, ALU.add))
                link(gp.tensor_tensor(pc[:, 6, :], pc[:, 6, :], pc[:, 1, :], ALU.add))
                if not first:
                    gp.wait_ge(s_scat, it * 32)
                    gp.sem_inc(s_turn, 1)
                gp.tensor_copy(pos_i[:, :], pc[:, 3, :])
                gp.tensor_copy(pidx_i[:, :], pc[:, 6, :]).then_inc(s_used, 1)
                gp.wait_ge(s_used, it + 1)
                gp.sem_inc(s_turn, 1)
                for i in range(2):
                    gp.indirect_dma_start(end_dram[:, :], bass.IndirectOffsetOnAxis(pidx_i[:, i:i + 1], 0), pos_i[:, i:i + 1], None,
                                          bounds_check=NP - 1, oob_is_err=False).then_inc(s_scat, 16)

            LINKS = 7
            load_count_dst(0, True)
            gp.wait_ge(s_sgn, 1)
            load_count_dst(1, False)
            ends(0, True)
            with gp.Fori(1, STEPS - 1) as it:
                gp.wait_ge(s_sgn, it + 1)
                gp.sem_inc(s_turn, 1)
                load_count_dst(it + 1, False)
                ends(it, False)
            ends(STEPS - 1, False)

            gp.wait_ge(s_htab, 16)
            with gp.Fori(0, STEPS) as it:
                for i in range(2):
                    gp.wait_ge(s_idx[i], it + 1)
                    gp.sem_inc(s_turn, 1)
                    for t in range(HALF[i]):
                        gp.indirect_dma_start(rows[i][:, t, :], None, h_dram[:, :],
                                              bass.IndirectOffsetOnAxis(idx_st[i][:, t:t + 1], 0)).then_inc(s_rows[i], 16)
            gp.wait_ge(s_endidx, 1)
            gp.wait_ge(s_candf, 1)
            gp.wait_ge(s_vout[0], 16 * STEPS)
            gp.wait_ge(s_vout[1], 16 * STEPS)
            for k in range(NB):
                gp.indirect_dma_start(cand[:, k, :], None, v_dram[:, :], bass.IndirectOffsetOnAxis(end_idx[:, k:k + 1], 0),
                                      bounds_check=P * TILES - 1, oob_is_err=False).then_inc(s_cand, 16)

        @block.scalar
        def _(act):
            act.wait_ge(s_sqrt_in, 1)
            nc.scalar.activation(stat[:, 2, :], stat[:, 1, :], ACT.Sqrt).then_inc(s_sqrt, 1)
            act.wait_ge(s_shift, 1)
            nc.scalar.activation(g[:, :, 0, :], logit[:, :, :], ACT.Exp).then_inc(s_exp, 1)
            act.wait_ge(s_winprep, 1)

            def evac(c0, k, j0, j1, first):
                for j in range(j0, j1):
                    grp = CHUNK * (c0 + k) + j
                    if not (first and k == 0):
                        act.wait_ge(s_shuf[j], 16 * (c0 + k))
                    act.wait_ge(s_tile, GT * grp + GT)
                    nc.scalar.activation(cg[:, j, 0:LO], ps_cnt[:, j % 4, 0:LO], ACT.Copy).then_inc(s_evac, 1)

            def signs(it):
                for i in range(2):
                    w = 32 * HALF[i]
                    for b, m in ((0, bias_le), (1, bias_lt)):
                        last = nc.scalar.activation(sgn[i][:, w * b:w * b + w], dcount[:, i, 0:w], ACT.Sign, bias=m[:, ds(2 * it + i, 1)],
                                                    accum_out=ssum[:, b, i:i + 1])
                last.then_inc(s_sgn, 1)

            def counted(step_):
                for i in range(2):
                    act.wait_ge(s_dcl[i], step_ * 16 + 16)
                if not (isinstance(step_, int) and step_ == 0):
                    act.wait_ge(s_used, step_)

            def count_pair(it, first, with_signs, groups):
                for k, n in enumerate((CHUNK, groups)):
                    evac(2 * it, k, 0, n - 3, first)
                    if with_signs:
                        counted(2 * it + k)
                    evac(2 * it, k, n - 3, n - 2, first)
                    if with_signs:
                        signs(2 * it + k)
                    evac(2 * it, k, n - 2, n, first)

            count_pair(0, True, True, CHUNK)
            with act.Fori(1, SIGN_PAIRS) as it:
                count_pair(it, False, True, CHUNK)
            with act.Fori(SIGN_PAIRS, PAIRS) as it:
                count_pair(it, False, False, CHUNK)
            count_pair(PAIRS, False, False, TAIL_GROUPS)

            def root(n):
                act.wait_ge(s_sqrt_in, n)
                nc.scalar.activation(stat[:, 2, :], stat[:, 1, :], ACT.Sqrt).then_inc(s_sqrt, 1)

            def first_mlp(r):
                for f in range(2):
                    for s in range(2):
                        act.wait_ge(s_m1, 4 * r + 2 * f + s + 1)
                        nc.scalar.activation(mT[:, s, 400 * f:400 * f + 400], ps[0][:, s, 0:400], ACT.Relu, bias=b01c[:, 0:1]).then_inc(s_m1r, 1)

            act.wait_ge(s_weights, 16 * 31)
            first_mlp(0)
            root(2)

            def hidden(it, first):
                for i in range(2):
                    w = 32 * HALF[i]
                    if not first:
                        act.wait_ge(s_pre[i], it)
                    act.wait_ge(s_hd[i], it + 1)
                    nc.scalar.activation(hdT[i], ps[i][:, 0, 0:w], ACT.Copy).then_inc(s_hdc[i], 1)
                    if not first:
                        act.wait_ge(s_v[i], it)
                    act.wait_ge(s_pre[i], it + 1)
                    for s in range(2):
                        last = nc.scalar.activation(hid[i][:, s, :], ps[i][:, 1 + s, 0:w], ACT.Relu, bias=b11c[:, 0:1])
                    last.then_inc(s_hid[i], 1)

            hidden(0, True)
            with act.Fori(1, STEPS) as it:
                hidden(it, False)

            with if_general(act):
                root(3)
                with act.Fori(0, GCHUNKS) as c:
                    act.wait_ge(s_gdiff, c + 1)
                    nc.scalar.activation(g_exp[:, :], g_diff[:, :], ACT.Exp).then_inc(s_gexp, 1)
                first_mlp(1)
                root(4)
                with act.Fori(0, GCHUNKS) as c:
                    act.wait_ge(s_gpre, c + 1)
                    nc.scalar.activation(g_hid[0:H, :], ps[0][0:H, 1, 0:GE], ACT.Relu, bias=b11c[0:H, 0:1]).then_inc(s_ghid, 1)

        @block.tensor
        def _(pe):
            pe.wait_ge(s_ext, 1)
            nc.tensor.transpose(ps[0][0:H, 0, 0:P], ext[:, :, :].rearrange("p a c -> p (a c)"), ident[:, :]).then_inc(s_extT, 1)
            pe.wait_ge(s_topd, 1)
            nc.tensor.matmul(ps[0][:, 1, 0:H], ones[0:H, :], topd[:, :], start=True, stop=True).then_inc(s_topb, 1)
            for b in range(4):
                nc.tensor.matmul(ps[1][:, b, :], zero_b[:, 0:P], zero_b[:, :], start=True, stop=False, skip_group_check=True)

            def count_tile(c0, u, first):
                if u % GT == 0 and not (first and u < 4 * GT):
                    pe.wait_ge(s_evac, CHUNK * c0 + u // GT - 3)
                pe.wait_ge(s_onehot, CT * c0 + u + 1)
                nc.tensor.matmul(ps_cnt[:, (u // GT) % 4, 0:LO], oh_win[:, u % RING, :], oh_lo[:, u % RING, 0:LO],
                                 start=(u % GT == 0), stop=(u % GT == GT - 1)).then_inc(s_tile, 1)

            def sum_blocks(c, k, b0, b1):
                for b in range(b0, b1):
                    for part_ in range(3):
                        last = nc.tensor.matmul(ps_sum[:, b, :], cnt[:, k, P * b:P * b + P], grow_of(c)[:, H * part_:H * part_ + H],
                                                start=False, stop=False, skip_group_check=True)
                if b1 == NB:
                    last.then_inc(s_chunk, 1)

            def grow_of(c):
                return grow[:, ds(c, 1), :].rearrange("p a n -> p (a n)")

            def chunk_ready(c):
                for r in range(CHUNK):
                    pe.wait_ge(s_shuf[r], 16 * (c + 1))

            def count_chunk(c0, k, tiles, first):
                late = tiles // 2 - 1
                for u in range(tiles):
                    count_tile(c0, u + CT * k, first)
                    if first and k == 0 or u < late:
                        continue
                    if u == late:
                        if first:
                            pe.wait_ge(s_grow, 16 * CHUNKS)
                            pe.wait_ge(s_zero, 3)
                        chunk_ready(c0 + k - 1)
                    n = tiles - late
                    sum_blocks(c0 + k - 1, (k + 1) % 2, NB * (u - late) // n, NB * (u - late + 1) // n)

            count_chunk(0, 0, CT, True)
            count_chunk(0, 1, CT, True)
            with pe.Fori(1, PAIRS) as it:
                count_chunk(2 * it, 0, CT, False)
                count_chunk(2 * it, 1, CT, False)
            count_chunk(2 * PAIRS, 0, CT, False)
            count_chunk(2 * PAIRS, 1, GT * TAIL_GROUPS, False)
            for r in range(TAIL_GROUPS):
                pe.wait_ge(s_shuf[r], 16 * CHUNKS)
            sum_blocks(CHUNKS - 1, (CHUNKS - 1) % 2, 0, NB)

            def first_mlp(r):
                pe.wait_ge(s_h0T, r + 1)
                for f in range(2):
                    for s in range(2):
                        if f:
                            pe.wait_ge(s_m1r, 4 * r + s + 1)
                        nc.tensor.matmul(ps[0][:, s, 0:400], w01d[:, s, :], hT[:, 400 * f:400 * f + 400], start=True, stop=True).then_inc(s_m1, 1)
                for f in range(2):
                    pe.wait_ge(s_m1r, 4 * r + 2 * f + 2)
                    for s in range(2):
                        last = nc.tensor.matmul(ps[0][:, 2 + f, 0:400], w02d[:, s, :], mT[:, s, 400 * f:400 * f + 400], start=(s == 0), stop=(s == 1))
                    last.then_inc(s_m2, 1)

            pe.wait_ge(s_weights, 16 * 31)
            first_mlp(0)
            pe.wait_ge(s_broken, 1)
            nc.tensor.matmul(ps[1][0:1, 0, 0:5], ones[:, 0:1], broken[:, :], start=True, stop=True).then_inc(s_count, 1)

            pe.wait_ge(s_h1, 1)

            def layers(it, first):
                for i in range(2):
                    w = 32 * HALF[i]
                    pd, pv = ps[i][:, 0, 0:w], ps[i][:, 3, 0:w]
                    pe.wait_ge(s_wrow[i], 64 * it + 64)
                    pe.wait_ge(s_ohd[i], it + 1)
                    nc.tensor.matmul(pd, win[i][:, :], ohd[i], start=True, stop=True).then_inc(s_hd[i], 1)
                    pe.wait_ge(s_ea[i], 16 * it + 16)
                    for s in range(2):
                        nc.tensor.matmul(ps[i][:, 1 + s, 0:w], w1ed[:, s, :], eab[i][:, :], start=True, stop=False)
                    pe.wait_ge(s_hdc[i], it + 1)
                    for s in range(2):
                        nc.tensor.matmul(ps[i][:, 1 + s, 0:w], w1dd[:, s, :], hdT[i], start=False, stop=False)
                    pe.wait_ge(s_idx[i], it + 2)
                    for s in range(2):
                        last = nc.tensor.matmul(ps[i][:, 1 + s, 0:w], w1sd[:, s, :], hsT[i][:, :], start=False, stop=True)
                    last.then_inc(s_pre[i], 1)
                    pe.wait_ge(s_hid[i], it + 1)
                    if not first:
                        pe.wait_ge(s_run[i], it)
                    for s in range(2):
                        last = nc.tensor.matmul(pv, w12d[:, s, :], hid[i][:, s, :], start=(s == 0), stop=(s == 1))
                    last.then_inc(s_v[i], 1)

            layers(0, True)
            with pe.Fori(1, STEPS) as it:
                layers(it, False)

            with if_general(pe):
                first_mlp(1)
                pe.wait_ge(s_h1, 2)
                with pe.Fori(0, GCHUNKS) as c:
                    pe.wait_ge(s_gea, 16 * c + 16)
                    nc.tensor.transpose(ps[0][0:D, 0, 0:GE], g_ea[:, :], ident[0:GE, 0:GE]).then_inc(s_geaT, 1)
                    pe.wait_ge(s_gin, c + 1)
                    nc.tensor.matmul(ps[0][0:H, 1, 0:GE], w11f[:, :], g_in[:, :], start=True, stop=True).then_inc(s_gpre, 1)
                    pe.wait_ge(s_ghid, c + 1)
                    nc.tensor.matmul(ps[0][:, 2, 0:GE], w12d[:, 0, :], g_hid[:, :], start=True, stop=True).then_inc(s_gv, 1)

        @block.vector
        def _(ve):
            done = [0]
            V = nc.vector

            def step(ins):
                done[0] += 1
                ins.then_inc(s_dve, 1)
                ve.wait_ge(s_dve, done[0])

            def bc(col):
                return col.rearrange("p (k o) -> p k o", o=1).to_broadcast([P, NB, D])

            def chan(row):
                return row.rearrange("p (o c) -> p o c", o=1).to_broadcast([P, NB, D])

            def norm_relu(src, n):
                step(V.reduce_sum(stat[:, 0, :], src, AX))
                step(V.tensor_scalar(stat[:, 0, :], stat[:, 0, :], 1.0 / D, None, ALU.mult))
                step(V.tensor_tensor(xc[:, :, :], src, bc(stat[:, 0, :]), ALU.subtract))
                step(V.tensor_tensor(sq[:, :, :], xc[:, :, :], xc[:, :, :], ALU.mult))
                step(V.reduce_sum(stat[:, 1, :], sq[:, :, :], AX))
                V.tensor_scalar(stat[:, 1, :], stat[:, 1, :], 1.0 / D, LN_EPS, ALU.mult, ALU.add).then_inc(s_sqrt_in, 1)
                ve.wait_ge(s_sqrt, n)
                step(V.reciprocal(stat[:, 3, :], stat[:, 2, :]))
                step(V.tensor_tensor(xc[:, :, :], xc[:, :, :], bc(stat[:, 3, :]), ALU.mult))
                return V.tensor_scalar(h[:, :, :], xc[:, :, :], 0.0, None, ALU.max)

            V.memset(ones[:, :], 1.0)
            V.memset(zero_b[:, :], 0.0)
            ve.wait_ge(s_const, 1)
            step(V.tensor_scalar(ident[:, :], diff_i[:, :], 0.0, None, ALU.is_equal))
            ve.wait_ge(s_x, 32)
            step(norm_relu(x[:, :, :], 1))
            step(V.tensor_scalar(h[:, :, :], h[:, :, :], MSG_EPS, None, ALU.add))
            step(V.tensor_scalar(logit[:, :, :], h[:, :, :], betac[:, 0:1], None, ALU.mult))
            step(V.tensor_scalar(sq[:, :, :], logit[:, :, :], -1.0, None, ALU.mult))
            step(V.reduce_max(ext[:, 0, :], logit[:, :, :].rearrange("p k c -> p c k"), AX))
            V.reduce_max(ext[:, 1, :], sq[:, :, :].rearrange("p k c -> p c k"), AX).then_inc(s_ext, 1)
            ve.wait_ge(s_extT, 1)
            step(V.reduce_max(top[:, :], ps[0][0:H, 0, 0:P], AX))
            V.tensor_scalar(topd[:, :], ident[0:H, 0:H], top[:, 0:1], None, ALU.mult).then_inc(s_topd, 1)
            ve.wait_ge(s_topb, 1)
            step(V.tensor_copy(topb[:, :, :].rearrange("p a c -> p (a c)"), ps[0][:, 1, 0:H]))
            V.tensor_tensor(logit[:, :, :], logit[:, :, :], chan(topb[:, 0, :]), ALU.subtract).then_inc(s_shift, 1)
            ve.wait_ge(s_exp, 1)
            step(V.tensor_tensor(g[:, :, 1, :], g[:, :, 0, :], h[:, :, :], ALU.mult))
            gf = g[:, :, :, :].rearrange("p k a c -> p k (a c)")
            step(V.tensor_copy(gs[:, :, 0, :], gf))
            step(V.tensor_tensor(gf, gf, gs[:, :, 0, :], ALU.subtract))
            step(V.tensor_copy(gs[:, :, 1, :], gf))
            step(V.tensor_tensor(gf, gf, gs[:, :, 1, :], ALU.subtract))
            V.tensor_copy(gs[:, :, 2, :], gf).then_inc(s_gsplit, 1)

            ve.wait_ge(s_win, 16 * (CHUNK + 9))
            step(V.tensor_scalar(part16[:, :], part[:, :], W0 - 1, None, ALU.bitwise_and))
            step(V.tensor_scalar(part32[:, :], part[:, :], W1 - 1, None, ALU.bitwise_and))
            step(V.tensor_copy(part16f[:, :], part16[:, :]))
            step(V.tensor_copy(part32f[:, :], part32[:, :]))
            V.tensor_scalar(gidx[:, :], gidx_b[:, :], part16f[:, 0:1], float(NP), ALU.add, ALU.min).then_inc(s_gidx, 1)
            step(V.tensor_scalar(base1c[:, :], base1r[:, :], float(N - W1), None, ALU.min))
            V.tensor_scalar(base1c[:, :], base1c[:, :], 0.0, None, ALU.max).then_inc(s_base1c, 1)
            step(V.tensor_scalar(win_id[:, :], base1_i[:, :], float(N - W1), part32f[:, 0:1], ALU.min, ALU.add))
            step(V.tensor_tensor(ends_in[:, :], next1_i[:, :], win_id[:, :], ALU.is_gt))
            step(V.tensor_scalar(bias_le[:, :], win_id[:, :], -1.0, -0.5, ALU.mult, ALU.add))
            step(V.tensor_scalar(part32[:, :], part[:, :], 5, 15, ALU.arith_shift_right, ALU.logical_shift_left))
            step(V.tensor_copy(part16f[:, :], part32[:, :]))
            step(V.tensor_scalar(pos_off[:, :], pos_off[:, :], part16f[:, 0:1], None, ALU.add))
            V.tensor_scalar(bias_lt[:, :], win_id[:, :], -1.0, 0.5, ALU.mult, ALU.add).then_inc(s_winprep, 1)

            ve.wait_ge(s_edges, 48)
            step(V.tensor_copy(srcf, src_i))
            step(V.tensor_scalar(hif[:, 0, :], srcf, float(LO), None, ALU.is_ge))
            for k in range(2, HI):
                step(V.scalar_tensor_tensor(hif[:, (k + 1) % 2, :], srcf, float(k * LO), hif[:, k % 2, :], ALU.is_ge, ALU.add))
            hi = hif[:, (HI - 1 + 1) % 2, :]
            step(V.scalar_tensor_tensor(key_lo, hi, -float(LO), srcf, ALU.mult, ALU.add))
            step(V.tensor_tensor(key_win.rearrange("p (g t) -> p g t", t=GT), dst_i.rearrange("p (g t) -> p g t", t=GT),
                                 base0_i[:, :].rearrange("p (g o) -> p g o", o=1).to_broadcast([P, GROUPS, GT]), ALU.subtract))
            step(V.scalar_tensor_tensor(key_win, key_win, float(HI), hi, ALU.mult, ALU.add))

            def onehots(it, tiles, first):
                for u in range(tiles):
                    if not (first and u < RING):
                        ve.wait_ge(s_tile, 2 * CT * it + u - (RING - 1))
                    V.tensor_scalar(oh_win[:, u % RING, :], lo_iota[:, 0:P], key_win[:, ds(2 * CT * it + u, 1)], None, ALU.is_equal)
                    V.tensor_scalar(oh_lo[:, u % RING, :], lo_iota[:, :], key_lo[:, ds(2 * CT * it + u, 1)], None, ALU.is_equal).then_inc(s_onehot, 1)

            onehots(0, 2 * CT, True)
            with ve.Fori(1, PAIRS) as it:
                onehots(it, 2 * CT, False)
            onehots(PAIRS, CT + GT * TAIL_GROUPS, False)

            ve.wait_ge(s_chunk, CHUNKS)
            step(V.tensor_scalar(sq[:, :, :], ps_sum[:, :, 0:D], 1e-38, None, ALU.max))
            step(V.reciprocal(logit[:, :, :], sq[:, :, :]))
            step(V.tensor_tensor(xc[:, :, :], ps_sum[:, :, D:2 * D], logit[:, :, :], ALU.mult))
            V.transpose(hT[:, :], xc[:, :, :].rearrange("p k c -> p (k c)")).then_inc(s_h0T, 1)
            def after_mlp(r):
                for f in range(2):
                    ve.wait_ge(s_m2, 2 * r + f + 1)
                    step(V.tensor_copy(mT[:, 0, 400 * f:400 * f + 400], ps[0][:, 2 + f, 0:400]))
                step(V.transpose(sq[:, :, :].rearrange("p k c -> p (k c)"), mT[:, 0, :]))
                step(V.tensor_tensor(sq[:, :, :], sq[:, :, :], chan(b02r[:, :]), ALU.add))
                step(V.tensor_tensor(x1[:, :, :], sq[:, :, :], x[:, :, :], ALU.add))
                norm_relu(x1[:, :, :], 2 * r + 2).then_inc(s_h1, 1)

            ve.wait_ge(s_weights, 16 * 31)
            after_mlp(0)

            step(V.memset(broken[:, :], 0.0))
            ve.wait_ge(s_bounds, 112)
            step(V.tensor_tensor(wide0[:, :], last0_i[:, :], base0_r[:, :], ALU.subtract))
            step(V.tensor_scalar(wide0[:, :], wide0[:, :], float(W0 - 1), None, ALU.is_gt))
            step(V.tensor_tensor(wide1[:, :], last1_i[:, :], base1c[:, :], ALU.subtract))
            step(V.tensor_scalar(wide1[:, :], wide1[:, :], float(W1 - 1), None, ALU.is_gt))
            step(V.tensor_tensor(order_f[:, 0:n_order], order_i[:, 0, :], order_i[:, 1, :], ALU.is_gt))
            step(V.tensor_tensor(wide2[:, :], topb[0:1, 0, :], topb[0:1, 1, :], ALU.add))
            step(V.tensor_scalar(wide2[:, :], wide2[:, :], RANGE, None, ALU.is_gt))
            step(V.tensor_tensor(far_f, far_i[:, 0, :], far_i[:, 1, :], ALU.is_equal))
            step(V.reduce_sum(broken[:, 4:5], far_f, AX))
            step(V.reduce_sum(broken[0:1, 0:1], wide0[:, :], AX))
            step(V.reduce_sum(broken[0:1, 1:2], wide1[:, :], AX))
            step(V.reduce_sum(broken[0:127, 2:3], order_f[:, 0:n_order], AX))
            V.reduce_sum(broken[0:1, 3:4], wide2[:, :], AX).then_inc(s_broken, 1)
            ve.wait_ge(s_count, 1)
            step(V.reduce_sum(flag_f[:, :], ps[1][0:1, 0, 0:5], AX))
            V.tensor_copy(flag[:, :], flag_f[:, :]).then_inc(s_flag, 1)

            ve.wait_ge(s_endld, 16)
            step(V.tensor_scalar(end_t[:, 0, :], end_i[:, :], 15, None, ALU.arith_shift_right))
            step(V.tensor_scalar(end_t[:, 1, :], end_i[:, :], 31, None, ALU.bitwise_and))
            step(V.tensor_scalar(end_t[:, 2, :], end_i[:, :], (1 << 15) - 1, None, ALU.bitwise_and))
            step(V.tensor_scalar(end_t[:, 2, :], end_t[:, 2, :], 5, None, ALU.arith_shift_right))
            step(V.tensor_copy(end_f[:, 0:3, :], end_t[:, :, :]))
            step(V.scalar_tensor_tensor(end_f[:, 3, :], end_f[:, 0, :], 32.0, end_f[:, 1, :], ALU.mult, ALU.add))
            V.scalar_tensor_tensor(end_idx[:, :], end_f[:, 3, :], float(TILES), end_f[:, 2, :], ALU.mult, ALU.add).then_inc(s_endidx, 1)
            ve.wait_ge(s_srcq, 32)
            step(V.tensor_copy(edge_nf[:, :], edge_n[:, :]))
            for q in range(3):
                step(V.tensor_scalar(edge_p[:, q, :], node_id[:, :], edge_nf[:, q:q + 1], None, ALU.is_equal))
            step(V.tensor_scalar(edge_p[:, :, :], edge_p[:, :, :], 1.0, BIG, ALU.subtract, ALU.mult))

            def stage(it, i):
                return V.tensor_copy(idx_st[i][:, :], srcq_i[:, ds(it * STEP + HALF[0] * i, HALF[i])])

            ve.wait_ge(s_zero, 3)
            for i in range(2):
                stage(0, i).then_inc(s_idx[i], 1)

            def half(it, i, first):
                w = 32 * HALF[i]
                ve.wait_ge(s_dst[i], 16 * it + 16)
                if not first:
                    ve.wait_ge(s_hd[i], it)
                V.tensor_scalar(ohd[i], dstb[i][:, 1:w + 1], win_id[:, ds(2 * it + i, 1)], None, ALU.is_equal).then_inc(s_ohd[i], 1)
                V.tensor_tensor(same[i], dstb[i][:, 1:w + 1], dstb[i][:, 0:w], ALU.is_equal).then_inc(s_same[i], 1)
                ve.wait_ge(s_same[i], it + 1)
                V.tensor_scalar(lim[i], same[i], 0.5, 3.4e38, ALU.subtract, ALU.mult).then_inc(s_lim[i], 1)
                if not first:
                    ve.wait_ge(s_pre[i], it)
                ve.wait_ge(s_rows[i], (16 * HALF[i]) * (it + 1))
                V.transpose(hsT[i][:, :], rows[i][:, :, :].rearrange("p t c -> p (t c)"))
                stage(it + 1, i).then_inc(s_idx[i], 1)
                ve.wait_ge(s_lim[i], it + 1)
                if i == 1:
                    ve.wait_ge(s_run[0], it + 1)
                elif not first:
                    ve.wait_ge(s_run[1], it)
                ve.wait_ge(s_v[i], it + 1)
                V.tensor_tensor_scan(run[i][:, :], lim[i], ps[i][:, 3, 0:w],
                                     run[1 - i][:, 32 * HALF[1 - i] - 1:32 * HALF[1 - i]], ALU.min, ALU.max).then_inc(s_run[i], 1)
                if not first:
                    ve.wait_ge(s_vout[i], 16 * it)
                ve.wait_ge(s_run[i], it + 1)
                V.transpose(vrow[i][:, :], run[i][:, :]).then_inc(s_vrow[i], 1)

            half(0, 0, True)
            half(0, 1, True)
            with ve.Fori(1, STEPS) as it:
                half(it, 0, False)
                half(it, 1, False)

            def finish():
                step(V.tensor_tensor(cand[:, :, :], cand[:, :, :], chan(b12r[:, :]), ALU.add))
                step(V.tensor_tensor(cand[:, :, :], cand[:, :, :], h[:, :, :], ALU.max))
                V.tensor_tensor(res[:, :, :], cand[:, :, :], x1[:, :, :], ALU.add).then_inc(s_res, 1)

            ve.wait_ge(s_edgev, 48)
            for q in range(3):
                step(V.tensor_tensor(tmp[:, q, :, :], bc(edge_p[:, q, :]), chan(edge_v[:, q, :]), ALU.add))
            ve.wait_ge(s_cand, 16 * NB)
            for q in range(3):
                step(V.tensor_tensor(cand[:, :, :], cand[:, :, :], tmp[:, q, :, :], ALU.max))
            finish()

            def columns(table, q):
                return table.rearrange("c (k q r) -> c k q r", q=4, r=32)[:, :, q, :]

            def quad(q):
                return hT[32 * q:32 * q + 32, :].rearrange("c (k r) -> c k r", r=32)

            def rows_to_table(rows_, table):
                step(V.transpose(hT[:, :], rows_.rearrange("p k c -> p (k c)")))
                for q in range(4):
                    step(V.tensor_copy(columns(table, q), quad(q)))

            def table_to_quads(table):
                for q in range(4):
                    last = V.tensor_copy(quad(q), columns(table, q))
                return last

            def edges(body):
                ve.sem_inc(s_gturn, 1)
                with ve.Fori(0, GE) as j:
                    body(j, ve.value_load(g_src[0:1, ds(j, 1)], min_val=0, max_val=N - 1),
                         ve.value_load(g_dst[0:1, ds(j, 1)], min_val=0, max_val=N - 1))

            with if_general(ve):
                ve.sem_inc(s_gused, 1)
                step(norm_relu(x[:, :, :], 3))
                step(V.tensor_scalar(h[:, :, :], h[:, :, :], MSG_EPS, None, ALU.add))
                rows_to_table(h[:, :, :], feat)
                V.memset(g_hid[:, :], 0.0)
                V.memset(total, 0.0)
                V.memset(wsum, 0.0)
                step(V.memset(peak, -BIG))
                with ve.Fori(0, GCHUNKS) as c:
                    ve.wait_ge(s_gidx3[0], 32 * c + 32)

                    def largest(j, s, d):
                        V.scalar_tensor_tensor(peak[:, ds(s, 1)], feat[:, ds(d, 1)], betac[0:D, 0:1], peak[:, ds(s, 1)], ALU.mult, ALU.max)
                        ve.drain()

                    edges(largest)
                    ve.sem_inc(s_gused, 1)
                with ve.Fori(0, GCHUNKS) as c:
                    ve.wait_ge(s_gidx3[1], 32 * c + 32)

                    def shifted(j, s, d):
                        V.scalar_tensor_tensor(g_diff[:, ds(j, 1)], feat[:, ds(d, 1)], betac[0:D, 0:1], peak[:, ds(s, 1)], ALU.mult, ALU.subtract)

                    def summed(j, s, d):
                        V.tensor_tensor(total[:, ds(s, 1)], total[:, ds(s, 1)], g_exp[:, ds(j, 1)], ALU.add)
                        V.scalar_tensor_tensor(wsum[:, ds(s, 1)], feat[:, ds(d, 1)], g_exp[:, ds(j, 1)], wsum[:, ds(s, 1)], ALU.mult, ALU.add)
                        ve.drain()

                    edges(shifted)
                    ve.drain()
                    ve.sem_inc(s_gdiff, 1)
                    ve.wait_ge(s_gexp, c + 1)
                    edges(summed)
                    ve.sem_inc(s_gused, 1)
                step(V.tensor_scalar(total, total, 1e-38, None, ALU.max))
                step(V.reciprocal(total, total))
                step(V.tensor_tensor(wsum, wsum, total, ALU.mult))
                table_to_quads(wsum).then_inc(s_h0T, 1)
                after_mlp(1)
                ve.wait_ge(s_h1, 2)
                rows_to_table(h[:, :, :], feat)
                step(V.memset(peak, -BIG))
                with ve.Fori(0, GCHUNKS) as c:
                    ve.wait_ge(s_gidx3[2], 32 * c + 32)

                    def fill(j, s, d):
                        V.tensor_copy(g_in[0:D, ds(j, 1)], feat[:, ds(s, 1)])
                        V.tensor_copy(g_in[D:2 * D, ds(j, 1)], feat[:, ds(d, 1)])

                    def maximum(j, s, d):
                        V.tensor_tensor(peak[:, ds(d, 1)], peak[:, ds(d, 1)], ps[0][0:D, 2, ds(j, 1)], ALU.max)
                        ve.drain()

                    edges(fill)
                    ve.wait_ge(s_geaT, c + 1)
                    V.tensor_copy(g_in[2 * D:3 * D, :], ps[0][0:D, 0, 0:GE])
                    ve.drain()
                    ve.sem_inc(s_gin, 1)
                    ve.wait_ge(s_gv, c + 1)
                    edges(maximum)
                    ve.sem_inc(s_gused, 1)
                step(table_to_quads(peak))
                step(V.transpose(cand[:, :, :].rearrange("p k c -> p (k c)"), hT[:, :]))
                finish()


def kernel(**inputs):
    import numpy as np
    import concourse.bacc as bacc
    from concourse import mybir as mb
    from concourse.bass_utils import run_bass_kernel_spmd as launch

    a = {k: np.ascontiguousarray(v) for k, v in inputs.items()}
    x, src, dst, ea = a["x"], a["src"], a["dst"], a["edge_attr_32"]
    i32 = dst.dtype
    src_p = np.concatenate([src, np.zeros(EPAD - E, i32)])
    dst_p = np.concatenate([dst, np.full(EPAD - E + 1, NO_DST, i32)])
    ea_p = np.concatenate([ea, np.zeros((EPAD - E, D), ea.dtype)])
    x_p = np.concatenate([x, np.zeros((NP - N, D), x.dtype)])
    starts0 = [GT * P * k for k in range(GROUPS)]
    ends0 = [min(s + GT * P, E) - 1 for s in starts0]
    starts1 = [[Q * q + 32 * (STEP * (n // 2) + HALF[0] * (n % 2)) for n in range(HALVES)] for q in range(4)]
    ends1 = [[min(s + 32 * HALF[n % 2], E) - 1 for n, s in enumerate(row)] for row in starts1]
    nexts1 = [[s + 32 * HALF[n % 2] for n, s in enumerate(row)] for row in starts1]
    base0 = dst_p[starts0]
    arrays = {
        "xb": x_p.reshape(NB, P, D).transpose(1, 0, 2).reshape(P, NB * D),
        "src0": np.concatenate([src_p, np.zeros(P * ATILES - EPAD, i32)]).reshape(ATILES, P).T,
        "dst0": np.concatenate([dst_p[:-1], np.full(P * ATILES - EPAD, NO_DST, i32)]).reshape(ATILES, P).T,
        "srcq": src_p.reshape(4, TILES, 32).transpose(0, 2, 1).reshape(P, TILES),
        "dstq": np.stack([np.concatenate([np.full(1, -1, i32) if q == 0 else dst_p[Q * q - 1:Q * q], dst_p[Q * q:Q * q + Q]]) for q in range(4)]),
        "eat": ea_p.reshape(4, Q, D).transpose(0, 2, 1).reshape(P, Q),
        "base0": base0, "base0c": np.concatenate([base0, np.full(CHUNK * CHUNKS - GROUPS, NO_DST, i32)]).reshape(CHUNKS, CHUNK).T,
        "last0": dst_p[ends0], "base1": dst_p[starts1], "last1": dst_p[ends1], "next1": dst_p[nexts1],
        "slast": dst_p[[Q * q + Q - 1 for q in range(3)]],
        "dstp": dst_p[:-1], "src": src, "dst": dst, "ea": ea,
        "beta": a["L0_gnn_beta"], "w01": a["L0_gnn_W1"], "b01": a["L0_gnn_b1"], "w02": a["L0_gnn_W2"], "b02": a["L0_gnn_b2"],
        "w11": a["L1_gnn_W1"], "b11": a["L1_gnn_b1"], "w12": a["L1_gnn_W2"], "b12": a["L1_gnn_b2"],
    }
    nc = bacc.Bacc("TRN2", target_bir_lowering=False, num_devices=1)
    feeds, aps = {}, {}
    for name, v in arrays.items():
        v = np.ascontiguousarray(v)
        feeds[f"in_{name}"] = v
        aps[name] = nc.dram_tensor(f"in_{name}", v.shape, mb.dt.from_np(v.dtype), kind="ExternalInput").ap()
    out = nc.dram_tensor("out_0", (P, NB * D), mb.dt.float32, kind="ExternalOutput").ap()
    build(nc, **aps, out=out)
    got = launch(nc, [feeds], core_ids=[0]).results[0]["out_0"]
    return got.reshape(P, NB, D).transpose(1, 0, 2).reshape(NP, D)[:N]
```

```python
from contextlib import ExitStack

import concourse.bass as bass
from concourse import mybir

P = 128
N, D, H, E = 3125, 32, 64, 103125
NB = (N + P - 1) // P
NP = NB * P
NB4 = (NB + 3) // 4
MSG_EPS, LN_EPS = 1e-7, 1e-5

HI = 8
LO = (N + HI - 1) // HI
TILES = (E + P - 1) // P
GT = 3
W0 = P // HI
LATE = 1
GROUPS = (TILES + GT - 1) // GT
ATILES = GT * GROUPS
CHUNK = P // W0
CHUNKS = (GROUPS + CHUNK - 1) // CHUNK
CT = GT * CHUNK
TAIL_GROUPS = GROUPS - CHUNK * (CHUNKS - 1)
PAIRS = CHUNKS // 2 - 1
Q = TILES * 32
HALF = (16, 15)
STEP = sum(HALF)
STEPS = TILES // STEP
W1 = 32
PC = 4
PT = (HALF[0] - PC, HALF[1] - PC)
PW = 32 * PC
MID = N // 2
HALVES = 2 * STEPS
EPAD = 4 * Q
NO_DST = 8000
BIG = 3.0e38
RANGE = 60.0
NOT_FOUND = 1 << 20
COUNT_MAX = 256
GE = 125
GCHUNKS = E // GE
assert E % GE == 0
RING_S = 8
EARLY = 9
RING = 8
RING_W = 4
SIGNS_AT = 2
SIGN_PAIRS = STEPS // 2
assert TILES % STEP == 0 and CHUNKS % 2 == 0 and 2 * SIGN_PAIRS == STEPS and SIGN_PAIRS < PAIRS


def build(nc, xb, src0, dst0, srcq, srcs, dstq, eat, base0, base0c, last0, base1, last1, next1, slast, dstp, src, dst, ea,
          beta, w01, b01, w02, b02, w11, b11, w12, b12, out):
    f32, f16, bf16, i32 = mybir.dt.float32, mybir.dt.float16, mybir.dt.bfloat16, mybir.dt.int32
    ALU, ACT, AX = mybir.AluOpType, mybir.ActivationFunctionType, mybir.AxisListType.X
    ds = bass.ds
    ctx = ExitStack()
    with ctx:
        def sb(name, shape, dt):
            return ctx.enter_context(nc.sbuf_tensor(name, shape, dt))

        def sem(name):
            return ctx.enter_context(nc.semaphore(name))

        g_dram = nc.dram_tensor("g_dram", (NP + 1, 3 * H), bf16).ap()
        b_dram = nc.dram_tensor("b_dram", (512 * NB4, 3 * H), bf16).ap()
        h_dram = nc.dram_tensor("h_dram", (NP, D), f32).ap()
        v_dram = nc.dram_tensor("v_dram", (P * TILES, D), f32).ap()
        end_dram = nc.dram_tensor("end_dram", (NP, 1), i32).ap()

        ident = sb("ident", [P, P], f32)
        diff_i = sb("diff_i", [P, P], f32)
        lo_iota = sb("lo_iota", [P, LO + 1], f16)
        win_iota = sb("win_iota", [P, P, GT], f16)
        part = sb("part", [P, 1], i32)
        part16 = sb("part16", [P, 1], i32)
        part32 = sb("part32", [P, 1], i32)
        part32f = sb("part32f", [P, 1], f32)
        part16f = sb("part16f", [P, 1], f32)
        node_id = sb("node_id", [P, NB], f32)
        ones = sb("ones", [P, P], f32)
        zero_b = sb("zero_b", [P, 512], bf16)
        w01d = sb("w01d", [P, 2, P], f32)
        w02d = sb("w02d", [P, 2, P], f32)
        w1sd = sb("w1sd", [P, 2, P], f32)
        w1dd = sb("w1dd", [P, 2, P], f32)
        w1ed = sb("w1ed", [P, 2, P], f32)
        w12d = sb("w12d", [P, 2, P], f32)
        b01c = sb("b01c", [P, 1], f32)
        b11c = sb("b11c", [P, 1], f32)
        b02r = sb("b02r", [P, D], f32)
        b12r = sb("b12r", [P, D], f32)
        betac = sb("betac", [P, 1], f32)
        x = sb("x", [P, NB, D], f32)
        xc = sb("xc", [P, NB, D], f32)
        sq = sb("sq", [P, NB, D], f32)
        stat = sb("stat", [P, 4, NB], f32)
        h = sb("h", [P, NB, D], f32)
        logit = sb("logit", [P, NB, D], f32)
        g = sb("g", [P, NB, 2, D], f32)
        gs = sb("gs", [P, NB, 3, H], bf16)
        ext = sb("ext", [P, 2, D], f32)
        top = sb("top", [H, 1], f32)
        topd = sb("topd", [H, H], f32)
        topb = sb("topb", [P, 2, D], f32)
        hT = sb("hT", [P, NB * D], f32)
        mT = sb("mT", [P, 2, NB * D], f32)
        x1 = sb("x1", [P, NB, D], f32)
        scan_bufs = sb("scan_bufs", [P, 8 * 512], f32)
        src_i, dst_i = (scan_bufs[:, ATILES * n:ATILES * n + ATILES].bitcast(i32) for n in range(2))
        keys = sb("keys", [P, 5, ATILES], f32)
        srcf, hif, key_win, key_lo = keys[:, 0, :], keys[:, 1:3, :], keys[:, 3, :], keys[:, 4, :]
        key_win16 = srcf.bitcast(f16)[:, 0:ATILES]
        base0_i = sb("base0_i", [P, GROUPS], i32)
        gidx_b = sb("gidx_b", [P, CHUNKS], i32)
        gidx = sb("gidx", [P, CHUNKS], i32)
        grow = sb("grow", [P, CHUNKS, 3 * H], bf16)
        onehot = sb("onehot", [P, RING_W * P * GT + RING * (LO + 1)], f16)
        oh_win = onehot[:, 0:RING_W * P * GT].rearrange("p (r c t) -> p r c t", r=RING_W, t=GT)
        oh_lo = onehot[:, RING_W * P * GT:].rearrange("p (r c) -> p r c", r=RING)
        cg = sb("cg", [P, CHUNK, LO + 1], bf16)
        cnt = sb("cnt", [P, 2, NP], bf16)
        base1_i = sb("base1_i", [P, HALVES], i32)
        next1_i = sb("next1_i", [P, HALVES], i32)
        win_id = sb("win_id", [P, HALVES], f32)
        bias_le = sb("bias_le", [P, HALVES], f32)
        bias_lt = sb("bias_lt", [P, HALVES], f32)
        ends_in = sb("ends_in", [P, HALVES], f32)
        pos_off = sb("pos_off", [P, HALVES], f32)
        dcount = sb("dcount", [P, 2, 512], i32)
        ssum = sb("ssum", [P, 2, 2], f32)
        pc = sb("pc", [P, 8, 2], f32)
        pos_i = sb("pos_i", [P, 2], i32)
        pidx_i = sb("pidx_i", [P, 2], i32)
        end_i = sb("end_i", [P, NB], i32)
        end_t = sb("end_t", [P, 3, NB], i32)
        end_f = sb("end_f", [P, 4, NB], f32)
        end_idx = sb("end_idx", [P, NB], i32)
        srcq_i = sb("srcq_i", [P, TILES + STEP], i32)
        base1r = sb("base1r", [1, 4 * HALVES], i32)
        base1c = sb("base1c", [1, 4 * HALVES], i32)
        idx_st = [sb(f"idx_st{i}", [P, PT[i]], i32) for i in range(2)]
        rows = [sb(f"rows{i}", [P, HALF[i], D], f32) for i in range(2)]
        sgn = [rows[i][:, :, :].rearrange("p t c -> p (t c)").bitcast(bf16) for i in range(2)]
        hsT = [sb(f"hsT{i}", [P, 32 * PT[i]], f32) for i in range(2)]
        eab = [sb(f"eab{i}", [P, 32 * HALF[i]], f32) for i in range(2)]
        dstb = [sb(f"dstb{i}", [P, 32 * HALF[i] + 1], i32) for i in range(2)]
        same, lim = ([scan_bufs[:, 1024 * n + 512 * i:1024 * n + 512 * i + 32 * HALF[i]] for i in range(2)] for n in range(2))
        ohd = [scan_bufs[:, 2048 + 256 * i:2048 + 256 * i + 16 * HALF[i]].bitcast(bf16) for i in range(2)]
        h3 = gs[:, :, :, :].rearrange("p k s c -> p (k s c)")[:, 0:NB * 3 * D].rearrange("p (k s c) -> p k s c", s=3, c=D)
        wins = gs[:, :, :, :].rearrange("p k s c -> p (k s c)")[:, NB * 3 * D:NB * 3 * D + 12 * P].rearrange("p (i s t c) -> p i s t c", i=2, s=2, t=3)
        oh_src = onehot[:, 0:RING * 512].bitcast(bf16).rearrange("p (r c) -> p r c", r=RING)
        srcb = mT[:, :, 0:4 * PW].bitcast(i32)
        srch = logit[:, :, :].rearrange("p k c -> p (k c)").bitcast(f16)[:, 0:8 * PW].rearrange("p (i c) -> p i c", i=2)
        hg3 = g[:, :, :, :].rearrange("p k a c -> p (k a c)")[0:3 * D, 0:8 * PW].rearrange("p (i c) -> p i c", i=2)
        bf = keys[:, :, :].rearrange("p a b -> p (a b)")[:, 0:NB4 * 4 * H]
        b3 = cnt[:, :, :].rearrange("p a b -> p (a b)")[:, 0:NB4 * 4 * 3 * H].rearrange("p (m s c) -> p m s c", s=3, c=H)
        w1s3 = sb("w1s3", [3 * D, H], f32)
        mid_id = sb("mid_id", [P, NB], f32)
        hid = [sb(f"hid{i}", [P, 2, 32 * HALF[i]], f32) for i in range(2)]
        run = [sb(f"run{i}", [P, 32 * HALF[i]], f32) for i in range(2)]
        vrow = [sb(f"vrow{i}", [P, 32 * HALF[i]], f32) for i in range(2)]
        cand = sb("cand", [P, NB, D], f32)
        edge_v = sb("edge_v", [P, 3, D], f32)
        edge_n = sb("edge_n", [P, 3], i32)
        edge_nf = sb("edge_nf", [P, 3], f32)
        edge_p = sb("edge_p", [P, 3, NB], f32)
        tmp = sb("tmp", [P, 3, NB, D], f32)
        res = sb("res", [P, NB, D], f32)
        last0_i = sb("last0_i", [1, GROUPS], i32)
        base0_r = sb("base0_r", [1, GROUPS], i32)
        last1_i = sb("last1_i", [1, 4 * HALVES], i32)
        n_order = (E - 1) // 127
        order_i = tmp[:, :, :, :].rearrange("p a k c -> p (a k c)").bitcast(i32)[0:127, 0:2 * n_order].rearrange("p (a n) -> p a n", a=2)
        n_far = (EPAD - COUNT_MAX) // P
        assert EPAD - E < COUNT_MAX and (EPAD - COUNT_MAX) % P == 0
        far_i = scan_bufs[:, 2 * ATILES:2 * ATILES + 2 * n_far].bitcast(i32).rearrange("p (a n) -> p a n", a=2)
        far_f = srcf[:, 0:n_far]
        order_f = keys[:, :, :].rearrange("p a b -> p (a b)")[0:127, 2 * ATILES:]
        wide0 = sb("wide0", [1, GROUPS], f32)
        wide1 = sb("wide1", [1, 4 * HALVES], f32)
        wide2 = sb("wide2", [1, D], f32)
        broken = sb("broken", [P, 5], f32)
        flag_f = sb("flag_f", [1, 1], f32)
        flag = sb("flag", [1, 1], i32)
        feat = grow[:, :, :].rearrange("p a b -> p (a b)").bitcast(f32)[0:D, 0:NP]
        peak = cnt[:, :, :].rearrange("p a b -> p (a b)").bitcast(f32)[0:D, 0:NP]
        total = keys[:, :, :].rearrange("p a b -> p (a b)")[0:D, 0:NP]
        wsum = scan_bufs[0:D, 0:NP]
        w11f = sb("w11f", [3 * D, H], f32)
        g_src = sb("g_src", [1, GE], i32)
        g_dst = sb("g_dst", [1, GE], i32)
        g_ea = sb("g_ea", [GE, D], f32)
        g_diff = sb("g_diff", [D, GE], f32)
        g_exp = sb("g_exp", [D, GE], f32)
        g_in = sb("g_in", [3 * D, GE], f32)
        g_hid = sb("g_hid", [P, GE], f32)

        ps = [ctx.enter_context(nc.psum_tensor(f"ps{i}", [P, 4, 512], f32)) for i in range(2)]
        ps_cnt = ps[0]
        ps_sum = ps[1][:, :, :].rearrange("p a b -> p (a b)")[:, 0:NB * H].rearrange("p (k c) -> p k c", c=H)

        s_const = sem("s_const")
        s_zero = sem("s_zero")
        s_x = sem("s_x")
        s_edges = sem("s_edges")
        s_win = sem("s_win")
        s_weights = sem("s_weights")
        s_dve = sem("s_dve")
        s_pool = sem("s_pool")
        s_sqrt_in = sem("s_sqrt_in")
        s_sqrt = sem("s_sqrt")
        s_ext = sem("s_ext")
        s_extT = sem("s_extT")
        s_topd = sem("s_topd")
        s_topb = sem("s_topb")
        s_shift = sem("s_shift")
        s_exp = sem("s_exp")
        s_gsplit = sem("s_gsplit")
        s_gtab = sem("s_gtab")
        s_gidx = sem("s_gidx")
        s_grow0 = sem("s_grow0")
        s_grow = sem("s_grow")
        s_onehot = sem("s_onehot")
        s_tile = sem("s_tile")
        s_evac = sem("s_evac")
        s_shuf = [sem(f"s_shuf{i}") for i in range(CHUNK)]
        s_chunk = sem("s_chunk")
        s_dcl = [sem(f"s_dcl{i}") for i in range(2)]
        s_sgn = sem("s_sgn")
        s_used = sem("s_used")
        s_endp = sem("s_endp")
        s_turn = sem("s_turn")
        s_winprep = sem("s_winprep")
        s_endinit = sem("s_endinit")
        s_scat = sem("s_scat")
        s_endld = sem("s_endld")
        s_endidx = sem("s_endidx")
        s_h0T = sem("s_h0T")
        s_m1 = sem("s_m1")
        s_m1r = sem("s_m1r")
        s_m2 = sem("s_m2")
        s_h1 = sem("s_h1")
        s_htab = sem("s_htab")
        s_idx = [sem(f"s_idx{i}") for i in range(2)]
        s_rows = [sem(f"s_rows{i}") for i in range(2)]
        s_ea = [sem(f"s_ea{i}") for i in range(2)]
        s_dst = [sem(f"s_dst{i}") for i in range(2)]
        s_wrow = [sem(f"s_wrow{i}") for i in range(2)]
        s_srcq = sem("s_srcq")
        s_ohd = [sem(f"s_ohd{i}") for i in range(2)]
        s_same = [sem(f"s_same{i}") for i in range(2)]
        s_lim = [sem(f"s_lim{i}") for i in range(2)]
        s_srcb = [sem(f"s_srcb{i}") for i in range(2)]
        s_srch = [sem(f"s_srch{i}") for i in range(2)]
        s_ohs = sem("s_ohs")
        s_gat = sem("s_gat")
        s_hg3 = [sem(f"s_hg3_{i}") for i in range(2)]
        s_hT = sem("s_hT")
        s_bmm = sem("s_bmm")
        s_b3 = sem("s_b3")
        s_btab = sem("s_btab")
        s_h3 = sem("s_h3")
        s_winz = sem("s_winz")
        s_pre = [sem(f"s_pre{i}") for i in range(2)]
        s_hid = [sem(f"s_hid{i}") for i in range(2)]
        s_v = [sem(f"s_v{i}") for i in range(2)]
        s_run = [sem(f"s_run{i}") for i in range(2)]
        s_vrow = [sem(f"s_vrow{i}") for i in range(2)]
        s_vout = [sem(f"s_vout{i}") for i in range(2)]
        s_base1c = sem("s_base1c")
        s_candf = sem("s_candf")
        s_cand = sem("s_cand")
        s_edgev = sem("s_edgev")
        s_res = sem("s_res")
        s_out = sem("s_out")
        s_bounds = sem("s_bounds")
        s_broken = sem("s_broken")
        s_count = sem("s_count")
        s_flag = sem("s_flag")
        s_gidx3 = [sem(f"s_gidx3_{i}") for i in range(3)]
        s_gused = sem("s_gused")
        s_gea = sem("s_gea")
        s_gdiff = sem("s_gdiff")
        s_gexp = sem("s_gexp")
        s_geaT = sem("s_geaT")
        s_gin = sem("s_gin")
        s_gpre = sem("s_gpre")
        s_ghid = sem("s_ghid")
        s_gv = sem("s_gv")
        s_gturn = sem("s_gturn")

        block = ctx.enter_context(nc.Block())

        def windowed(rows_of_streams, w):
            return rows_of_streams.rearrange("q (o c) -> q o c", o=1).to_broadcast([4, W1, w])

        def if_general(eng):
            eng.wait_ge(s_flag, 1)
            eng.wait_ge(s_out, 16)
            return eng.If(eng.value_load(flag[0:1, 0:1], min_val=0, max_val=4 * E) > 0)

        @block.sync
        def _(sp):
            sp.dma_start(x[:, :, :].rearrange("p k c -> p (k c)"), xb).then_inc(s_x, 16)
            sp.dma_start(betac[:, :], beta.rearrange("(o a) -> o a", o=1).to_broadcast([P, 1])).then_inc(s_x, 16)
            sp.dma_start(src_i, src0).then_inc(s_edges, 16)
            sp.dma_start(dst_i, dst0).then_inc(s_edges, 16)
            sp.dma_start(base0_i[:, :], base0.rearrange("(o a) -> o a", o=1).to_broadcast([P, GROUPS])).then_inc(s_edges, 16)
            for r in range(CHUNK):
                sp.dma_start(gidx_b[W0 * r:W0 * r + W0, :], base0c[r:r + 1, :].to_broadcast([W0, CHUNKS])).then_inc(s_win, 16)
            for q in range(4):
                sp.dma_start(base1_i[32 * q:32 * q + 32, :], base1[q:q + 1, :].to_broadcast([32, HALVES])).then_inc(s_win, 16)
                sp.dma_start(next1_i[32 * q:32 * q + 32, :], next1[q:q + 1, :].to_broadcast([32, HALVES])).then_inc(s_win, 16)
            sp.dma_start(base1r[:, :], base1.rearrange("(o q) n -> o (q n)", o=1)).then_inc(s_win, 16)
            sp.dma_start(srcq_i[:, 0:TILES], srcq).then_inc(s_srcq, 16)
            sp.dma_start(last0_i[:, :], last0.rearrange("(o a) -> o a", o=1)).then_inc(s_bounds, 16)
            sp.dma_start(base0_r[:, :], base0.rearrange("(o a) -> o a", o=1)).then_inc(s_bounds, 16)
            sp.dma_start(last1_i[:, :], last1.rearrange("(o q) n -> o (q n)", o=1)).then_inc(s_bounds, 16)
            for i in range(2):
                sp.dma_start(order_i[:, i, :], dst[i:i + E - 1].rearrange("(p n) -> p n", p=127)).then_inc(s_bounds, 16)
            for i in range(2):
                sp.dma_start(far_i[:, i, :], dstp[COUNT_MAX * i:COUNT_MAX * i + P * n_far].rearrange("(p n) -> p n", p=P)).then_inc(s_bounds, 16)
            sp.wait_ge(s_zero, 2)
            sp.dma_start(end_dram.rearrange("(p k) o -> p (k o)", p=P), end_i[:, :]).then_inc(s_endinit, 16)
            sp.dma_start(edge_n[:, :], slast.rearrange("(o a) -> o a", o=1).to_broadcast([P, 3])).then_inc(s_srcq, 16)
            sp.wait_ge(s_gsplit, 1)
            sp.dma_start(g_dram[NP:NP + 1, :], zero_b[0:1, 0:3 * H]).then_inc(s_gtab, 16)
            sp.dma_start(g_dram[0:NP, :].rearrange("(k p) c -> p k c", p=P), gs[:, :, :, :].rearrange("p k s c -> p k (s c)")).then_inc(s_gtab, 16)

            sp.wait_ge(s_zero, 1)
            for q in range(4):
                rq, s, c = slice(32 * q, 32 * q + 32), q // 2, 64 * (q % 2)
                for m, wt in ((w01d, w01[:, :]), (w1sd, w11[0:D, :]), (w1dd, w11[D:2 * D, :]), (w1ed, w11[2 * D:3 * D, :])):
                    sp.dma_start(m[rq, s, c:c + H], wt).then_inc(s_weights, 16)
                for m, wt in ((w02d, w02), (w12d, w12)):
                    sp.dma_start(m[64 * (q % 2):64 * (q % 2) + 64, s, 32 * q:32 * q + 32], wt).then_inc(s_weights, 16)
            for m, b in ((b01c, b01), (b11c, b11)):
                for i in range(2):
                    sp.dma_start(m[64 * i:64 * i + 64, :], b.rearrange("(a o) -> a o", o=1)).then_inc(s_weights, 16)
            for m, b in ((b02r, b02), (b12r, b12)):
                sp.dma_start(m[:, :], b.rearrange("(o a) -> o a", o=1).to_broadcast([P, D])).then_inc(s_weights, 16)
            sp.dma_start(w11f[:, :], w11).then_inc(s_weights, 16)
            for t in range(3):
                sp.dma_start(w1s3[D * t:D * t + D, :], w11[0:D, :]).then_inc(s_weights, 16)
            def shuffle(c0, k, groups, first):
                for j in range(groups):
                    grp = CHUNK * (c0 + k) + j
                    if j == 0 and not first:
                        sp.wait_ge(s_chunk, c0 + k - 1)
                    sp.wait_ge(s_evac, grp + 1)
                    sp.dma_start(cnt[W0 * j:W0 * j + W0, k % 2, 0:HI * LO].rearrange("n (a b) -> n a b", a=HI),
                                 cg[:, j, 0:LO]).then_inc(s_shuf[j], 16)

            shuffle(0, 0, CHUNK, True)
            shuffle(0, 1, CHUNK, True)
            with sp.Fori(1, PAIRS) as it:
                shuffle(2 * it, 0, CHUNK, False)
                shuffle(2 * it, 1, CHUNK, False)
            shuffle(2 * PAIRS, 0, CHUNK, False)
            shuffle(2 * PAIRS, 1, TAIL_GROUPS, False)

            sp.wait_ge(s_h1, 1)
            sp.dma_start(h_dram.rearrange("(k p) c -> p k c", p=P), h[:, :, :]).then_inc(s_htab, 16)
            sp.wait_ge(s_scat, 16 * HALVES)
            sp.dma_start(end_i[:, :], end_dram.rearrange("(k p) o -> p (k o)", p=P), allow_slow_non_contiguous=True).then_inc(s_endld, 16)
            sp.wait_ge(s_b3, 1)
            b3v = b_dram.rearrange("(m k q r) c -> k r m q c", k=4, q=4, r=32)
            for k in range(4):
                for q in range(4):
                    sp.dma_start(b3v[k][:, :, q, :], b3[32 * k:32 * k + 32, :, :, :].rearrange("r (m q) s c -> r m q (s c)", q=4)[:, :, q, :]).then_inc(s_btab, 16)
            sp.wait_ge(s_base1c, 1)
            sp.wait_ge(s_winz, 1)

            def load_half(it, i, first):
                w = 32 * HALF[i]
                c0 = it * (32 * STEP) + 32 * HALF[0] * i
                if not first:
                    sp.wait_ge(s_lim[i], it)
                sp.dma_start(dstb[i][:, :], windowed(dstq[:, ds(c0, w + 1)], w + 1)).then_inc(s_dst[i], 16)
                if not first:
                    sp.wait_ge(s_srch[i], it)
                sp.dma_start(srcb[:, i, :].rearrange("p (q c) -> p q c", q=4),
                             srcs[:, ds(c0 + 32 * PT[i], PW)].rearrange("(o q) c -> o q c", o=1).to_broadcast([P, 4, PW])).then_inc(s_srcb[i], 16)
                if not first:
                    sp.wait_ge(s_pre[i], it)
                sp.dma_start(eab[i][:, :], eat[:, ds(c0, w)]).then_inc(s_ea[i], 16)
                if first and i == 0:
                    sp.wait_ge(s_btab, 256)
                for q in range(4):
                    first_node = sp.value_load(base1c[0:1, ds(2 * it + i + q * HALVES, 1)], min_val=0, max_val=N - W1)
                    sp.dma_start(wins[32 * q:32 * q + 32, i, q // 2, :, 64 * (q % 2):64 * (q % 2) + 64],
                                 b_dram[ds(first_node, W1), :].rearrange("n (s c) -> n s c", s=3)).then_inc(s_wrow[i], 16)

            def store_half(it, i):
                w = HALF[i]
                sp.wait_ge(s_vrow[i], it + 1)
                sp.dma_start(v_dram.rearrange("(p t) c -> p t c", p=P)[:, ds(it * STEP + HALF[0] * i, w), :],
                             vrow[i][:, :].rearrange("p (t c) -> p t c", c=D)).then_inc(s_vout[i], 16)

            load_half(0, 0, True)
            load_half(0, 1, True)
            with sp.Fori(1, STEPS) as it:
                load_half(it, 0, False)
                store_half(it - 1, 0)
                load_half(it, 1, False)
                store_half(it - 1, 1)
            store_half(STEPS - 1, 0)
            store_half(STEPS - 1, 1)
            sp.wait_ge(s_vout[0], 16 * STEPS)
            sp.wait_ge(s_vout[1], 16 * STEPS)
            for q in range(3):
                sp.dma_start(edge_v[:, q, :], v_dram[(32 * q + 32) * TILES - 1:(32 * q + 32) * TILES, :].to_broadcast([P, D])).then_inc(s_edgev, 16)
            sp.wait_ge(s_res, 1)
            sp.dma_start(out, res[:, :, :].rearrange("p k c -> p (k c)")).then_inc(s_out, 16)
            sp.wait_ge(s_out, 16)

            def load_edges(c, at, features):
                sp.wait_ge(s_gused, c + (at + 1))
                sp.dma_start(g_src[:, :], src[ds(c * GE, GE)].rearrange("(o a) -> o a", o=1)).then_inc(s_gidx3[at // GCHUNKS], 16)
                sp.dma_start(g_dst[:, :], dst[ds(c * GE, GE)].rearrange("(o a) -> o a", o=1)).then_inc(s_gidx3[at // GCHUNKS], 16)
                if features:
                    sp.dma_start(g_ea[:, :], ea[ds(c * GE, GE), :]).then_inc(s_gea, 16)

            with if_general(sp):
                for n in range(3):
                    with sp.Fori(0, GCHUNKS) as c:
                        load_edges(c, n * GCHUNKS, n == 2)
                sp.wait_ge(s_res, 2)
                sp.dma_start(out, res[:, :, :].rearrange("p k c -> p (k c)")).then_inc(s_out, 16)
                sp.wait_ge(s_out, 32)

        @block.gpsimd
        def _(gp):
            done = [0]

            def step(ins):
                done[0] += 1
                ins.then_inc(s_pool, 1)
                gp.wait_ge(s_pool, done[0])

            gp.iota(diff_i[:, :], [[1, P]], base=0, channel_multiplier=-1, allow_small_or_imprecise_dtypes=True)
            gp.iota(lo_iota[:, :], [[1, LO + 1]], base=0, channel_multiplier=0, allow_small_or_imprecise_dtypes=True)
            gp.iota(win_iota[:, :, :], [[1, P], [0, GT]], base=0, channel_multiplier=0, allow_small_or_imprecise_dtypes=True)
            gp.iota(node_id[:, :], [[P, NB]], base=0, channel_multiplier=1, allow_small_or_imprecise_dtypes=True)
            for i in range(2):
                gp.iota(pos_off[:, :].rearrange("p (s i) -> p s i", i=2)[:, :, i], [[32 * STEP, STEPS]],
                        base=32 * HALF[0] * i - 1 + 16 * HALF[i], channel_multiplier=0, allow_small_or_imprecise_dtypes=True)
            gp.iota(part[:, :], [[0, 1]], base=0, channel_multiplier=1).then_inc(s_const, 1)
            for m in (w01d, w1sd, w1dd, w1ed, w02d):
                gp.memset(m[:, :, :], 0.0)
            gp.memset(w12d[:, :, :], 0.0).then_inc(s_zero, 1)
            gp.memset(end_i[:, :], NOT_FOUND).then_inc(s_zero, 1)
            gp.memset(srcq_i[:, TILES:], 0)
            gp.memset(cand[:, :, :], -BIG).then_inc(s_candf, 1)
            gp.memset(cnt[:, :, HI * LO:], 0.0)
            gp.memset(run[1][:, :], -BIG)
            gp.memset(pc[:, :, :], 0.0).then_inc(s_zero, 1)
            gp.wait_ge(s_gidx, 1)
            gp.wait_ge(s_gtab, 32)
            for c in range(CHUNKS):
                gp.indirect_dma_start(grow[:, c, :], None, g_dram[:, :], bass.IndirectOffsetOnAxis(gidx[:, c:c + 1], 0)).then_inc(s_grow0 if c == 0 else s_grow, 16)

            gp.wait_ge(s_winprep, 1)
            gp.wait_ge(s_endinit, 16)

            def load_count_dst(it, first):
                for i in range(2):
                    c0 = it * (32 * STEP) + 32 * HALF[0] * i
                    w = 32 * HALF[i]
                    gp.dma_start(dcount[:, i, 0:w], windowed(dstq[:, ds(c0 + 1, w)], w)).then_inc(s_dcl[i], 16)

            def ends(it, first):
                at = [0]

                def link(ins):
                    at[0] += 1
                    ins.then_inc(s_endp, 1)
                    gp.wait_ge(s_endp, it * LINKS + at[0])
                    gp.sem_inc(s_turn, 1)

                for k, m in ((0, pos_off), (1, win_id), (2, ends_in)):
                    gp.tensor_copy(pc[:, k, :], m[:, ds(2 * it, 2)])
                gp.wait_ge(s_sgn, it + 1)
                gp.sem_inc(s_turn, 1)
                link(gp.tensor_scalar(pc[:, 3, :], ssum[:, 0, :], -0.5, None, ALU.mult))
                link(gp.tensor_tensor(pc[:, 4, :], ssum[:, 1, :], ssum[:, 0, :], ALU.subtract))
                link(gp.tensor_scalar(pc[:, 4, :], pc[:, 4, :], 0.5, None, ALU.is_gt))
                link(gp.tensor_tensor(pc[:, 5, :], pc[:, 4, :], pc[:, 2, :], ALU.mult))
                link(gp.tensor_tensor(pc[:, 3, :], pc[:, 3, :], pc[:, 0, :], ALU.add))
                link(gp.tensor_scalar(pc[:, 6, :], pc[:, 5, :], -float(NOT_FOUND), float(NOT_FOUND), ALU.mult, ALU.add))
                link(gp.tensor_tensor(pc[:, 6, :], pc[:, 6, :], pc[:, 1, :], ALU.add))
                if not first:
                    gp.wait_ge(s_scat, it * 32)
                    gp.sem_inc(s_turn, 1)
                gp.tensor_copy(pos_i[:, :], pc[:, 3, :])
                gp.tensor_copy(pidx_i[:, :], pc[:, 6, :]).then_inc(s_used, 1)
                gp.wait_ge(s_used, it + 2)
                gp.sem_inc(s_turn, 1)
                for i in range(2):
                    gp.indirect_dma_start(end_dram[:, :], bass.IndirectOffsetOnAxis(pidx_i[:, i:i + 1], 0), pos_i[:, i:i + 1], None,
                                          bounds_check=NP - 1, oob_is_err=False).then_inc(s_scat, 16)

            LINKS = 7
            gp.sem_inc(s_used, 1)
            load_count_dst(0, True)
            gp.wait_ge(s_sgn, 1)
            load_count_dst(1, False)
            ends(0, True)
            with gp.Fori(1, STEPS - 1) as it:
                gp.wait_ge(s_sgn, it + 1)
                gp.sem_inc(s_turn, 1)
                load_count_dst(it + 1, False)
                ends(it, False)
            ends(STEPS - 1, False)

            gp.wait_ge(s_htab, 16)
            with gp.Fori(0, STEPS) as it:
                for i in range(2):
                    gp.wait_ge(s_idx[i], it + 1)
                    gp.sem_inc(s_turn, 1)
                    for t in range(PT[i]):
                        gp.indirect_dma_start(rows[i][:, t, :], None, h_dram[:, :],
                                              bass.IndirectOffsetOnAxis(idx_st[i][:, t:t + 1], 0)).then_inc(s_rows[i], 16)
            gp.wait_ge(s_endidx, 1)
            gp.wait_ge(s_candf, 1)
            gp.wait_ge(s_vout[0], 16 * STEPS)
            gp.wait_ge(s_vout[1], 16 * STEPS)
            for k in range(NB):
                gp.indirect_dma_start(cand[:, k, :], None, v_dram[:, :], bass.IndirectOffsetOnAxis(end_idx[:, k:k + 1], 0),
                                      bounds_check=P * TILES - 1, oob_is_err=False).then_inc(s_cand, 16)

        @block.scalar
        def _(act):
            act.wait_ge(s_sqrt_in, 1)
            nc.scalar.activation(stat[:, 2, :], stat[:, 1, :], ACT.Sqrt).then_inc(s_sqrt, 1)
            act.wait_ge(s_shift, 1)
            nc.scalar.activation(g[:, :, 0, :], logit[:, :, :], ACT.Exp).then_inc(s_exp, 1)
            act.wait_ge(s_winprep, 1)

            def evac(c0, k, j0, j1, first):
                for j in range(j0, j1):
                    grp = CHUNK * (c0 + k) + j
                    if not (first and k == 0):
                        act.wait_ge(s_shuf[j], 16 * (c0 + k))
                    act.wait_ge(s_tile, GT * grp + GT)
                    nc.scalar.activation(cg[:, j, 0:LO], ps_cnt[:, j % 4, 0:LO], ACT.Copy).then_inc(s_evac, 1)

            def sign(step_, i, b):
                w = 32 * HALF[i]
                m = (bias_le, bias_lt)[b]
                if b == 0:
                    act.wait_ge(s_dcl[i], step_ * 16 + 16)
                if b == 0 and i == 0:
                    act.wait_ge(s_used, step_ + 1)
                last = nc.scalar.activation(sgn[i][:, w * b:w * b + w], dcount[:, i, 0:w], ACT.Sign, bias=m[:, ds(2 * step_ + i, 1)],
                                            accum_out=ssum[:, b, i:i + 1])
                if b == 1 and i == 1:
                    last.then_inc(s_sgn, 1)

            def count_pair(it, first, with_signs, groups):
                for k, n in enumerate((CHUNK, groups)):
                    for j in range(n):
                        evac(2 * it, k, j, j + 1, first)
                        if with_signs and 0 <= j - SIGNS_AT < 4:
                            sign(2 * it - 2 + k, (j - SIGNS_AT) // 2, (j - SIGNS_AT) % 2)

            count_pair(0, True, False, CHUNK)
            with act.Fori(1, SIGN_PAIRS + 1) as it:
                count_pair(it, False, True, CHUNK)
            with act.Fori(SIGN_PAIRS + 1, PAIRS) as it:
                count_pair(it, False, False, CHUNK)
            count_pair(PAIRS, False, False, TAIL_GROUPS)

            def root(n):
                act.wait_ge(s_sqrt_in, n)
                nc.scalar.activation(stat[:, 2, :], stat[:, 1, :], ACT.Sqrt).then_inc(s_sqrt, 1)

            def first_mlp(r):
                for f in range(2):
                    for s in range(2):
                        act.wait_ge(s_m1, 4 * r + 2 * f + s + 1)
                        nc.scalar.activation(mT[:, s, 400 * f:400 * f + 400], ps[0][:, s, 0:400], ACT.Relu, bias=b01c[:, 0:1]).then_inc(s_m1r, 1)

            act.wait_ge(s_weights, 16 * 34)
            first_mlp(0)
            root(2)

            def gathered(it, i, first):
                if not first:
                    act.wait_ge(s_pre[i], it)
                act.wait_ge(s_gat, NB * (2 * it + i + 1))
                nc.scalar.activation(hg3[:, i, :], ps[i][0:3 * D, 0, 0:4 * PW], ACT.Copy).then_inc(s_hg3[i], 1)

            def hidden(it, i, first):
                w = 32 * HALF[i]
                if not first:
                    act.wait_ge(s_v[i], it)
                act.wait_ge(s_pre[i], it + 1)
                for s in range(2):
                    last = nc.scalar.activation(hid[i][:, s, :], ps[i][:, 1 + s, 0:w], ACT.Relu, bias=b11c[:, 0:1])
                last.then_inc(s_hid[i], 1)

            gathered(0, 0, True)
            hidden(0, 0, True)
            gathered(0, 1, True)
            hidden(0, 1, True)
            gathered(1, 0, False)
            with act.Fori(1, STEPS - 1) as it:
                hidden(it, 0, False)
                gathered(it, 1, False)
                hidden(it, 1, False)
                gathered(it + 1, 0, False)
            hidden(STEPS - 1, 0, False)
            gathered(STEPS - 1, 1, False)
            hidden(STEPS - 1, 1, False)

            with if_general(act):
                root(3)
                with act.Fori(0, GCHUNKS) as c:
                    act.wait_ge(s_gdiff, c + 1)
                    nc.scalar.activation(g_exp[:, :], g_diff[:, :], ACT.Exp).then_inc(s_gexp, 1)
                first_mlp(1)
                root(4)
                with act.Fori(0, GCHUNKS) as c:
                    act.wait_ge(s_gpre, c + 1)
                    nc.scalar.activation(g_hid[0:H, :], ps[0][0:H, 1, 0:GE], ACT.Relu, bias=b11c[0:H, 0:1]).then_inc(s_ghid, 1)

        @block.tensor
        def _(pe):
            pe.wait_ge(s_ext, 1)
            nc.tensor.transpose(ps[0][0:H, 0, 0:P], ext[:, :, :].rearrange("p a c -> p (a c)"), ident[:, :]).then_inc(s_extT, 1)
            pe.wait_ge(s_topd, 1)
            nc.tensor.matmul(ps[0][:, 1, 0:H], ones[0:H, :], topd[:, :], start=True, stop=True).then_inc(s_topb, 1)
            for b in range(4):
                nc.tensor.matmul(ps[1][:, b, :], zero_b[:, 0:P], zero_b[:, :], start=True, stop=False, skip_group_check=True)

            def count_tile(c0, u, first):
                if u % GT == 0 and not (first and u < 4 * GT):
                    pe.wait_ge(s_evac, CHUNK * c0 + u // GT - 3)
                pe.wait_ge(s_onehot, CT * c0 + u + 1)
                nc.tensor.matmul(ps_cnt[:, (u // GT) % 4, 0:LO], oh_win[:, (u // GT) % RING_W, :, u % GT], oh_lo[:, u % RING, 0:LO],
                                 start=(u % GT == 0), stop=(u % GT == GT - 1)).then_inc(s_tile, 1)

            def sum_blocks(c, k, b0, b1):
                for b in range(b0, b1):
                    for part_ in range(3):
                        last = nc.tensor.matmul(ps_sum[:, b, :], cnt[:, k, P * b:P * b + P], grow_of(c)[:, H * part_:H * part_ + H],
                                                start=False, stop=False, skip_group_check=True)
                if b1 == NB:
                    last.then_inc(s_chunk, 1)

            def grow_of(c):
                return grow[:, ds(c, 1), :].rearrange("p a n -> p (a n)")

            def chunk_ready(c):
                for r in range(CHUNK):
                    pe.wait_ge(s_shuf[r], 16 * (c + 1))

            def count_chunk(c0, k, tiles, first):
                late = tiles // 2 + LATE
                for u in range(tiles):
                    count_tile(c0, u + CT * k, first)
                    if first and k == 0 or u < late:
                        continue
                    if u == late:
                        if first:
                            pe.wait_ge(s_grow0, 16)
                            pe.wait_ge(s_zero, 3)
                        else:
                            pe.wait_ge(s_grow, 16 * (CHUNKS - 1))
                        chunk_ready(c0 + k - 1)
                    n = tiles - late
                    sum_blocks(c0 + k - 1, (k + 1) % 2, NB * (u - late) // n, NB * (u - late + 1) // n)

            count_chunk(0, 0, CT, True)
            count_chunk(0, 1, CT, True)
            with pe.Fori(1, PAIRS) as it:
                count_chunk(2 * it, 0, CT, False)
                count_chunk(2 * it, 1, CT, False)
            count_chunk(2 * PAIRS, 0, CT, False)
            count_chunk(2 * PAIRS, 1, GT * TAIL_GROUPS, False)
            for r in range(TAIL_GROUPS):
                pe.wait_ge(s_shuf[r], 16 * CHUNKS)
            sum_blocks(CHUNKS - 1, (CHUNKS - 1) % 2, 0, NB)

            def first_mlp(r):
                pe.wait_ge(s_h0T, r + 1)
                for f in range(2):
                    for s in range(2):
                        if f:
                            pe.wait_ge(s_m1r, 4 * r + s + 1)
                        nc.tensor.matmul(ps[0][:, s, 0:400], w01d[:, s, :], hT[:, 400 * f:400 * f + 400], start=True, stop=True).then_inc(s_m1, 1)
                for f in range(2):
                    pe.wait_ge(s_m1r, 4 * r + 2 * f + 2)
                    for s in range(2):
                        last = nc.tensor.matmul(ps[0][:, 2 + f, 0:400], w02d[:, s, :], mT[:, s, 400 * f:400 * f + 400], start=(s == 0), stop=(s == 1))
                    last.then_inc(s_m2, 1)

            pe.wait_ge(s_weights, 16 * 34)
            first_mlp(0)
            pe.wait_ge(s_hT, 1)
            for k in range(NB):
                m, kk = k // 4, k % 4
                last = nc.tensor.matmul(ps[1][:, :, :].rearrange("p a b -> p (a b)")[32 * kk:32 * kk + 32, 4 * H * m:4 * H * m + 4 * H],
                                        hT[:, 32 * k:32 * k + 32], w1dd[:, :, :].rearrange("p s c -> p (s c)"), start=True, stop=True, skip_group_check=True)
            for kk in range(NB % 4, 4):
                last = nc.tensor.matmul(ps[1][:, :, :].rearrange("p a b -> p (a b)")[32 * kk:32 * kk + 32, 4 * H * (NB4 - 1):4 * H * NB4],
                                        zero_b[:, 0:32], zero_b[:, 0:4 * H], start=True, stop=True, skip_group_check=True)
            last.then_inc(s_bmm, 1)

            def gather(it, i, k0, k1, first):
                if k0 == 0 and not first:
                    pe.wait_ge(s_hg3[i], it)
                for k in range(k0, k1):
                    pe.wait_ge(s_ohs, NB * (2 * it + i) + k + 1)
                    nc.tensor.matmul(ps[i][0:3 * D, 0, 0:4 * PW], h3[:, k, :, :].rearrange("p s c -> p (s c)"), oh_src[:, k % RING_S, :],
                                     start=(k == 0), stop=(k == NB - 1)).then_inc(s_gat, 1)

            def layers(it, i, first, beside=None):
                w, wp = 32 * HALF[i], 32 * PT[i]
                add = dict(start=False, stop=False, skip_group_check=True)
                pe.wait_ge(s_ea[i], 16 * it + 16)
                if not first:
                    pe.wait_ge(s_hid[i], it)
                for s in range(2):
                    nc.tensor.matmul(ps[i][:, 1 + s, 0:w], w1ed[:, s, :], eab[i][:, :], start=True, stop=False, skip_group_check=True)
                pe.wait_ge(s_wrow[i], 64 * it + 64)
                pe.wait_ge(s_ohd[i], it + 1)
                for s in range(2):
                    for t in range(3):
                        nc.tensor.matmul(ps[i][:, 1 + s, 0:w], wins[:, i, s, t, :], ohd[i], **add)
                pe.wait_ge(s_hg3[i], it + 1)
                for q in range(4):
                    nc.tensor.matmul(ps[i][64 * (q % 2):64 * (q % 2) + 64, 1 + q // 2, wp:w], w1s3[:, :], hg3[:, i, PW * q:PW * q + PW], **add)
                pe.wait_ge(s_idx[i], it + 2)
                for s in range(2):
                    last = nc.tensor.matmul(ps[i][:, 1 + s, 0:wp], w1sd[:, s, :], hsT[i][:, :], **add)
                last.then_inc(s_pre[i], 1)
                if beside:
                    gather(beside[0], beside[1], 0, EARLY, beside[2])
                pe.wait_ge(s_hid[i], it + 1)
                if not first:
                    pe.wait_ge(s_run[i], it)
                for s in range(2):
                    last = nc.tensor.matmul(ps[i][64 * s:64 * s + 64, 3, 0:w], w12d[:, s, 64 * s:64 * s + 64], hid[i][:, s, :], start=True, stop=True)
                last.then_inc(s_v[i], 1)
                if beside:
                    gather(beside[0], beside[1], EARLY, NB, beside[2])

            pe.wait_ge(s_b3, 1)
            pe.wait_ge(s_broken, 1)
            nc.tensor.matmul(ps[1][0:1, 0, 0:5], ones[:, 0:1], broken[:, :], start=True, stop=True).then_inc(s_count, 1)

            pe.wait_ge(s_h3, 1)
            gather(0, 0, 0, NB, True)
            layers(0, 0, True, (0, 1, True))
            layers(0, 1, True, (1, 0, False))
            with pe.Fori(1, STEPS - 1) as it:
                layers(it, 0, False, (it, 1, False))
                layers(it, 1, False, (it + 1, 0, False))
            layers(STEPS - 1, 0, False, (STEPS - 1, 1, False))
            layers(STEPS - 1, 1, False)

            with if_general(pe):
                first_mlp(1)
                pe.wait_ge(s_h1, 2)
                with pe.Fori(0, GCHUNKS) as c:
                    pe.wait_ge(s_gea, 16 * c + 16)
                    nc.tensor.transpose(ps[0][0:D, 0, 0:GE], g_ea[:, :], ident[0:GE, 0:GE]).then_inc(s_geaT, 1)
                    pe.wait_ge(s_gin, c + 1)
                    nc.tensor.matmul(ps[0][0:H, 1, 0:GE], w11f[:, :], g_in[:, :], start=True, stop=True).then_inc(s_gpre, 1)
                    pe.wait_ge(s_ghid, c + 1)
                    nc.tensor.matmul(ps[0][:, 2, 0:GE], w12d[:, 0, :], g_hid[:, :], start=True, stop=True).then_inc(s_gv, 1)

        @block.vector
        def _(ve):
            done = [0]
            V = nc.vector

            def step(ins):
                done[0] += 1
                ins.then_inc(s_dve, 1)
                ve.wait_ge(s_dve, done[0])

            def bc(col):
                return col.rearrange("p (k o) -> p k o", o=1).to_broadcast([P, NB, D])

            def chan(row):
                return row.rearrange("p (o c) -> p o c", o=1).to_broadcast([P, NB, D])

            def norm_relu(src, n):
                step(V.reduce_sum(stat[:, 0, :], src, AX))
                step(V.tensor_scalar(stat[:, 0, :], stat[:, 0, :], 1.0 / D, None, ALU.mult))
                step(V.tensor_tensor(xc[:, :, :], src, bc(stat[:, 0, :]), ALU.subtract))
                step(V.tensor_tensor(sq[:, :, :], xc[:, :, :], xc[:, :, :], ALU.mult))
                step(V.reduce_sum(stat[:, 1, :], sq[:, :, :], AX))
                V.tensor_scalar(stat[:, 1, :], stat[:, 1, :], 1.0 / D, LN_EPS, ALU.mult, ALU.add).then_inc(s_sqrt_in, 1)
                ve.wait_ge(s_sqrt, n)
                step(V.reciprocal(stat[:, 3, :], stat[:, 2, :]))
                return V.scalar_tensor_tensor(h[:, :, :], xc[:, :, :], 0.0, bc(stat[:, 3, :]), ALU.max, ALU.mult)

            V.memset(ones[:, :], 1.0)
            V.memset(zero_b[:, :], 0.0)
            ve.wait_ge(s_const, 1)
            step(V.tensor_scalar(ident[:, :], diff_i[:, :], 0.0, None, ALU.is_equal))
            ve.wait_ge(s_x, 32)
            step(norm_relu(x[:, :, :], 1))
            step(V.tensor_scalar(h[:, :, :], h[:, :, :], MSG_EPS, None, ALU.add))
            step(V.tensor_scalar(logit[:, :, :], h[:, :, :], betac[:, 0:1], None, ALU.mult))
            step(V.tensor_scalar(sq[:, :, :], logit[:, :, :], -1.0, None, ALU.mult))
            step(V.reduce_max(ext[:, 0, :], logit[:, :, :].rearrange("p k c -> p c k"), AX))
            V.reduce_max(ext[:, 1, :], sq[:, :, :].rearrange("p k c -> p c k"), AX).then_inc(s_ext, 1)
            ve.wait_ge(s_extT, 1)
            step(V.reduce_max(top[:, :], ps[0][0:H, 0, 0:P], AX))
            V.tensor_scalar(topd[:, :], ident[0:H, 0:H], top[:, 0:1], None, ALU.mult).then_inc(s_topd, 1)
            ve.wait_ge(s_topb, 1)
            step(V.tensor_copy(topb[:, :, :].rearrange("p a c -> p (a c)"), ps[0][:, 1, 0:H]))
            V.tensor_tensor(logit[:, :, :], logit[:, :, :], chan(topb[:, 0, :]), ALU.subtract).then_inc(s_shift, 1)
            ve.wait_ge(s_exp, 1)
            step(V.tensor_tensor(g[:, :, 1, :], g[:, :, 0, :], h[:, :, :], ALU.mult))
            gf = g[:, :, :, :].rearrange("p k a c -> p k (a c)")
            step(V.tensor_copy(gs[:, :, 0, :], gf))
            step(V.tensor_tensor(gf, gf, gs[:, :, 0, :], ALU.subtract))
            step(V.tensor_copy(gs[:, :, 1, :], gf))
            step(V.tensor_tensor(gf, gf, gs[:, :, 1, :], ALU.subtract))
            V.tensor_copy(gs[:, :, 2, :], gf).then_inc(s_gsplit, 1)

            ve.wait_ge(s_win, 16 * (CHUNK + 9))
            step(V.tensor_scalar(part16[:, :], part[:, :], W0 - 1, None, ALU.bitwise_and))
            step(V.tensor_scalar(part32[:, :], part[:, :], W1 - 1, None, ALU.bitwise_and))
            step(V.tensor_copy(part16f[:, :], part16[:, :]))
            step(V.tensor_copy(part32f[:, :], part32[:, :]))
            V.tensor_scalar(gidx[:, :], gidx_b[:, :], part16f[:, 0:1], float(NP), ALU.add, ALU.min).then_inc(s_gidx, 1)
            step(V.tensor_scalar(base1c[:, :], base1r[:, :], float(N - W1), None, ALU.min))
            V.tensor_scalar(base1c[:, :], base1c[:, :], 0.0, None, ALU.max).then_inc(s_base1c, 1)
            step(V.tensor_scalar(win_id[:, :], base1_i[:, :], float(N - W1), part32f[:, 0:1], ALU.min, ALU.add))
            step(V.tensor_tensor(ends_in[:, :], next1_i[:, :], win_id[:, :], ALU.is_gt))
            step(V.tensor_scalar(bias_le[:, :], win_id[:, :], -1.0, -0.5, ALU.mult, ALU.add))
            step(V.tensor_scalar(part32[:, :], part[:, :], 5, 15, ALU.arith_shift_right, ALU.logical_shift_left))
            step(V.tensor_copy(part16f[:, :], part32[:, :]))
            step(V.tensor_scalar(pos_off[:, :], pos_off[:, :], part16f[:, 0:1], None, ALU.add))
            V.tensor_scalar(bias_lt[:, :], win_id[:, :], -1.0, 0.5, ALU.mult, ALU.add).then_inc(s_winprep, 1)

            def stage(it, i):
                return V.tensor_copy(idx_st[i][:, :], srcq_i[:, ds(it * STEP + HALF[0] * i, PT[i])])

            ve.wait_ge(s_srcq, 32)
            ve.wait_ge(s_zero, 3)
            for i in range(2):
                stage(0, i).then_inc(s_idx[i], 1)
            step(V.tensor_scalar(mid_id[:, :], node_id[:, :], float(MID), None, ALU.subtract))
            ve.wait_ge(s_edges, 48)
            step(V.tensor_copy(srcf, src_i))
            step(V.tensor_scalar(hif[:, 0, :], srcf, float(LO), None, ALU.is_ge))
            for k in range(2, HI):
                step(V.scalar_tensor_tensor(hif[:, (k + 1) % 2, :], srcf, float(k * LO), hif[:, k % 2, :], ALU.is_ge, ALU.add))
            hi = hif[:, (HI - 1 + 1) % 2, :]
            step(V.scalar_tensor_tensor(key_lo, hi, -float(LO), srcf, ALU.mult, ALU.add))
            step(V.tensor_tensor(key_win.rearrange("p (g t) -> p g t", t=GT), dst_i.rearrange("p (g t) -> p g t", t=GT),
                                 base0_i[:, :].rearrange("p (g o) -> p g o", o=1).to_broadcast([P, GROUPS, GT]), ALU.subtract))
            step(V.scalar_tensor_tensor(key_win16, key_win, float(HI), hi, ALU.mult, ALU.add))

            def onehots(it, tiles, first):
                for u in range(tiles):
                    if u % GT == 0:
                        if not (first and u < RING_W * GT):
                            ve.wait_ge(s_tile, 2 * CT * it + u - (RING_W - 1) * GT)
                        V.tensor_tensor(oh_win[:, (u // GT) % RING_W, :, :], win_iota[:, :, :],
                                        key_win16[:, ds(2 * CT * it + u, GT)].rearrange("p (o t) -> p o t", o=1).to_broadcast([P, P, GT]), ALU.is_equal)
                    if not (first and u < RING):
                        ve.wait_ge(s_tile, 2 * CT * it + u - (RING - 1))
                    V.tensor_scalar(oh_lo[:, u % RING, :], lo_iota[:, :], key_lo[:, ds(2 * CT * it + u, 1)], None, ALU.is_equal).then_inc(s_onehot, 1)

            onehots(0, 2 * CT, True)
            with ve.Fori(1, PAIRS) as it:
                onehots(it, 2 * CT, False)
            onehots(PAIRS, CT + GT * TAIL_GROUPS, False)

            ve.wait_ge(s_chunk, CHUNKS)
            step(V.tensor_scalar(sq[:, :, :], ps_sum[:, :, 0:D], 1e-38, None, ALU.max))
            step(V.reciprocal(logit[:, :, :], sq[:, :, :]))
            step(V.tensor_tensor(xc[:, :, :], ps_sum[:, :, D:2 * D], logit[:, :, :], ALU.mult))
            V.transpose(hT[:, :], xc[:, :, :].rearrange("p k c -> p (k c)")).then_inc(s_h0T, 1)
            def after_mlp(r):
                for f in range(2):
                    ve.wait_ge(s_m2, 2 * r + f + 1)
                    step(V.tensor_copy(mT[:, 0, 400 * f:400 * f + 400], ps[0][:, 2 + f, 0:400]))
                step(V.transpose(sq[:, :, :].rearrange("p k c -> p (k c)"), mT[:, 0, :]))
                step(V.tensor_tensor(sq[:, :, :], sq[:, :, :], chan(b02r[:, :]), ALU.add))
                step(V.tensor_tensor(x1[:, :, :], sq[:, :, :], x[:, :, :], ALU.add))
                norm_relu(x1[:, :, :], 2 * r + 2).then_inc(s_h1, 1)

            ve.wait_ge(s_weights, 16 * 34)
            ve.wait_ge(s_gtab, 32)
            V.memset(wins, 0.0).then_inc(s_winz, 1)
            after_mlp(0)

            def three_parts(parts, value):
                step(V.tensor_copy(parts[0], value))
                step(V.tensor_tensor(value, value, parts[0], ALU.subtract))
                step(V.tensor_copy(parts[1], value))
                step(V.tensor_tensor(value, value, parts[1], ALU.subtract))
                return V.tensor_copy(parts[2], value)

            ve.wait_ge(s_h1, 1)
            V.transpose(hT[:, :], h[:, :, :].rearrange("p k c -> p (k c)")).then_inc(s_hT, 1)
            step(V.tensor_copy(sq[:, :, :], h[:, :, :]))
            three_parts([h3[:, :, t, :] for t in range(3)], sq[:, :, :]).then_inc(s_h3, 1)
            ve.wait_ge(s_bmm, 1)
            step(V.tensor_copy(bf, ps[1][:, :, :].rearrange("p a b -> p (a b)")[:, 0:NB4 * 4 * H]))
            three_parts([b3[:, :, t, :] for t in range(3)], bf.rearrange("p (m c) -> p m c", c=H)).then_inc(s_b3, 1)

            step(V.memset(broken[:, :], 0.0))
            ve.wait_ge(s_bounds, 112)
            step(V.tensor_tensor(wide0[:, :], last0_i[:, :], base0_r[:, :], ALU.subtract))
            step(V.tensor_scalar(wide0[:, :], wide0[:, :], float(W0 - 1), None, ALU.is_gt))
            step(V.tensor_tensor(wide1[:, :], last1_i[:, :], base1c[:, :], ALU.subtract))
            step(V.tensor_scalar(wide1[:, :], wide1[:, :], float(W1 - 1), None, ALU.is_gt))
            step(V.tensor_tensor(order_f[:, 0:n_order], order_i[:, 0, :], order_i[:, 1, :], ALU.is_gt))
            step(V.tensor_tensor(wide2[:, :], topb[0:1, 0, :], topb[0:1, 1, :], ALU.add))
            step(V.tensor_scalar(wide2[:, :], wide2[:, :], RANGE, None, ALU.is_gt))
            step(V.tensor_tensor(far_f, far_i[:, 0, :], far_i[:, 1, :], ALU.is_equal))
            step(V.reduce_sum(broken[:, 4:5], far_f, AX))
            step(V.reduce_sum(broken[0:1, 0:1], wide0[:, :], AX))
            step(V.reduce_sum(broken[0:1, 1:2], wide1[:, :], AX))
            step(V.reduce_sum(broken[0:127, 2:3], order_f[:, 0:n_order], AX))
            V.reduce_sum(broken[0:1, 3:4], wide2[:, :], AX).then_inc(s_broken, 1)
            ve.wait_ge(s_count, 1)
            step(V.reduce_sum(flag_f[:, :], ps[1][0:1, 0, 0:5], AX))
            V.tensor_copy(flag[:, :], flag_f[:, :]).then_inc(s_flag, 1)

            ve.wait_ge(s_endld, 16)
            step(V.tensor_scalar(end_t[:, 0, :], end_i[:, :], 15, None, ALU.arith_shift_right))
            step(V.tensor_scalar(end_t[:, 1, :], end_i[:, :], 31, None, ALU.bitwise_and))
            step(V.tensor_scalar(end_t[:, 2, :], end_i[:, :], (1 << 15) - 1, None, ALU.bitwise_and))
            step(V.tensor_scalar(end_t[:, 2, :], end_t[:, 2, :], 5, None, ALU.arith_shift_right))
            step(V.tensor_copy(end_f[:, 0:3, :], end_t[:, :, :]))
            step(V.scalar_tensor_tensor(end_f[:, 3, :], end_f[:, 0, :], 32.0, end_f[:, 1, :], ALU.mult, ALU.add))
            V.scalar_tensor_tensor(end_idx[:, :], end_f[:, 3, :], float(TILES), end_f[:, 2, :], ALU.mult, ALU.add).then_inc(s_endidx, 1)
            ve.wait_ge(s_srcq, 32)
            step(V.tensor_copy(edge_nf[:, :], edge_n[:, :]))
            for q in range(3):
                step(V.tensor_scalar(edge_p[:, q, :], node_id[:, :], edge_nf[:, q:q + 1], None, ALU.is_equal))
            step(V.tensor_scalar(edge_p[:, :, :], edge_p[:, :, :], 1.0, BIG, ALU.subtract, ALU.mult))


            def finish():
                step(V.tensor_tensor(cand[:, :, :], cand[:, :, :], chan(b12r[:, :]), ALU.add))
                step(V.tensor_tensor(cand[:, :, :], cand[:, :, :], h[:, :, :], ALU.max))
                V.tensor_tensor(res[:, :, :], cand[:, :, :], x1[:, :, :], ALU.add).then_inc(s_res, 1)

            def last_use(slot):
                return max(k for k in range(NB) if k % RING_S == slot)

            def prepare(it, i, first):
                w = 32 * HALF[i]
                ve.wait_ge(s_dst[i], 16 * it + 16)
                if not first:
                    ve.wait_ge(s_pre[i], it)
                V.tensor_scalar(ohd[i], dstb[i][:, 1:w + 1], win_id[:, ds(2 * it + i, 1)], None, ALU.is_equal).then_inc(s_ohd[i], 1)
                V.tensor_tensor(same[i], dstb[i][:, 1:w + 1], dstb[i][:, 0:w], ALU.is_equal).then_inc(s_same[i], 1)
                ve.wait_ge(s_srcb[i], 16 * it + 16)
                if not first:
                    ve.wait_ge(s_gat, NB * (2 * it + i - 1))
                V.tensor_scalar(srch[:, i, :], srcb[:, i, :], float(MID), None, ALU.subtract).then_inc(s_srch[i], 1)
                ve.wait_ge(s_same[i], it + 1)
                V.tensor_scalar(lim[i], same[i], 0.5, 3.4e38, ALU.subtract, ALU.mult).then_inc(s_lim[i], 1)
                ve.wait_ge(s_srch[i], it + 1)
                for k in range(NB):
                    if not (first and i == 0 and k < RING_S):
                        ve.wait_ge(s_gat, NB * (2 * it + i) + (k - (RING_S - 1) if k >= RING_S else last_use(k) + 1 - NB))
                    V.tensor_scalar(oh_src[:, k % RING_S, :], srch[:, i, :], mid_id[:, k:k + 1], None, ALU.is_equal).then_inc(s_ohs, 1)

            def turned(it, i, first):
                if not first:
                    ve.wait_ge(s_pre[i], it)
                ve.wait_ge(s_rows[i], (16 * PT[i]) * (it + 1))
                V.transpose(hsT[i][:, :], rows[i][:, 0:PT[i], :].rearrange("p t c -> p (t c)"))
                stage(it + 1, i).then_inc(s_idx[i], 1)

            def scan(it, i, first):
                w = 32 * HALF[i]
                if i == 1:
                    ve.wait_ge(s_run[0], it + 1)
                elif not first:
                    ve.wait_ge(s_run[1], it)
                ve.wait_ge(s_lim[i], it + 1)
                ve.wait_ge(s_v[i], it + 1)
                V.tensor_tensor_scan(run[i][:, :], lim[i], ps[i][:, 3, 0:w],
                                     run[1 - i][:, 32 * HALF[1 - i] - 1:32 * HALF[1 - i]], ALU.min, ALU.max).then_inc(s_run[i], 1)
                if not first:
                    ve.wait_ge(s_vout[i], 16 * it)
                ve.wait_ge(s_run[i], it + 1)
                V.transpose(vrow[i][:, :], run[i][:, :]).then_inc(s_vrow[i], 1)

            prepare(0, 0, True)
            turned(0, 0, True)
            prepare(0, 1, True)
            turned(0, 1, True)
            scan(0, 0, True)
            prepare(1, 0, False)
            turned(1, 0, False)
            scan(0, 1, True)
            prepare(1, 1, False)
            with ve.Fori(1, STEPS - 1) as it:
                turned(it, 1, False)
                scan(it, 0, False)
                prepare(it + 1, 0, False)
                turned(it + 1, 0, False)
                scan(it, 1, False)
                prepare(it + 1, 1, False)
            turned(STEPS - 1, 1, False)
            scan(STEPS - 1, 0, False)
            scan(STEPS - 1, 1, False)

            ve.wait_ge(s_edgev, 48)
            for q in range(3):
                step(V.tensor_tensor(tmp[:, q, :, :], bc(edge_p[:, q, :]), chan(edge_v[:, q, :]), ALU.add))
            for q in range(1, 3):
                step(V.tensor_tensor(tmp[:, 0, :, :], tmp[:, 0, :, :], tmp[:, q, :, :], ALU.max))
            ve.wait_ge(s_cand, 16 * NB)
            step(V.tensor_tensor(cand[:, :, :], cand[:, :, :], tmp[:, 0, :, :], ALU.max))
            finish()

            def columns(table, q):
                return table.rearrange("c (k q r) -> c k q r", q=4, r=32)[:, :, q, :]

            def quad(q):
                return hT[32 * q:32 * q + 32, :].rearrange("c (k r) -> c k r", r=32)

            def rows_to_table(rows_, table):
                step(V.transpose(hT[:, :], rows_.rearrange("p k c -> p (k c)")))
                for q in range(4):
                    step(V.tensor_copy(columns(table, q), quad(q)))

            def table_to_quads(table):
                for q in range(4):
                    last = V.tensor_copy(quad(q), columns(table, q))
                return last

            def edges(body):
                ve.sem_inc(s_gturn, 1)
                with ve.Fori(0, GE) as j:
                    body(j, ve.value_load(g_src[0:1, ds(j, 1)], min_val=0, max_val=N - 1),
                         ve.value_load(g_dst[0:1, ds(j, 1)], min_val=0, max_val=N - 1))

            with if_general(ve):
                ve.sem_inc(s_gused, 1)
                step(norm_relu(x[:, :, :], 3))
                step(V.tensor_scalar(h[:, :, :], h[:, :, :], MSG_EPS, None, ALU.add))
                rows_to_table(h[:, :, :], feat)
                V.memset(g_hid[:, :], 0.0)
                V.memset(total, 0.0)
                V.memset(wsum, 0.0)
                step(V.memset(peak, -BIG))
                with ve.Fori(0, GCHUNKS) as c:
                    ve.wait_ge(s_gidx3[0], 32 * c + 32)

                    def largest(j, s, d):
                        V.scalar_tensor_tensor(peak[:, ds(s, 1)], feat[:, ds(d, 1)], betac[0:D, 0:1], peak[:, ds(s, 1)], ALU.mult, ALU.max)
                        ve.drain()

                    edges(largest)
                    ve.sem_inc(s_gused, 1)
                with ve.Fori(0, GCHUNKS) as c:
                    ve.wait_ge(s_gidx3[1], 32 * c + 32)

                    def shifted(j, s, d):
                        V.scalar_tensor_tensor(g_diff[:, ds(j, 1)], feat[:, ds(d, 1)], betac[0:D, 0:1], peak[:, ds(s, 1)], ALU.mult, ALU.subtract)

                    def summed(j, s, d):
                        V.tensor_tensor(total[:, ds(s, 1)], total[:, ds(s, 1)], g_exp[:, ds(j, 1)], ALU.add)
                        V.scalar_tensor_tensor(wsum[:, ds(s, 1)], feat[:, ds(d, 1)], g_exp[:, ds(j, 1)], wsum[:, ds(s, 1)], ALU.mult, ALU.add)
                        ve.drain()

                    edges(shifted)
                    ve.drain()
                    ve.sem_inc(s_gdiff, 1)
                    ve.wait_ge(s_gexp, c + 1)
                    edges(summed)
                    ve.sem_inc(s_gused, 1)
                step(V.tensor_scalar(total, total, 1e-38, None, ALU.max))
                step(V.reciprocal(total, total))
                step(V.tensor_tensor(wsum, wsum, total, ALU.mult))
                table_to_quads(wsum).then_inc(s_h0T, 1)
                after_mlp(1)
                ve.wait_ge(s_h1, 2)
                rows_to_table(h[:, :, :], feat)
                step(V.memset(peak, -BIG))
                with ve.Fori(0, GCHUNKS) as c:
                    ve.wait_ge(s_gidx3[2], 32 * c + 32)

                    def fill(j, s, d):
                        V.tensor_copy(g_in[0:D, ds(j, 1)], feat[:, ds(s, 1)])
                        V.tensor_copy(g_in[D:2 * D, ds(j, 1)], feat[:, ds(d, 1)])

                    def maximum(j, s, d):
                        V.tensor_tensor(peak[:, ds(d, 1)], peak[:, ds(d, 1)], ps[0][0:D, 2, ds(j, 1)], ALU.max)
                        ve.drain()

                    edges(fill)
                    ve.wait_ge(s_geaT, c + 1)
                    V.tensor_copy(g_in[2 * D:3 * D, :], ps[0][0:D, 0, 0:GE])
                    ve.drain()
                    ve.sem_inc(s_gin, 1)
                    ve.wait_ge(s_gv, c + 1)
                    edges(maximum)
                    ve.sem_inc(s_gused, 1)
                step(table_to_quads(peak))
                step(V.transpose(cand[:, :, :].rearrange("p k c -> p (k c)"), hT[:, :]))
                finish()


def kernel(**inputs):
    import numpy as np
    import concourse.bacc as bacc
    from concourse import mybir as mb
    from concourse.bass_utils import run_bass_kernel_spmd as launch

    a = {k: np.ascontiguousarray(v) for k, v in inputs.items()}
    x, src, dst, ea = a["x"], a["src"], a["dst"], a["edge_attr_32"]
    i32 = dst.dtype
    src_p = np.concatenate([src, np.zeros(EPAD - E, i32)])
    dst_p = np.concatenate([dst, np.full(EPAD - E + 1, NO_DST, i32)])
    ea_p = np.concatenate([ea, np.zeros((EPAD - E, D), ea.dtype)])
    x_p = np.concatenate([x, np.zeros((NP - N, D), x.dtype)])
    starts0 = [GT * P * k for k in range(GROUPS)]
    ends0 = [min(s + GT * P, E) - 1 for s in starts0]
    starts1 = [[Q * q + 32 * (STEP * (n // 2) + HALF[0] * (n % 2)) for n in range(HALVES)] for q in range(4)]
    ends1 = [[min(s + 32 * HALF[n % 2], E) - 1 for n, s in enumerate(row)] for row in starts1]
    nexts1 = [[s + 32 * HALF[n % 2] for n, s in enumerate(row)] for row in starts1]
    base0 = dst_p[starts0]
    arrays = {
        "xb": x_p.reshape(NB, P, D).transpose(1, 0, 2).reshape(P, NB * D),
        "src0": np.concatenate([src_p, np.zeros(P * ATILES - EPAD, i32)]).reshape(ATILES, P).T,
        "dst0": np.concatenate([dst_p[:-1], np.full(P * ATILES - EPAD, NO_DST, i32)]).reshape(ATILES, P).T,
        "srcs": src_p.reshape(4, Q),
        "srcq": src_p.reshape(4, TILES, 32).transpose(0, 2, 1).reshape(P, TILES),
        "dstq": np.stack([np.concatenate([np.full(1, -1, i32) if q == 0 else dst_p[Q * q - 1:Q * q], dst_p[Q * q:Q * q + Q]]) for q in range(4)]),
        "eat": ea_p.reshape(4, Q, D).transpose(0, 2, 1).reshape(P, Q),
        "base0": base0, "base0c": np.concatenate([base0, np.full(CHUNK * CHUNKS - GROUPS, NO_DST, i32)]).reshape(CHUNKS, CHUNK).T,
        "last0": dst_p[ends0], "base1": dst_p[starts1], "last1": dst_p[ends1], "next1": dst_p[nexts1],
        "slast": dst_p[[Q * q + Q - 1 for q in range(3)]],
        "dstp": dst_p[:-1], "src": src, "dst": dst, "ea": ea,
        "beta": a["L0_gnn_beta"], "w01": a["L0_gnn_W1"], "b01": a["L0_gnn_b1"], "w02": a["L0_gnn_W2"], "b02": a["L0_gnn_b2"],
        "w11": a["L1_gnn_W1"], "b11": a["L1_gnn_b1"], "w12": a["L1_gnn_W2"], "b12": a["L1_gnn_b2"],
    }
    nc = bacc.Bacc("TRN2", target_bir_lowering=False, num_devices=1)
    feeds, aps = {}, {}
    for name, v in arrays.items():
        v = np.ascontiguousarray(v)
        feeds[f"in_{name}"] = v
        aps[name] = nc.dram_tensor(f"in_{name}", v.shape, mb.dt.from_np(v.dtype), kind="ExternalInput").ap()
    out = nc.dram_tensor("out_0", (P, NB * D), mb.dt.float32, kind="ExternalOutput").ap()
    build(nc, **aps, out=out)
    got = launch(nc, [feeds], core_ids=[0]).results[0]["out_0"]
    return got.reshape(P, NB, D).transpose(1, 0, 2).reshape(NP, D)[:N]
```

```python
from contextlib import ExitStack

import concourse.bass as bass
from concourse import mybir

P = 128
N, D, H, E = 3125, 32, 64, 103125
NB = (N + P - 1) // P
NP = NB * P
NB4 = (NB + 3) // 4
MSG_EPS, LN_EPS = 1e-7, 1e-5

HI = 8
LO = (N + HI - 1) // HI
TILES = (E + P - 1) // P
GT = 3
W0 = P // HI
GROW0 = 5
LATE = 1
GROUPS = (TILES + GT - 1) // GT
ATILES = GT * GROUPS
CHUNK = P // W0
CHUNKS = (GROUPS + CHUNK - 1) // CHUNK
CT = GT * CHUNK
TAIL_GROUPS = GROUPS - CHUNK * (CHUNKS - 1)
PAIRS = CHUNKS // 2 - 1
Q = TILES * 32
HALF = (16, 15)
STEP = sum(HALF)
STEPS = TILES // STEP
W1 = 32
PC = (5, 4)
PT = (HALF[0] - PC[0], HALF[1] - PC[1])
PW = (32 * PC[0], 32 * PC[1])
GATHER_BANKS = (((0, 0, 2 * PW[0]), (3, 2 * PW[0], 4 * PW[0])), ((0, 0, 4 * PW[1]),))
MID = N // 2
HALVES = 2 * STEPS
EPAD = 4 * Q
NO_DST = 8000
BIG = 3.0e38
RANGE = 60.0
NOT_FOUND = 1 << 20
ROUND = 1.5 * 2 ** 23
COUNT_MAX = 256
MLP_BLOCKS = ((0, 13), (13, NB))
CAND = ((0, 16), (16, 23), (23, NB))
GE = 125
GCHUNKS = E // GE
assert E % GE == 0
RING_S = 7
EARLY = 9
RING = 8
ACT_TILES = (14,)
RING_W = 4
SIGNS_FROM = 3
SIGNS_AT = 2
SIGN_PAIRS = STEPS // 2
assert TILES % STEP == 0 and STEPS % 2 == 0 and CHUNKS % 2 == 0 and 2 * SIGN_PAIRS == STEPS and SIGNS_FROM + SIGN_PAIRS <= PAIRS


def build(nc, xb, src0, dst0, srcq, srcs, dstq, eat, base0, base0c, last0, base1, last1, next1, slast, dstp, src, dst, ea,
          beta, w01, b01, w02, b02, w11, b11, w12, b12, out):
    f32, f16, bf16, i32 = mybir.dt.float32, mybir.dt.float16, mybir.dt.bfloat16, mybir.dt.int32
    ALU, ACT, AX = mybir.AluOpType, mybir.ActivationFunctionType, mybir.AxisListType.X
    ds = bass.ds
    ctx = ExitStack()
    with ctx:
        def sb(name, shape, dt):
            return ctx.enter_context(nc.sbuf_tensor(name, shape, dt))

        def sem(name):
            return ctx.enter_context(nc.semaphore(name))

        g_dram = nc.dram_tensor("g_dram", (NP + 1, 3 * H), bf16).ap()
        b_dram = nc.dram_tensor("b_dram", (512 * NB4, 3 * H), bf16).ap()
        h_dram = nc.dram_tensor("h_dram", (NP, D), f32).ap()
        v_dram = nc.dram_tensor("v_dram", (P * TILES, D), f32).ap()
        end_dram = nc.dram_tensor("end_dram", (NP, 1), i32).ap()

        ident = sb("ident", [P, P], f32)
        diff_i = sb("diff_i", [P, P], f32)
        lo_iota = sb("lo_iota", [P, LO + 1], f16)
        win_iota = sb("win_iota", [P, P, GT], f16)
        part = sb("part", [P, 1], i32)
        part16 = sb("part16", [P, 1], i32)
        part32 = sb("part32", [P, 1], i32)
        part32f = sb("part32f", [P, 1], f32)
        part16f = sb("part16f", [P, 1], f32)
        node_id = sb("node_id", [P, NB], f32)
        ones = sb("ones", [P, P], f32)
        zero_b = sb("zero_b", [P, 512], bf16)
        w01d = sb("w01d", [P, 2, P], f32)
        w02d = sb("w02d", [P, 2, P], f32)
        w1ind = sb("w1ind", [P, 2, P], f32)
        w1dd = sb("w1dd", [P, 2, P], f32)
        w12d = sb("w12d", [P, 2, P], f32)
        b01c = sb("b01c", [P, 1], f32)
        b11c = sb("b11c", [P, 1], f32)
        b02c = sb("b02c", [P, 1], f32)
        b12r = sb("b12r", [P, D], f32)
        betac = sb("betac", [P, 1], f32)
        x = sb("x", [P, NB, D], f32)
        xc = sb("xc", [P, NB, D], f32)
        sq = sb("sq", [P, NB, D], f32)
        stat = sb("stat", [P, 4, NB], f32)
        h = sb("h", [P, NB, D], f32)
        logit = sb("logit", [P, NB, D], f32)
        g = sb("g", [P, NB, 2, D], f32)
        gs = sb("gs", [P, NB, 3, H], bf16)
        ext = sb("ext", [P, 2, D], f32)
        top = sb("top", [H, 1], f32)
        topd = sb("topd", [H, H], f32)
        topb = sb("topb", [P, 2, D], f32)
        hT = sb("hT", [P, NB * D], f32)
        mT = sb("mT", [P, 2, NB * D], f32)
        x1 = sb("x1", [P, NB, D], f32)
        scan_bufs = sb("scan_bufs", [P, 8 * 512], f32)
        src_i, dst_i = (scan_bufs[:, ATILES * n:ATILES * n + ATILES].bitcast(i32) for n in range(2))
        keys = sb("keys", [P, 5, ATILES], f32)
        srcf, hi, key_win, key_lo = keys[:, 0, :], keys[:, 1, :], keys[:, 3, :], keys[:, 4, :]
        key_win16 = srcf.bitcast(f16)[:, 0:ATILES]
        base0_i = sb("base0_i", [P, GROUPS], i32)
        gidx_b = sb("gidx_b", [P, CHUNKS], i32)
        gidx = sb("gidx", [P, CHUNKS], i32)
        grow = sb("grow", [P, CHUNKS, 3 * H], bf16)
        onehot = sb("onehot", [P, RING_W * P * GT + RING * (LO + 1)], f16)
        oh_win = onehot[:, 0:RING_W * P * GT].rearrange("p (r c t) -> p r c t", r=RING_W, t=GT)
        oh_lo = onehot[:, RING_W * P * GT:].rearrange("p (r c) -> p r c", r=RING)
        oh_act = sb("oh_act", [P, len(ACT_TILES), LO + 1], f16)
        lo_dist = sb("lo_dist", [P, len(ACT_TILES), LO + 1], bf16)
        cg = sb("cg", [P, CHUNK, LO + 1], bf16)
        cnt = sb("cnt", [P, 2, NP], bf16)
        base1_i = sb("base1_i", [P, HALVES], i32)
        next1_i = sb("next1_i", [P, HALVES], i32)
        win_id = sb("win_id", [P, HALVES], f32)
        bias_le = sb("bias_le", [P, HALVES], f32)
        bias_lt = sb("bias_lt", [P, HALVES], f32)
        ends_in = sb("ends_in", [P, HALVES], f32)
        pos_off = sb("pos_off", [P, HALVES], f32)
        dcount = sb("dcount", [P, 2, 512], i32)
        ssum = sb("ssum", [P, 2, 2, 2], f32)
        pc = sb("pc", [P, 8, 2], f32)
        pos_i = sb("pos_i", [P, 2], i32)
        pidx_i = sb("pidx_i", [P, 2], i32)
        end_i = sb("end_i", [P, NB], i32)
        end_t = sb("end_t", [P, 3, NB], i32)
        end_f = sb("end_f", [P, 4, NB], f32)
        end_idx = sb("end_idx", [P, NB], i32)
        srcq_i = sb("srcq_i", [P, TILES + STEP], i32)
        base1r = sb("base1r", [1, 4 * HALVES], i32)
        base1c = sb("base1c", [1, 4 * HALVES], i32)
        idx_st = [sb(f"idx_st{i}", [P, PT[i]], i32) for i in range(2)]
        rows = [sb(f"rows{i}", [P, HALF[i], D], f32) for i in range(2)]
        sgn = [rows[i][:, :, :].rearrange("p t c -> p (t c)").bitcast(bf16) for i in range(2)]
        layer_in = [sb(f"layer_in{i}", [P, 2, 32 * HALF[i]], f32) for i in range(2)]
        dstb = [sb(f"dstb{i}", [P, 32 * HALF[i] + 1], i32) for i in range(2)]
        same, lim = ([scan_bufs[:, 1024 * n + 512 * i:1024 * n + 512 * i + 32 * HALF[i]] for i in range(2)] for n in range(2))
        ohd = [scan_bufs[:, 2048 + 256 * i:2048 + 256 * i + 16 * HALF[i]].bitcast(bf16) for i in range(2)]
        h3 = gs[:, :, :, :].rearrange("p k s c -> p (k s c)")[:, 0:NB * 3 * D].rearrange("p (k s c) -> p k s c", s=3, c=D)
        wins = gs[:, :, :, :].rearrange("p k s c -> p (k s c)")[:, NB * 3 * D:NB * 3 * D + 12 * P].rearrange("p (i s t c) -> p i s t c", i=2, s=2, t=3)
        oh_src = onehot[:, 0:RING_S * 4 * PW[0]].bitcast(bf16).rearrange("p (r c) -> p r c", r=RING_S)
        srcb = [mT[:, i, 0:4 * PW[i]].bitcast(i32) for i in range(2)]
        srch = [logit[:, :, :].rearrange("p k c -> p (k c)").bitcast(f16)[:, 4 * PW[0] * i:4 * PW[0] * i + 4 * PW[i]] for i in range(2)]
        hg3 = [g[:, :, :, :].rearrange("p k a c -> p (k a c)")[0:3 * D, 4 * PW[0] * i:4 * PW[0] * i + 4 * PW[i]] for i in range(2)]
        bf = keys[:, :, :].rearrange("p a b -> p (a b)")[:, 0:NB4 * 4 * H]
        b3 = cnt[:, :, :].rearrange("p a b -> p (a b)")[:, 0:NB4 * 4 * 3 * H].rearrange("p (m s c) -> p m s c", s=3, c=H)
        w1s3 = sb("w1s3", [3 * D, H], f32)
        mid_id = sb("mid_id", [P, NB], f32)
        hid = [sb(f"hid{i}", [P, 2, 32 * HALF[i]], f32) for i in range(2)]
        run = [sb(f"run{i}", [P, 32 * HALF[i]], f32) for i in range(2)]
        vrow = [sb(f"vrow{i}", [P, 32 * HALF[i]], f32) for i in range(2)]
        cand = sb("cand", [P, NB, D], f32)
        edge_v = sb("edge_v", [P, 3, D], f32)
        edge_n = sb("edge_n", [P, 3], i32)
        edge_nf = sb("edge_nf", [P, 3], f32)
        edge_p = sb("edge_p", [P, 3, NB], f32)
        tmp = sb("tmp", [P, 3, NB, D], f32)
        res = sb("res", [P, NB, D], f32)
        last0_i = sb("last0_i", [1, GROUPS], i32)
        base0_r = sb("base0_r", [1, GROUPS], i32)
        last1_i = sb("last1_i", [1, 4 * HALVES], i32)
        n_order = (E - 1) // 127
        order_i = tmp[:, :, :, :].rearrange("p a k c -> p (a k c)").bitcast(i32)[0:127, 0:2 * n_order].rearrange("p (a n) -> p a n", a=2)
        n_far = (EPAD - COUNT_MAX) // P
        assert EPAD - E < COUNT_MAX and (EPAD - COUNT_MAX) % P == 0
        far_i = scan_bufs[:, 2 * ATILES:2 * ATILES + 2 * n_far].bitcast(i32).rearrange("p (a n) -> p a n", a=2)
        far_f = srcf[:, 0:n_far]
        order_f = keys[:, :, :].rearrange("p a b -> p (a b)")[0:127, 2 * ATILES:]
        wide0 = sb("wide0", [1, GROUPS], f32)
        wide1 = sb("wide1", [1, 4 * HALVES], f32)
        wide2 = sb("wide2", [1, D], f32)
        broken = sb("broken", [P, 5], f32)
        flag_f = sb("flag_f", [1, 1], f32)
        flag = sb("flag", [1, 1], i32)
        feat = grow[:, :, :].rearrange("p a b -> p (a b)").bitcast(f32)[0:D, 0:NP]
        peak = cnt[:, :, :].rearrange("p a b -> p (a b)").bitcast(f32)[0:D, 0:NP]
        total = keys[:, :, :].rearrange("p a b -> p (a b)")[0:D, 0:NP]
        wsum = scan_bufs[0:D, 0:NP]
        w11f = sb("w11f", [3 * D, H], f32)
        g_src = sb("g_src", [1, GE], i32)
        g_dst = sb("g_dst", [1, GE], i32)
        g_ea = sb("g_ea", [GE, D], f32)
        g_diff = sb("g_diff", [D, GE], f32)
        g_exp = sb("g_exp", [D, GE], f32)
        g_in = sb("g_in", [3 * D, GE], f32)
        g_hid = sb("g_hid", [P, GE], f32)

        ps = [ctx.enter_context(nc.psum_tensor(f"ps{i}", [P, 4, 512], f32)) for i in range(2)]
        ps_cnt = ps[0]
        ps_broken = ps[0][0:1, 3, 500:505]
        ps_sum = ps[1][:, :, :].rearrange("p a b -> p (a b)")[:, 0:NB * H].rearrange("p (k c) -> p k c", c=H)

        s_const = sem("s_const")
        s_zero = sem("s_zero")
        s_x = sem("s_x")
        s_edges = sem("s_edges")
        s_win = sem("s_win")
        s_weights0 = sem("s_weights0")
        s_weights1 = sem("s_weights1")
        s_dve = sem("s_dve")
        s_pool = sem("s_pool")
        s_sqrt_in = sem("s_sqrt_in")
        s_sqrt = sem("s_sqrt")
        s_ext = sem("s_ext")
        s_extT = sem("s_extT")
        s_topd = sem("s_topd")
        s_topb = sem("s_topb")
        s_shift = sem("s_shift")
        s_exp = sem("s_exp")
        s_gpart_in = sem("s_gpart_in")
        s_gpart = sem("s_gpart")
        s_gtab = sem("s_gtab")
        s_gidx = sem("s_gidx")
        s_grow0 = sem("s_grow0")
        s_grow = sem("s_grow")
        s_onehot = sem("s_onehot")
        s_onehot_act = sem("s_onehot_act")
        s_lo_dist = sem("s_lo_dist")
        s_tile = sem("s_tile")
        s_evac = sem("s_evac")
        s_shuf = [sem(f"s_shuf{i}") for i in range(CHUNK)]
        s_chunk = sem("s_chunk")
        s_dcl = [sem(f"s_dcl{i}") for i in range(2)]
        s_sgn = [sem(f"s_sgn{i}") for i in range(2)]
        s_used = sem("s_used")
        s_endp = sem("s_endp")
        s_turn = sem("s_turn")
        s_winprep = sem("s_winprep")
        s_endinit = sem("s_endinit")
        s_scat = sem("s_scat")
        s_endld = sem("s_endld")
        s_endidx = sem("s_endidx")
        s_h0T = sem("s_h0T")
        s_m1 = sem("s_m1")
        s_m1r = sem("s_m1r")
        s_m2 = sem("s_m2")
        s_h1 = sem("s_h1")
        s_htab = sem("s_htab")
        s_idx = [sem(f"s_idx{i}") for i in range(2)]
        s_rows = [sem(f"s_rows{i}") for i in range(2)]
        s_ea = [sem(f"s_ea{i}") for i in range(2)]
        s_dst = [sem(f"s_dst{i}") for i in range(2)]
        s_wrow = [sem(f"s_wrow{i}") for i in range(2)]
        s_srcq = sem("s_srcq")
        s_ohd = [sem(f"s_ohd{i}") for i in range(2)]
        s_same = [sem(f"s_same{i}") for i in range(2)]
        s_lim = [sem(f"s_lim{i}") for i in range(2)]
        s_srcb = [sem(f"s_srcb{i}") for i in range(2)]
        s_srch = [sem(f"s_srch{i}") for i in range(2)]
        s_ohs = sem("s_ohs")
        s_gat = sem("s_gat")
        s_hg3 = [sem(f"s_hg3_{i}") for i in range(2)]
        s_hT = sem("s_hT")
        s_bmm = sem("s_bmm")
        s_b3 = sem("s_b3")
        s_btab = sem("s_btab")
        s_h3 = sem("s_h3")
        s_winz = sem("s_winz")
        s_pre = [sem(f"s_pre{i}") for i in range(2)]
        s_hid = [sem(f"s_hid{i}") for i in range(2)]
        s_v = [sem(f"s_v{i}") for i in range(2)]
        s_run = [sem(f"s_run{i}") for i in range(2)]
        s_vrow = [sem(f"s_vrow{i}") for i in range(2)]
        s_vout = [sem(f"s_vout{i}") for i in range(2)]
        s_base1c = sem("s_base1c")
        s_candf = sem("s_candf")
        s_cand = [sem(f"s_cand{n}") for n in range(len(CAND))]
        s_edgev = sem("s_edgev")
        s_res = sem("s_res")
        s_out = sem("s_out")
        s_bounds = sem("s_bounds")
        s_broken = sem("s_broken")
        s_count = sem("s_count")
        s_flag = sem("s_flag")
        s_gidx3 = [sem(f"s_gidx3_{i}") for i in range(3)]
        s_gused = sem("s_gused")
        s_gea = sem("s_gea")
        s_gdiff = sem("s_gdiff")
        s_gexp = sem("s_gexp")
        s_geaT = sem("s_geaT")
        s_gin = sem("s_gin")
        s_gpre = sem("s_gpre")
        s_ghid = sem("s_ghid")
        s_gv = sem("s_gv")
        s_gturn = sem("s_gturn")

        block = ctx.enter_context(nc.Block())

        def mc(f):
            return slice(D * MLP_BLOCKS[f][0], D * MLP_BLOCKS[f][1])

        def mw(f):
            return D * (MLP_BLOCKS[f][1] - MLP_BLOCKS[f][0])

        def windowed(rows_of_streams, w):
            return rows_of_streams.rearrange("q (o c) -> q o c", o=1).to_broadcast([4, W1, w])

        def if_general(eng):
            eng.wait_ge(s_flag, 1)
            eng.wait_ge(s_out, 16)
            return eng.If(eng.value_load(flag[0:1, 0:1], min_val=0, max_val=4 * E) > 0)

        @block.sync
        def _(sp):
            sp.dma_start(x[:, :, :].rearrange("p k c -> p (k c)"), xb).then_inc(s_x, 16)
            sp.dma_start(betac[:, :], beta.rearrange("(o a) -> o a", o=1).to_broadcast([P, 1])).then_inc(s_x, 16)
            sp.dma_start(src_i, src0).then_inc(s_edges, 16)
            sp.dma_start(dst_i, dst0).then_inc(s_edges, 16)
            sp.dma_start(base0_i[:, :], base0.rearrange("(o a) -> o a", o=1).to_broadcast([P, GROUPS])).then_inc(s_edges, 16)
            for r in range(CHUNK):
                sp.dma_start(gidx_b[W0 * r:W0 * r + W0, :], base0c[r:r + 1, :].to_broadcast([W0, CHUNKS])).then_inc(s_win, 16)
            for q in range(4):
                sp.dma_start(base1_i[32 * q:32 * q + 32, :], base1[q:q + 1, :].to_broadcast([32, HALVES])).then_inc(s_win, 16)
                sp.dma_start(next1_i[32 * q:32 * q + 32, :], next1[q:q + 1, :].to_broadcast([32, HALVES])).then_inc(s_win, 16)
            sp.dma_start(base1r[:, :], base1.rearrange("(o q) n -> o (q n)", o=1)).then_inc(s_win, 16)
            sp.dma_start(srcq_i[:, 0:TILES], srcq).then_inc(s_srcq, 16)
            sp.dma_start(last0_i[:, :], last0.rearrange("(o a) -> o a", o=1)).then_inc(s_bounds, 16)
            sp.dma_start(base0_r[:, :], base0.rearrange("(o a) -> o a", o=1)).then_inc(s_bounds, 16)
            sp.dma_start(last1_i[:, :], last1.rearrange("(o q) n -> o (q n)", o=1)).then_inc(s_bounds, 16)
            for i in range(2):
                sp.dma_start(order_i[:, i, :], dst[i:i + E - 1].rearrange("(p n) -> p n", p=127)).then_inc(s_bounds, 16)
            for i in range(2):
                sp.dma_start(far_i[:, i, :], dstp[COUNT_MAX * i:COUNT_MAX * i + P * n_far].rearrange("(p n) -> p n", p=P)).then_inc(s_bounds, 16)
            sp.wait_ge(s_zero, 2)
            sp.dma_start(end_dram.rearrange("(p k) o -> p (k o)", p=P), end_i[:, :]).then_inc(s_endinit, 16)
            sp.dma_start(edge_n[:, :], slast.rearrange("(o a) -> o a", o=1).to_broadcast([P, 3])).then_inc(s_srcq, 16)
            sp.wait_ge(s_zero, 1)
            for q in range(4):
                s, c = q // 2, 64 * (q % 2)
                sp.dma_start(w01d[32 * q:32 * q + 32, s, c:c + H], w01).then_inc(s_weights0, 16)
                sp.dma_start(w02d[c:c + H, s, 32 * q:32 * q + 32], w02).then_inc(s_weights0, 16)
                sp.dma_start(b02c[32 * q:32 * q + 32, :], b02.rearrange("(a o) -> a o", o=1)).then_inc(s_weights0, 16)
            for i in range(2):
                sp.dma_start(b01c[H * i:H * i + H, :], b01.rearrange("(a o) -> a o", o=1)).then_inc(s_weights0, 16)
            sp.wait_ge(s_gpart, 3)
            sp.dma_start(g_dram[NP:NP + 1, :], zero_b[0:1, 0:3 * H]).then_inc(s_gtab, 16)
            sp.dma_start(g_dram[0:NP, :].rearrange("(k p) c -> p k c", p=P), gs[:, :, :, :].rearrange("p k s c -> p k (s c)")).then_inc(s_gtab, 16)

            def shuffle(c0, k, groups, first):
                for j in range(groups):
                    grp = CHUNK * (c0 + k) + j
                    if j == 0 and not first:
                        sp.wait_ge(s_chunk, c0 + k - 1)
                    sp.wait_ge(s_evac, grp + 1)
                    sp.dma_start(cnt[W0 * j:W0 * j + W0, k % 2, 0:HI * LO].rearrange("n (a b) -> n a b", a=HI),
                                 cg[:, j, 0:LO]).then_inc(s_shuf[j], 16)

            shuffle(0, 0, CHUNK, True)
            shuffle(0, 1, CHUNK, True)
            with sp.Fori(1, PAIRS) as it:
                shuffle(2 * it, 0, CHUNK, False)
                shuffle(2 * it, 1, CHUNK, False)
            shuffle(2 * PAIRS, 0, CHUNK, False)
            shuffle(2 * PAIRS, 1, TAIL_GROUPS, False)

            sp.wait_ge(s_scat, 16 * HALVES)
            sp.dma_start(end_i[:, :], end_dram.rearrange("(k p) o -> p (k o)", p=P), allow_slow_non_contiguous=True).then_inc(s_endld, 16)
            for q in range(4):
                s, c = q // 2, 64 * (q % 2)
                sp.dma_start(w1dd[32 * q:32 * q + 32, s, c:c + H], w11[D:2 * D, :]).then_inc(s_weights1, 16)
                for top_row, wt in ((64 * s, w11[0:D, :]), (64 - 64 * s, w11[2 * D:3 * D, :])):
                    row = top_row + 32 * (q % 2)
                    sp.dma_start(w1ind[row:row + 32, s, c:c + H], wt).then_inc(s_weights1, 16)
                sp.dma_start(w12d[c:c + H, s, 32 * q:32 * q + 32], w12).then_inc(s_weights1, 16)
            for i in range(2):
                sp.dma_start(b11c[H * i:H * i + H, :], b11.rearrange("(a o) -> a o", o=1)).then_inc(s_weights1, 16)
            sp.dma_start(b12r[:, :], b12.rearrange("(o a) -> o a", o=1).to_broadcast([P, D])).then_inc(s_weights1, 16)
            sp.dma_start(w11f[:, :], w11).then_inc(s_weights1, 16)
            for t in range(3):
                sp.dma_start(w1s3[D * t:D * t + D, :], w11[0:D, :]).then_inc(s_weights1, 16)
            sp.wait_ge(s_h1, 1)
            sp.dma_start(h_dram.rearrange("(k p) c -> p k c", p=P), h[:, :, :]).then_inc(s_htab, 16)
            def load_edges_of(it, i, first):
                w = 32 * HALF[i]
                c0 = it * (32 * STEP) + 32 * HALF[0] * i
                if not first:
                    sp.wait_ge(s_lim[i], it)
                sp.dma_start(dstb[i][:, :], windowed(dstq[:, ds(c0, w + 1)], w + 1)).then_inc(s_dst[i], 16)
                if not first:
                    sp.wait_ge(s_srch[i], it)
                sp.dma_start(srcb[i].rearrange("p (q c) -> p q c", q=4),
                             srcs[:, ds(c0 + 32 * PT[i], PW[i])].rearrange("(o q) c -> o q c", o=1).to_broadcast([P, 4, PW[i]])).then_inc(s_srcb[i], 16)
                if not first:
                    sp.wait_ge(s_pre[i], it)
                for s in range(2):
                    sp.dma_start(layer_in[i][64 - 64 * s:128 - 64 * s, s, :], eat[64 * s:64 * s + 64, ds(c0, w)]).then_inc(s_ea[i], 16)

            def load_windows(it, i):
                for q in range(4):
                    first_node = sp.value_load(base1c[0:1, ds(2 * it + i + q * HALVES, 1)], min_val=0, max_val=N - W1)
                    sp.dma_start(wins[32 * q:32 * q + 32, i, q // 2, :, 64 * (q % 2):64 * (q % 2) + 64],
                                 b_dram[ds(first_node, W1), :].rearrange("n (s c) -> n s c", s=3)).then_inc(s_wrow[i], 16)

            def load_half(it, i):
                load_edges_of(it, i, False)
                load_windows(it, i)

            def store_half(it, i):
                w = HALF[i]
                sp.wait_ge(s_vrow[i], it + 1)
                sp.dma_start(v_dram.rearrange("(p t) c -> p t c", p=P)[:, ds(it * STEP + HALF[0] * i, w), :],
                             vrow[i][:, :].rearrange("p (t c) -> p t c", c=D)).then_inc(s_vout[i], 16)

            load_edges_of(0, 0, True)
            load_edges_of(0, 1, True)
            sp.wait_ge(s_b3, 1)
            b3v = b_dram.rearrange("(m k q r) c -> k r m q c", k=4, q=4, r=32)
            for k in range(4):
                for q in range(4):
                    sp.dma_start(b3v[k][:, :, q, :], b3[32 * k:32 * k + 32, :, :, :].rearrange("r (m q) s c -> r m q (s c)", q=4)[:, :, q, :]).then_inc(s_btab, 16)
            sp.wait_ge(s_base1c, 1)
            sp.wait_ge(s_winz, 1)

            sp.wait_ge(s_btab, 256)
            load_windows(0, 0)
            load_windows(0, 1)
            with sp.Fori(1, STEPS) as it:
                load_half(it, 0)
                store_half(it - 1, 0)
                load_half(it, 1)
                store_half(it - 1, 1)
            store_half(STEPS - 1, 0)
            store_half(STEPS - 1, 1)
            sp.wait_ge(s_vout[0], 16 * STEPS)
            sp.wait_ge(s_vout[1], 16 * STEPS)
            for q in range(3):
                sp.dma_start(edge_v[:, q, :], v_dram[(32 * q + 32) * TILES - 1:(32 * q + 32) * TILES, :].to_broadcast([P, D])).then_inc(s_edgev, 16)
            sp.wait_ge(s_res, len(CAND))
            sp.dma_start(out, res[:, :, :].rearrange("p k c -> p (k c)")).then_inc(s_out, 16)
            sp.wait_ge(s_out, 16)

            def load_edges(c, at, features):
                sp.wait_ge(s_gused, c + (at + 1))
                sp.dma_start(g_src[:, :], src[ds(c * GE, GE)].rearrange("(o a) -> o a", o=1)).then_inc(s_gidx3[at // GCHUNKS], 16)
                sp.dma_start(g_dst[:, :], dst[ds(c * GE, GE)].rearrange("(o a) -> o a", o=1)).then_inc(s_gidx3[at // GCHUNKS], 16)
                if features:
                    sp.dma_start(g_ea[:, :], ea[ds(c * GE, GE), :]).then_inc(s_gea, 16)

            with if_general(sp):
                for n in range(3):
                    with sp.Fori(0, GCHUNKS) as c:
                        load_edges(c, n * GCHUNKS, n == 2)
                sp.wait_ge(s_res, len(CAND) + 1)
                sp.dma_start(out, res[:, :, :].rearrange("p k c -> p (k c)")).then_inc(s_out, 16)
                sp.wait_ge(s_out, 32)

        @block.gpsimd
        def _(gp):
            done = [0]

            def step(ins):
                done[0] += 1
                ins.then_inc(s_pool, 1)
                gp.wait_ge(s_pool, done[0])

            gp.iota(diff_i[:, :], [[1, P]], base=0, channel_multiplier=-1, allow_small_or_imprecise_dtypes=True)
            gp.iota(lo_iota[:, :], [[1, LO + 1]], base=0, channel_multiplier=0, allow_small_or_imprecise_dtypes=True)
            gp.iota(win_iota[:, :, :], [[1, P], [0, GT]], base=0, channel_multiplier=0, allow_small_or_imprecise_dtypes=True)
            gp.iota(node_id[:, :], [[P, NB]], base=0, channel_multiplier=1, allow_small_or_imprecise_dtypes=True)
            for i in range(2):
                gp.iota(pos_off[:, :].rearrange("p (s i) -> p s i", i=2)[:, :, i], [[32 * STEP, STEPS]],
                        base=32 * HALF[0] * i - 1 + 16 * HALF[i], channel_multiplier=0, allow_small_or_imprecise_dtypes=True)
            gp.iota(part[:, :], [[0, 1]], base=0, channel_multiplier=1).then_inc(s_const, 1)
            for m in (w01d, w1ind, w1dd, w02d):
                gp.memset(m[:, :, :], 0.0)
            for i in range(2):
                gp.memset(layer_in[i][:, :, 32 * PT[i]:], 0.0)
            gp.memset(w12d[:, :, :], 0.0).then_inc(s_zero, 1)
            gp.memset(end_i[:, :], NOT_FOUND).then_inc(s_zero, 1)
            gp.memset(srcq_i[:, TILES:], 0)
            gp.memset(cand[:, :, :], -BIG).then_inc(s_candf, 1)
            gp.memset(cnt[:, :, HI * LO:], 0.0)
            gp.memset(run[1][:, :], -BIG)
            gp.memset(pc[:, :, :], 0.0).then_inc(s_zero, 1)
            gp.wait_ge(s_gidx, 1)
            gp.wait_ge(s_gtab, 32)
            for c in range(CHUNKS):
                gp.indirect_dma_start(grow[:, c, :], None, g_dram[:, :], bass.IndirectOffsetOnAxis(gidx[:, c:c + 1], 0)).then_inc(s_grow0 if c < GROW0 else s_grow, 16)

            gp.wait_ge(s_winprep, 1)
            gp.wait_ge(s_endinit, 16)

            def load_count_dst(it, first):
                for i in range(2):
                    if not first:
                        gp.wait_ge(s_sgn[i], it)
                        gp.sem_inc(s_turn, 1)
                    c0 = it * (32 * STEP) + 32 * HALF[0] * i
                    w = 32 * HALF[i]
                    gp.dma_start(dcount[:, i, 0:w], windowed(dstq[:, ds(c0 + 1, w)], w)).then_inc(s_dcl[i], 16)

            def ends(it, par, first):
                at = [0]

                def link(ins):
                    at[0] += 1
                    ins.then_inc(s_endp, 1)
                    gp.wait_ge(s_endp, it * LINKS + at[0])
                    gp.sem_inc(s_turn, 1)

                for k, m in ((0, pos_off), (1, win_id), (2, ends_in)):
                    gp.tensor_copy(pc[:, k, :], m[:, ds(2 * it, 2)])
                for i in range(2):
                    gp.wait_ge(s_sgn[i], it + 1)
                    gp.sem_inc(s_turn, 1)
                link(gp.tensor_scalar(pc[:, 3, :], ssum[:, par, 0, :], -0.5, None, ALU.mult))
                link(gp.tensor_tensor(pc[:, 4, :], ssum[:, par, 1, :], ssum[:, par, 0, :], ALU.subtract))
                link(gp.tensor_scalar(pc[:, 4, :], pc[:, 4, :], 0.5, None, ALU.is_gt))
                link(gp.tensor_tensor(pc[:, 5, :], pc[:, 4, :], pc[:, 2, :], ALU.mult))
                link(gp.tensor_tensor(pc[:, 3, :], pc[:, 3, :], pc[:, 0, :], ALU.add))
                link(gp.tensor_scalar(pc[:, 6, :], pc[:, 5, :], -float(NOT_FOUND), float(NOT_FOUND), ALU.mult, ALU.add))
                link(gp.tensor_tensor(pc[:, 6, :], pc[:, 6, :], pc[:, 1, :], ALU.add))
                if not first:
                    gp.wait_ge(s_scat, it * 32)
                    gp.sem_inc(s_turn, 1)
                gp.tensor_copy(pos_i[:, :], pc[:, 3, :])
                gp.tensor_copy(pidx_i[:, :], pc[:, 6, :]).then_inc(s_used, 1)
                gp.wait_ge(s_used, it + 3)
                gp.sem_inc(s_turn, 1)
                for i in range(2):
                    gp.indirect_dma_start(end_dram[:, :], bass.IndirectOffsetOnAxis(pidx_i[:, i:i + 1], 0), pos_i[:, i:i + 1], None,
                                          bounds_check=NP - 1, oob_is_err=False).then_inc(s_scat, 16)

            LINKS = 7
            gp.sem_inc(s_used, 2)
            load_count_dst(0, True)
            load_count_dst(1, False)
            ends(0, 0, True)
            with gp.Fori(0, STEPS // 2 - 1) as it:
                for par in (1, 0):
                    load_count_dst(2 * it + (3 - par), False)
                    ends(2 * it + (2 - par), par, False)
            ends(STEPS - 1, 1, False)

            gp.wait_ge(s_htab, 16)
            with gp.Fori(0, STEPS) as it:
                for i in range(2):
                    gp.wait_ge(s_idx[i], it + 1)
                    gp.sem_inc(s_turn, 1)
                    for t in range(PT[i]):
                        gp.indirect_dma_start(rows[i][:, t, :], None, h_dram[:, :],
                                              bass.IndirectOffsetOnAxis(idx_st[i][:, t:t + 1], 0)).then_inc(s_rows[i], 16)
            gp.wait_ge(s_endidx, 1)
            gp.wait_ge(s_candf, 1)
            gp.wait_ge(s_vout[0], 16 * STEPS)
            gp.wait_ge(s_vout[1], 16 * STEPS)
            for n, (k0, k1) in enumerate(CAND):
                for k in range(k0, k1):
                    gp.indirect_dma_start(cand[:, k, :], None, v_dram[:, :], bass.IndirectOffsetOnAxis(end_idx[:, k:k + 1], 0),
                                          bounds_check=P * TILES - 1, oob_is_err=False).then_inc(s_cand[n], 16)

        @block.scalar
        def _(act):
            act.wait_ge(s_sqrt_in, 1)
            nc.scalar.activation(stat[:, 2, :], stat[:, 1, :], ACT.Sqrt).then_inc(s_sqrt, 1)
            act.wait_ge(s_shift, 1)
            nc.scalar.activation(g[:, :, 0, :], logit[:, :, :], ACT.Exp).then_inc(s_exp, 1)
            for n in range(3):
                act.wait_ge(s_gpart_in, n + 1)
                nc.scalar.activation(gs[:, :, n, :], g[:, :, :, :].rearrange("p k a c -> p k (a c)"), ACT.Copy).then_inc(s_gpart, 1)
            act.wait_ge(s_winprep, 1)

            def evac(c0, k, j0, j1, first):
                for j in range(j0, j1):
                    grp = CHUNK * (c0 + k) + j
                    if not (first and k == 0):
                        act.wait_ge(s_shuf[j], 16 * (c0 + k))
                    act.wait_ge(s_tile, GT * grp + GT)
                    nc.scalar.activation(cg[:, j, 0:LO], ps_cnt[:, j % 4, 0:LO], ACT.Copy).then_inc(s_evac, 1)

            def sign(step_, k, i, b):
                w = 32 * HALF[i]
                m = (bias_le, bias_lt)[b]
                if b == 0:
                    act.wait_ge(s_dcl[i], step_ * 16 + 16)
                if b == 0 and i == 0:
                    act.wait_ge(s_used, step_ + 1)
                last = nc.scalar.activation(sgn[i][:, w * b:w * b + w], dcount[:, i, 0:w], ACT.Sign, bias=m[:, ds(2 * step_ + i, 1)],
                                            accum_out=ssum[:, k, b, i:i + 1])
                if b == 1:
                    last.then_inc(s_sgn[i], 1)

            def act_onehot(it, k, n):
                tile = 2 * CT * it + CT * k + ACT_TILES[n]
                nc.scalar.activation(lo_dist[:, n, :], lo_iota[:, :], ACT.Square, scale=-1.0, bias=key_lo[:, ds(tile, 1)]).then_inc(s_lo_dist, 1)
                act.wait_ge(s_lo_dist, len(ACT_TILES) * (2 * it + k) + n + 1)
                nc.scalar.activation(oh_act[:, n, :], lo_dist[:, n, :], ACT.Relu, scale=-1.0, bias=ones[:, 0:1]).then_inc(s_onehot_act, 1)

            def count_pair(it, first, with_signs, groups):
                for k, n in enumerate((CHUNK, groups)):
                    for j in range(n):
                        evac(2 * it, k, j, j + 1, first)
                        if j < len(ACT_TILES) and ACT_TILES[j] < GT * n:
                            act_onehot(it, k, j)
                        if with_signs and 0 <= j - SIGNS_AT < 4:
                            sign(2 * (it - SIGNS_FROM) + k, k, (j - SIGNS_AT) // 2, (j - SIGNS_AT) % 2)

            count_pair(0, True, False, CHUNK)
            with act.Fori(1, SIGNS_FROM) as it:
                count_pair(it, False, False, CHUNK)
            with act.Fori(SIGNS_FROM, SIGNS_FROM + SIGN_PAIRS) as it:
                count_pair(it, False, True, CHUNK)
            if SIGNS_FROM + SIGN_PAIRS < PAIRS:
                with act.Fori(SIGNS_FROM + SIGN_PAIRS, PAIRS) as it:
                    count_pair(it, False, False, CHUNK)
            count_pair(PAIRS, False, False, TAIL_GROUPS)

            def root(n):
                act.wait_ge(s_sqrt_in, n)
                nc.scalar.activation(stat[:, 2, :], stat[:, 1, :], ACT.Sqrt).then_inc(s_sqrt, 1)

            def first_mlp(r):
                for f in range(2):
                    for s in range(2):
                        act.wait_ge(s_m1, 4 * r + 2 * f + s + 1)
                        nc.scalar.activation(mT[:, s, mc(f)], ps[0][:, s, 0:mw(f)], ACT.Relu, bias=b01c[:, 0:1]).then_inc(s_m1r, 1)

            act.wait_ge(s_weights0, 16 * 14)
            first_mlp(0)
            root(2)

            act.wait_ge(s_weights1, 16 * 23)

            def gathered(it, i, first):
                if not first:
                    act.wait_ge(s_pre[i], it)
                act.wait_ge(s_gat, NB * (2 * it + i + 1))
                for bank, c0, c1 in GATHER_BANKS[i]:
                    last = nc.scalar.activation(hg3[i][:, c0:c1], ps[i][0:3 * D, bank, 0:c1 - c0], ACT.Copy)
                last.then_inc(s_hg3[i], 1)

            def hidden(it, i, first):
                w = 32 * HALF[i]
                if not first:
                    act.wait_ge(s_v[i], it)
                act.wait_ge(s_pre[i], it + 1)
                for s in range(2):
                    last = nc.scalar.activation(hid[i][:, s, :], ps[i][:, 1 + s, 0:w], ACT.Relu, bias=b11c[:, 0:1])
                last.then_inc(s_hid[i], 1)

            def centred(it, i, first):
                if not first:
                    act.wait_ge(s_ohs, NB * (2 * it + i - 1))
                act.wait_ge(s_srcb[i], 16 * it + 16)
                nc.scalar.activation(srch[i], srcb[i], ACT.Copy, bias=-float(MID)).then_inc(s_srch[i], 1)

            def limits(it, i, first):
                act.wait_ge(s_same[i], it + 1)
                if not first:
                    act.wait_ge(s_run[i], it)
                nc.scalar.activation(lim[i], same[i], ACT.Copy, scale=3.4e38, bias=-1.7e38).then_inc(s_lim[i], 1)

            for i in range(2):
                centred(0, i, True)
                limits(0, i, True)
                gathered(0, i, True)
            hidden(0, 0, True)
            centred(1, 0, False)
            hidden(0, 1, True)
            limits(1, 0, False)
            gathered(1, 0, False)
            with act.Fori(1, STEPS - 1) as it:
                centred(it, 1, False)
                hidden(it, 0, False)
                limits(it, 1, False)
                gathered(it, 1, False)
                centred(it + 1, 0, False)
                hidden(it, 1, False)
                limits(it + 1, 0, False)
                gathered(it + 1, 0, False)
            centred(STEPS - 1, 1, False)
            hidden(STEPS - 1, 0, False)
            limits(STEPS - 1, 1, False)
            gathered(STEPS - 1, 1, False)
            hidden(STEPS - 1, 1, False)

            with if_general(act):
                root(3)
                with act.Fori(0, GCHUNKS) as c:
                    act.wait_ge(s_gdiff, c + 1)
                    nc.scalar.activation(g_exp[:, :], g_diff[:, :], ACT.Exp).then_inc(s_gexp, 1)
                first_mlp(1)
                root(4)
                with act.Fori(0, GCHUNKS) as c:
                    act.wait_ge(s_gpre, c + 1)
                    nc.scalar.activation(g_hid[0:H, :], ps[0][0:H, 1, 0:GE], ACT.Relu, bias=b11c[0:H, 0:1]).then_inc(s_ghid, 1)

        @block.tensor
        def _(pe):
            pe.wait_ge(s_ext, 1)
            nc.tensor.transpose(ps[0][0:H, 0, 0:P], ext[:, :, :].rearrange("p a c -> p (a c)"), ident[:, :]).then_inc(s_extT, 1)
            pe.wait_ge(s_topd, 1)
            nc.tensor.matmul(ps[0][:, 1, 0:H], ones[0:H, :], topd[:, :], start=True, stop=True).then_inc(s_topb, 1)
            for b in range(4):
                nc.tensor.matmul(ps[1][:, b, :], zero_b[:, 0:P], zero_b[:, :], start=True, stop=False, skip_group_check=True)

            def count_tile(c0, u, first):
                if u % GT == 0 and not (first and u < 4 * GT):
                    pe.wait_ge(s_evac, CHUNK * c0 + u // GT - 3)
                taken = sum(t % CT in ACT_TILES for t in range(u + 1))
                pe.wait_ge(s_onehot, (CT - len(ACT_TILES)) * c0 + u + 1 - taken)
                moving = oh_lo[:, u % RING, 0:LO]
                if u % CT in ACT_TILES:
                    pe.wait_ge(s_onehot_act, len(ACT_TILES) * c0 + taken)
                    moving = oh_act[:, ACT_TILES.index(u % CT), 0:LO]
                nc.tensor.matmul(ps_cnt[:, (u // GT) % 4, 0:LO], oh_win[:, (u // GT) % RING_W, :, u % GT], moving,
                                 start=(u % GT == 0), stop=(u % GT == GT - 1)).then_inc(s_tile, 1)

            def sum_blocks(c, k, b0, b1):
                for b in range(b0, b1):
                    for part_ in range(3):
                        last = nc.tensor.matmul(ps_sum[:, b, :], cnt[:, k, P * b:P * b + P], grow_of(c)[:, H * part_:H * part_ + H],
                                                start=False, stop=False, skip_group_check=True)
                if b1 == NB:
                    last.then_inc(s_chunk, 1)

            def grow_of(c):
                return grow[:, ds(c, 1), :].rearrange("p a n -> p (a n)")

            def chunk_ready(c):
                for r in range(CHUNK):
                    pe.wait_ge(s_shuf[r], 16 * (c + 1))

            def count_chunk(c0, k, tiles, first, start=True):
                late = tiles // 2 + LATE
                for u in range(tiles):
                    count_tile(c0, u + CT * k, first and start)
                    if first and start and k == 0 or u < late:
                        continue
                    if u == late:
                        if first:
                            pe.wait_ge(s_grow0, 16 * GROW0)
                            pe.wait_ge(s_zero, 3)
                        else:
                            pe.wait_ge(s_grow, 16 * (CHUNKS - GROW0))
                        chunk_ready(c0 + k - 1)
                    n = tiles - late
                    sum_blocks(c0 + k - 1, (k + 1) % 2, NB * (u - late) // n, NB * (u - late + 1) // n)

            count_chunk(0, 0, CT, True)
            count_chunk(0, 1, CT, True)
            for c0 in range(2, GROW0, 2):
                count_chunk(c0, 0, CT, True, False)
                count_chunk(c0, 1, CT, True, False)
            with pe.Fori((GROW0 + 1) // 2, PAIRS) as it:
                count_chunk(2 * it, 0, CT, False)
                count_chunk(2 * it, 1, CT, False)
            count_chunk(2 * PAIRS, 0, CT, False)
            count_chunk(2 * PAIRS, 1, GT * TAIL_GROUPS, False)
            for r in range(TAIL_GROUPS):
                pe.wait_ge(s_shuf[r], 16 * CHUNKS)
            sum_blocks(CHUNKS - 1, (CHUNKS - 1) % 2, 0, NB)

            def first_mlp(r):
                for f in range(2):
                    pe.wait_ge(s_h0T, 2 * r + f + 1)
                    for s in range(2):
                        if f:
                            pe.wait_ge(s_m1r, 4 * r + s + 1)
                        nc.tensor.matmul(ps[0][:, s, 0:mw(f)], w01d[:, s, :], hT[:, mc(f)], start=True, stop=True).then_inc(s_m1, 1)
                for f in range(2):
                    pe.wait_ge(s_m1r, 4 * r + 2 * f + 2)
                    for s in range(2):
                        last = nc.tensor.matmul(ps[0][64 * s:64 * s + 64, 2 + f, 0:mw(f)], w02d[:, s, 64 * s:64 * s + 64], mT[:, s, mc(f)], start=True, stop=True)
                    last.then_inc(s_m2, 1)

            pe.wait_ge(s_broken, 1)
            nc.tensor.matmul(ps_broken, ones[:, 0:1], broken[:, :], start=True, stop=True).then_inc(s_count, 1)

            pe.wait_ge(s_weights0, 16 * 14)
            first_mlp(0)
            pe.wait_ge(s_hT, 1)
            pe.wait_ge(s_weights1, 16 * 23)
            for k in range(NB):
                m, kk = k // 4, k % 4
                last = nc.tensor.matmul(ps[1][:, :, :].rearrange("p a b -> p (a b)")[32 * kk:32 * kk + 32, 4 * H * m:4 * H * m + 4 * H],
                                        hT[:, 32 * k:32 * k + 32], w1dd[:, :, :].rearrange("p s c -> p (s c)"), start=True, stop=True, skip_group_check=True)
            for kk in range(NB % 4, 4):
                last = nc.tensor.matmul(ps[1][:, :, :].rearrange("p a b -> p (a b)")[32 * kk:32 * kk + 32, 4 * H * (NB4 - 1):4 * H * NB4],
                                        zero_b[:, 0:32], zero_b[:, 0:4 * H], start=True, stop=True, skip_group_check=True)
            last.then_inc(s_bmm, 1)

            def gather(it, i, k0, k1, first):
                if k0 == 0 and not first:
                    pe.wait_ge(s_hg3[i], it)
                for k in range(k0, k1):
                    pe.wait_ge(s_ohs, NB * (2 * it + i) + k + 1)
                    for bank, c0, c1 in GATHER_BANKS[i]:
                        last = nc.tensor.matmul(ps[i][0:3 * D, bank, 0:c1 - c0], h3[:, k, :, :].rearrange("p s c -> p (s c)"),
                                                oh_src[:, k % RING_S, c0:c1], start=(k == 0), stop=(k == NB - 1))
                    last.then_inc(s_gat, 1)

            def layers(it, i, first, beside=None):
                w, wp, pw = 32 * HALF[i], 32 * PT[i], PW[i]
                add = dict(start=False, stop=False, skip_group_check=True)
                if not first:
                    pe.wait_ge(s_hid[i], it)
                    pe.wait_ge(s_run[i], it)
                pe.wait_ge(s_wrow[i], 64 * it + 64)
                pe.wait_ge(s_ohd[i], it + 1)
                for s in range(2):
                    for t in range(3):
                        nc.tensor.matmul(ps[i][:, 1 + s, 0:w], wins[:, i, s, t, :], ohd[i], start=(t == 0), stop=False, skip_group_check=True)
                pe.wait_ge(s_hg3[i], it + 1)
                for q in range(4):
                    nc.tensor.matmul(ps[i][64 * (q % 2):64 * (q % 2) + 64, 1 + q // 2, wp:w], w1s3[:, :], hg3[i][:, pw * q:pw * q + pw], **add)
                pe.wait_ge(s_ea[i], 32 * it + 32)
                pe.wait_ge(s_idx[i], it + 2)
                for s in range(2):
                    last = nc.tensor.matmul(ps[i][:, 1 + s, 0:w], w1ind[:, s, :], layer_in[i][:, s, :], **add)
                last.then_inc(s_pre[i], 1)
                if beside:
                    gather(beside[0], beside[1], 0, EARLY, beside[2])
                pe.wait_ge(s_hid[i], it + 1)
                for s in range(2):
                    last = nc.tensor.matmul(ps[i][64 * s:64 * s + 64, 1, 0:w], w12d[:, s, 64 * s:64 * s + 64], hid[i][:, s, :], start=True, stop=True)
                last.then_inc(s_v[i], 1)
                if beside:
                    gather(beside[0], beside[1], EARLY, NB, beside[2])

            pe.wait_ge(s_h3, 1)
            gather(0, 0, 0, NB, True)
            pe.wait_ge(s_b3, 1)
            gather(0, 1, 0, NB, True)
            layers(0, 0, True)
            layers(0, 1, True, (1, 0, False))
            with pe.Fori(1, STEPS - 1) as it:
                layers(it, 0, False, (it, 1, False))
                layers(it, 1, False, (it + 1, 0, False))
            layers(STEPS - 1, 0, False, (STEPS - 1, 1, False))
            layers(STEPS - 1, 1, False)

            with if_general(pe):
                first_mlp(1)
                pe.wait_ge(s_h1, 2)
                with pe.Fori(0, GCHUNKS) as c:
                    pe.wait_ge(s_gea, 16 * c + 16)
                    nc.tensor.transpose(ps[0][0:D, 0, 0:GE], g_ea[:, :], ident[0:GE, 0:GE]).then_inc(s_geaT, 1)
                    pe.wait_ge(s_gin, c + 1)
                    nc.tensor.matmul(ps[0][0:H, 1, 0:GE], w11f[:, :], g_in[:, :], start=True, stop=True).then_inc(s_gpre, 1)
                    pe.wait_ge(s_ghid, c + 1)
                    nc.tensor.matmul(ps[0][:, 2, 0:GE], w12d[:, 0, :], g_hid[:, :], start=True, stop=True).then_inc(s_gv, 1)

        @block.vector
        def _(ve):
            done = [0]
            V = nc.vector

            def step(ins):
                done[0] += 1
                ins.then_inc(s_dve, 1)
                ve.wait_ge(s_dve, done[0])

            def bc(col):
                return col.rearrange("p (k o) -> p k o", o=1).to_broadcast([P, NB, D])

            def chan(row):
                return row.rearrange("p (o c) -> p o c", o=1).to_broadcast([P, NB, D])

            def norm_relu(src, n):
                step(V.reduce_sum(stat[:, 0, :], src, AX))
                step(V.tensor_scalar(stat[:, 0, :], stat[:, 0, :], 1.0 / D, None, ALU.mult))
                step(V.tensor_tensor(xc[:, :, :], src, bc(stat[:, 0, :]), ALU.subtract))
                step(V.tensor_tensor(sq[:, :, :], xc[:, :, :], xc[:, :, :], ALU.mult))
                step(V.reduce_sum(stat[:, 1, :], sq[:, :, :], AX))
                V.tensor_scalar(stat[:, 1, :], stat[:, 1, :], 1.0 / D, LN_EPS, ALU.mult, ALU.add).then_inc(s_sqrt_in, 1)
                ve.wait_ge(s_sqrt, n)
                step(V.reciprocal(stat[:, 3, :], stat[:, 2, :]))
                return V.scalar_tensor_tensor(h[:, :, :], xc[:, :, :], 0.0, bc(stat[:, 3, :]), ALU.max, ALU.mult)

            V.memset(ones[:, :], 1.0)
            V.memset(zero_b[:, :], 0.0)
            ve.wait_ge(s_const, 1)
            step(V.tensor_scalar(ident[:, :], diff_i[:, :], 0.0, None, ALU.is_equal))
            ve.wait_ge(s_x, 32)
            step(norm_relu(x[:, :, :], 1))
            step(V.tensor_scalar(h[:, :, :], h[:, :, :], MSG_EPS, None, ALU.add))
            step(V.tensor_scalar(logit[:, :, :], h[:, :, :], betac[:, 0:1], None, ALU.mult))
            step(V.tensor_scalar(sq[:, :, :], logit[:, :, :], -1.0, None, ALU.mult))
            step(V.reduce_max(ext[:, 0, :], logit[:, :, :].rearrange("p k c -> p c k"), AX))
            V.reduce_max(ext[:, 1, :], sq[:, :, :].rearrange("p k c -> p c k"), AX).then_inc(s_ext, 1)
            ve.wait_ge(s_extT, 1)
            step(V.reduce_max(top[:, :], ps[0][0:H, 0, 0:P], AX))
            V.tensor_scalar(topd[:, :], ident[0:H, 0:H], top[:, 0:1], None, ALU.mult).then_inc(s_topd, 1)
            ve.wait_ge(s_topb, 1)
            step(V.tensor_copy(topb[:, :, :].rearrange("p a c -> p (a c)"), ps[0][:, 1, 0:H]))
            V.tensor_tensor(logit[:, :, :], logit[:, :, :], chan(topb[:, 0, :]), ALU.subtract).then_inc(s_shift, 1)
            ve.wait_ge(s_exp, 1)
            step(V.tensor_tensor(g[:, :, 1, :], g[:, :, 0, :], h[:, :, :], ALU.mult))
            gf = g[:, :, :, :].rearrange("p k a c -> p k (a c)")
            def rounded(n):
                ve.sem_inc(s_gpart_in, 1)

            def remainder(n):
                ve.wait_ge(s_gpart, n + 1)
                step(V.tensor_tensor(gf, gf, gs[:, :, n, :], ALU.subtract))
                rounded(n + 1)

            rounded(0)
            ve.wait_ge(s_edges, 48)
            step(V.tensor_copy(srcf, src_i))
            step(V.tensor_scalar(hi, srcf, 1.0 / LO, 0.5 / LO - 0.5, ALU.mult, ALU.add))
            step(V.tensor_scalar(hi, hi, ROUND, None, ALU.add))
            step(V.tensor_scalar(hi, hi, ROUND, None, ALU.subtract))
            remainder(0)
            step(V.scalar_tensor_tensor(key_lo, hi, -float(LO), srcf, ALU.mult, ALU.add))
            step(V.tensor_tensor(key_win.rearrange("p (g t) -> p g t", t=GT), dst_i.rearrange("p (g t) -> p g t", t=GT),
                                 base0_i[:, :].rearrange("p (g o) -> p g o", o=1).to_broadcast([P, GROUPS, GT]), ALU.subtract))
            remainder(1)
            step(V.scalar_tensor_tensor(key_win16, key_win, float(HI), hi, ALU.mult, ALU.add))

            ve.wait_ge(s_win, 16 * (CHUNK + 9))
            step(V.tensor_scalar(part16[:, :], part[:, :], W0 - 1, None, ALU.bitwise_and))
            step(V.tensor_scalar(part32[:, :], part[:, :], W1 - 1, None, ALU.bitwise_and))
            step(V.tensor_copy(part16f[:, :], part16[:, :]))
            step(V.tensor_copy(part32f[:, :], part32[:, :]))
            V.tensor_scalar(gidx[:, :], gidx_b[:, :], part16f[:, 0:1], float(NP), ALU.add, ALU.min).then_inc(s_gidx, 1)
            step(V.tensor_scalar(base1c[:, :], base1r[:, :], float(N - W1), None, ALU.min))
            V.tensor_scalar(base1c[:, :], base1c[:, :], 0.0, None, ALU.max).then_inc(s_base1c, 1)
            step(V.tensor_scalar(win_id[:, :], base1_i[:, :], float(N - W1), part32f[:, 0:1], ALU.min, ALU.add))
            step(V.tensor_tensor(ends_in[:, :], next1_i[:, :], win_id[:, :], ALU.is_gt))
            step(V.tensor_scalar(bias_le[:, :], win_id[:, :], -1.0, -0.5, ALU.mult, ALU.add))
            step(V.tensor_scalar(part32[:, :], part[:, :], 5, 15, ALU.arith_shift_right, ALU.logical_shift_left))
            step(V.tensor_copy(part16f[:, :], part32[:, :]))
            step(V.tensor_scalar(pos_off[:, :], pos_off[:, :], part16f[:, 0:1], None, ALU.add))
            V.tensor_scalar(bias_lt[:, :], win_id[:, :], -1.0, 0.5, ALU.mult, ALU.add).then_inc(s_winprep, 1)

            def stage(it, i):
                return V.tensor_copy(idx_st[i][:, :], srcq_i[:, ds(it * STEP + HALF[0] * i, PT[i])])

            ve.wait_ge(s_srcq, 32)
            ve.wait_ge(s_zero, 3)
            for i in range(2):
                stage(0, i).then_inc(s_idx[i], 1)
            step(V.tensor_scalar(mid_id[:, :], node_id[:, :], float(MID), None, ALU.subtract))
            def onehots(it, tiles, first):
                for u in range(tiles):
                    if u % GT == 0:
                        if not (first and u < RING_W * GT):
                            ve.wait_ge(s_tile, 2 * CT * it + u - (RING_W - 1) * GT)
                        V.tensor_tensor(oh_win[:, (u // GT) % RING_W, :, :], win_iota[:, :, :],
                                        key_win16[:, ds(2 * CT * it + u, GT)].rearrange("p (o t) -> p o t", o=1).to_broadcast([P, P, GT]), ALU.is_equal)
                    if u % CT in ACT_TILES:
                        continue
                    if not (first and u < RING):
                        ve.wait_ge(s_tile, 2 * CT * it + u - (RING - 1))
                    V.tensor_scalar(oh_lo[:, u % RING, :], lo_iota[:, :], key_lo[:, ds(2 * CT * it + u, 1)], None, ALU.is_equal).then_inc(s_onehot, 1)

            onehots(0, 2 * CT, True)
            with ve.Fori(1, PAIRS) as it:
                onehots(it, 2 * CT, False)
            onehots(PAIRS, CT + GT * TAIL_GROUPS, False)

            step(V.memset(broken[:, :], 0.0))
            ve.wait_ge(s_bounds, 112)
            step(V.tensor_tensor(wide0[:, :], last0_i[:, :], base0_r[:, :], ALU.subtract))
            step(V.tensor_scalar(wide0[:, :], wide0[:, :], float(W0 - 1), None, ALU.is_gt))
            step(V.tensor_tensor(wide1[:, :], last1_i[:, :], base1c[:, :], ALU.subtract))
            step(V.tensor_scalar(wide1[:, :], wide1[:, :], float(W1 - 1), None, ALU.is_gt))
            step(V.tensor_tensor(order_f[:, 0:n_order], order_i[:, 0, :], order_i[:, 1, :], ALU.is_gt))
            step(V.tensor_tensor(wide2[:, :], topb[0:1, 0, :], topb[0:1, 1, :], ALU.add))
            step(V.tensor_scalar(wide2[:, :], wide2[:, :], RANGE, None, ALU.is_gt))
            step(V.tensor_tensor(far_f, far_i[:, 0, :], far_i[:, 1, :], ALU.is_equal))
            step(V.reduce_sum(broken[:, 4:5], far_f, AX))
            step(V.reduce_sum(broken[0:1, 0:1], wide0[:, :], AX))
            step(V.reduce_sum(broken[0:1, 1:2], wide1[:, :], AX))
            step(V.reduce_sum(broken[0:127, 2:3], order_f[:, 0:n_order], AX))
            V.reduce_sum(broken[0:1, 3:4], wide2[:, :], AX).then_inc(s_broken, 1)
            ve.wait_ge(s_endld, 16)
            step(V.tensor_scalar(end_t[:, 0, :], end_i[:, :], 15, None, ALU.arith_shift_right))
            step(V.tensor_scalar(end_t[:, 1, :], end_i[:, :], 31, None, ALU.bitwise_and))
            step(V.tensor_scalar(end_t[:, 2, :], end_i[:, :], (1 << 15) - 1, None, ALU.bitwise_and))
            step(V.tensor_scalar(end_t[:, 2, :], end_t[:, 2, :], 5, None, ALU.arith_shift_right))
            step(V.tensor_copy(end_f[:, 0:3, :], end_t[:, :, :]))
            step(V.scalar_tensor_tensor(end_f[:, 3, :], end_f[:, 0, :], 32.0, end_f[:, 1, :], ALU.mult, ALU.add))
            V.scalar_tensor_tensor(end_idx[:, :], end_f[:, 3, :], float(TILES), end_f[:, 2, :], ALU.mult, ALU.add).then_inc(s_endidx, 1)
            ve.wait_ge(s_srcq, 32)
            step(V.tensor_copy(edge_nf[:, :], edge_n[:, :]))
            for q in range(3):
                step(V.tensor_scalar(edge_p[:, q, :], node_id[:, :], edge_nf[:, q:q + 1], None, ALU.is_equal))
            step(V.tensor_scalar(edge_p[:, :, :], edge_p[:, :, :], 1.0, BIG, ALU.subtract, ALU.mult))

            ve.wait_ge(s_chunk, CHUNKS)
            step(V.tensor_scalar(sq[:, :, :], ps_sum[:, :, 0:D], 1e-38, None, ALU.max))
            ve.wait_ge(s_count, 1)
            step(V.reduce_sum(flag_f[:, :], ps_broken, AX))
            V.tensor_copy(flag[:, :], flag_f[:, :]).then_inc(s_flag, 1)
            for k0, k1 in MLP_BLOCKS:
                step(V.reciprocal(logit[:, k0:k1, :], sq[:, k0:k1, :]))
                step(V.tensor_tensor(xc[:, k0:k1, :], ps_sum[:, k0:k1, D:2 * D], logit[:, k0:k1, :], ALU.mult))
                V.transpose(hT[:, D * k0:D * k1], xc[:, k0:k1, :].rearrange("p k c -> p (k c)")).then_inc(s_h0T, 1)

            def after_mlp(r):
                for f in range(2):
                    ve.wait_ge(s_m2, 2 * r + f + 1)
                    step(V.tensor_scalar(mT[:, 0, mc(f)], ps[0][:, 2 + f, 0:mw(f)], b02c[:, 0:1], None, ALU.add))
                step(V.transpose(sq[:, :, :].rearrange("p k c -> p (k c)"), mT[:, 0, :]))
                step(V.tensor_tensor(x1[:, :, :], sq[:, :, :], x[:, :, :], ALU.add))
                norm_relu(x1[:, :, :], 2 * r + 2).then_inc(s_h1, 1)

            ve.wait_ge(s_weights0, 16 * 14)
            ve.wait_ge(s_gtab, 32)
            V.memset(wins, 0.0).then_inc(s_winz, 1)
            after_mlp(0)

            def three_parts(parts, value):
                step(V.tensor_copy(parts[0], value))
                step(V.tensor_tensor(value, value, parts[0], ALU.subtract))
                step(V.tensor_copy(parts[1], value))
                step(V.tensor_tensor(value, value, parts[1], ALU.subtract))
                return V.tensor_copy(parts[2], value)

            ve.wait_ge(s_h1, 1)
            V.transpose(hT[:, :], h[:, :, :].rearrange("p k c -> p (k c)")).then_inc(s_hT, 1)
            step(V.tensor_copy(sq[:, :, :], h[:, :, :]))
            three_parts([h3[:, :, t, :] for t in range(3)], sq[:, :, :]).then_inc(s_h3, 1)
            ve.wait_ge(s_bmm, 1)
            step(V.tensor_copy(bf, ps[1][:, :, :].rearrange("p a b -> p (a b)")[:, 0:NB4 * 4 * H]))
            three_parts([b3[:, :, t, :] for t in range(3)], bf.rearrange("p (m c) -> p m c", c=H)).then_inc(s_b3, 1)



            def finish(k0, k1, floor):
                w = k1 - k0
                step(V.tensor_tensor(cand[:, k0:k1, :], cand[:, k0:k1, :], b12r[:, :].rearrange("p (o c) -> p o c", o=1).to_broadcast([P, w, D]), ALU.add))
                step(V.tensor_tensor(cand[:, k0:k1, :], cand[:, k0:k1, :], floor[:, k0:k1, :], ALU.max))
                return V.tensor_tensor(res[:, k0:k1, :], cand[:, k0:k1, :], x1[:, k0:k1, :], ALU.add)

            def last_use(slot):
                return max(k for k in range(NB) if k % RING_S == slot)

            def prepare(it, i, first):
                w = 32 * HALF[i]
                ve.wait_ge(s_dst[i], 16 * it + 16)
                if not first:
                    ve.wait_ge(s_pre[i], it)
                    ve.wait_ge(s_lim[i], it)
                V.tensor_scalar(ohd[i], dstb[i][:, 1:w + 1], win_id[:, ds(2 * it + i, 1)], None, ALU.is_equal).then_inc(s_ohd[i], 1)
                V.tensor_tensor(same[i], dstb[i][:, 1:w + 1], dstb[i][:, 0:w], ALU.is_equal).then_inc(s_same[i], 1)
                ve.wait_ge(s_srch[i], it + 1)
                for k in range(NB):
                    if not (first and i == 0 and k < RING_S):
                        ve.wait_ge(s_gat, NB * (2 * it + i) + (k - (RING_S - 1) if k >= RING_S else last_use(k) + 1 - NB))
                    V.tensor_scalar(oh_src[:, k % RING_S, 0:4 * PW[i]], srch[i], mid_id[:, k:k + 1], None, ALU.is_equal).then_inc(s_ohs, 1)

            def turned(it, i, first):
                if not first:
                    ve.wait_ge(s_pre[i], it)
                ve.wait_ge(s_rows[i], (16 * PT[i]) * (it + 1))
                for s in range(2):
                    V.transpose(layer_in[i][64 * s:64 * s + 64, s, 0:32 * PT[i]], rows[i][64 * s:64 * s + 64, 0:PT[i], :].rearrange("p t c -> p (t c)"))
                stage(it + 1, i).then_inc(s_idx[i], 1)

            def scan(it, i, first):
                w = 32 * HALF[i]
                if i == 1:
                    ve.wait_ge(s_run[0], it + 1)
                elif not first:
                    ve.wait_ge(s_run[1], it)
                ve.wait_ge(s_lim[i], it + 1)
                ve.wait_ge(s_v[i], it + 1)
                V.tensor_tensor_scan(run[i][:, :], lim[i], ps[i][:, 1, 0:w],
                                     run[1 - i][:, 32 * HALF[1 - i] - 1:32 * HALF[1 - i]], ALU.min, ALU.max).then_inc(s_run[i], 1)
                if not first:
                    ve.wait_ge(s_vout[i], 16 * it)
                ve.wait_ge(s_run[i], it + 1)
                V.transpose(vrow[i][:, :], run[i][:, :]).then_inc(s_vrow[i], 1)

            prepare(0, 0, True)
            turned(0, 0, True)
            prepare(0, 1, True)
            turned(0, 1, True)
            scan(0, 0, True)
            prepare(1, 0, False)
            turned(1, 0, False)
            scan(0, 1, True)
            prepare(1, 1, False)
            with ve.Fori(1, STEPS - 1) as it:
                turned(it, 1, False)
                scan(it, 0, False)
                prepare(it + 1, 0, False)
                turned(it + 1, 0, False)
                scan(it, 1, False)
                prepare(it + 1, 1, False)
            turned(STEPS - 1, 1, False)
            scan(STEPS - 1, 0, False)
            scan(STEPS - 1, 1, False)

            ve.wait_ge(s_edgev, 48)
            ve.wait_ge(s_weights1, 16 * 23)
            for q in range(3):
                step(V.tensor_tensor(tmp[:, q, :, :], bc(edge_p[:, q, :]), chan(edge_v[:, q, :]), ALU.add))
            for q in range(1, 3):
                step(V.tensor_tensor(tmp[:, 0, :, :], tmp[:, 0, :, :], tmp[:, q, :, :], ALU.max))
            step(V.tensor_tensor(tmp[:, 0, :, :], tmp[:, 0, :, :], chan(b12r[:, :]), ALU.add))
            step(V.tensor_tensor(tmp[:, 0, :, :], tmp[:, 0, :, :], h[:, :, :], ALU.max))
            for n, (k0, k1) in enumerate(CAND):
                ve.wait_ge(s_cand[n], 16 * (k1 - k0))
                finish(k0, k1, tmp[:, 0, :, :]).then_inc(s_res, 1)

            def columns(table, q):
                return table.rearrange("c (k q r) -> c k q r", q=4, r=32)[:, :, q, :]

            def quad(q):
                return hT[32 * q:32 * q + 32, :].rearrange("c (k r) -> c k r", r=32)

            def rows_to_table(rows_, table):
                step(V.transpose(hT[:, :], rows_.rearrange("p k c -> p (k c)")))
                for q in range(4):
                    step(V.tensor_copy(columns(table, q), quad(q)))

            def table_to_quads(table):
                for q in range(4):
                    last = V.tensor_copy(quad(q), columns(table, q))
                return last

            def edges(body):
                ve.sem_inc(s_gturn, 1)
                with ve.Fori(0, GE) as j:
                    body(j, ve.value_load(g_src[0:1, ds(j, 1)], min_val=0, max_val=N - 1),
                         ve.value_load(g_dst[0:1, ds(j, 1)], min_val=0, max_val=N - 1))

            with if_general(ve):
                ve.sem_inc(s_gused, 1)
                step(norm_relu(x[:, :, :], 3))
                step(V.tensor_scalar(h[:, :, :], h[:, :, :], MSG_EPS, None, ALU.add))
                rows_to_table(h[:, :, :], feat)
                V.memset(g_hid[:, :], 0.0)
                V.memset(total, 0.0)
                V.memset(wsum, 0.0)
                step(V.memset(peak, -BIG))
                with ve.Fori(0, GCHUNKS) as c:
                    ve.wait_ge(s_gidx3[0], 32 * c + 32)

                    def largest(j, s, d):
                        V.scalar_tensor_tensor(peak[:, ds(s, 1)], feat[:, ds(d, 1)], betac[0:D, 0:1], peak[:, ds(s, 1)], ALU.mult, ALU.max)
                        ve.drain()

                    edges(largest)
                    ve.sem_inc(s_gused, 1)
                with ve.Fori(0, GCHUNKS) as c:
                    ve.wait_ge(s_gidx3[1], 32 * c + 32)

                    def shifted(j, s, d):
                        V.scalar_tensor_tensor(g_diff[:, ds(j, 1)], feat[:, ds(d, 1)], betac[0:D, 0:1], peak[:, ds(s, 1)], ALU.mult, ALU.subtract)

                    def summed(j, s, d):
                        V.tensor_tensor(total[:, ds(s, 1)], total[:, ds(s, 1)], g_exp[:, ds(j, 1)], ALU.add)
                        V.scalar_tensor_tensor(wsum[:, ds(s, 1)], feat[:, ds(d, 1)], g_exp[:, ds(j, 1)], wsum[:, ds(s, 1)], ALU.mult, ALU.add)
                        ve.drain()

                    edges(shifted)
                    ve.drain()
                    ve.sem_inc(s_gdiff, 1)
                    ve.wait_ge(s_gexp, c + 1)
                    edges(summed)
                    ve.sem_inc(s_gused, 1)
                step(V.tensor_scalar(total, total, 1e-38, None, ALU.max))
                step(V.reciprocal(total, total))
                step(V.tensor_tensor(wsum, wsum, total, ALU.mult))
                table_to_quads(wsum).then_inc(s_h0T, 2)
                after_mlp(1)
                ve.wait_ge(s_h1, 2)
                rows_to_table(h[:, :, :], feat)
                step(V.memset(peak, -BIG))
                with ve.Fori(0, GCHUNKS) as c:
                    ve.wait_ge(s_gidx3[2], 32 * c + 32)

                    def fill(j, s, d):
                        V.tensor_copy(g_in[0:D, ds(j, 1)], feat[:, ds(s, 1)])
                        V.tensor_copy(g_in[D:2 * D, ds(j, 1)], feat[:, ds(d, 1)])

                    def maximum(j, s, d):
                        V.tensor_tensor(peak[:, ds(d, 1)], peak[:, ds(d, 1)], ps[0][0:D, 2, ds(j, 1)], ALU.max)
                        ve.drain()

                    edges(fill)
                    ve.wait_ge(s_geaT, c + 1)
                    V.tensor_copy(g_in[2 * D:3 * D, :], ps[0][0:D, 0, 0:GE])
                    ve.drain()
                    ve.sem_inc(s_gin, 1)
                    ve.wait_ge(s_gv, c + 1)
                    edges(maximum)
                    ve.sem_inc(s_gused, 1)
                step(table_to_quads(peak))
                step(V.transpose(cand[:, :, :].rearrange("p k c -> p (k c)"), hT[:, :]))
                finish(0, NB, h[:, :, :]).then_inc(s_res, 1)


def kernel(**inputs):
    import numpy as np
    import concourse.bacc as bacc
    from concourse import mybir as mb
    from concourse.bass_utils import run_bass_kernel_spmd as launch

    a = {k: np.ascontiguousarray(v) for k, v in inputs.items()}
    x, src, dst, ea = a["x"], a["src"], a["dst"], a["edge_attr_32"]
    i32 = dst.dtype
    src_p = np.concatenate([src, np.zeros(EPAD - E, i32)])
    dst_p = np.concatenate([dst, np.full(EPAD - E + 1, NO_DST, i32)])
    ea_p = np.concatenate([ea, np.zeros((EPAD - E, D), ea.dtype)])
    x_p = np.concatenate([x, np.zeros((NP - N, D), x.dtype)])
    starts0 = [GT * P * k for k in range(GROUPS)]
    ends0 = [min(s + GT * P, E) - 1 for s in starts0]
    starts1 = [[Q * q + 32 * (STEP * (n // 2) + HALF[0] * (n % 2)) for n in range(HALVES)] for q in range(4)]
    ends1 = [[min(s + 32 * HALF[n % 2], E) - 1 for n, s in enumerate(row)] for row in starts1]
    nexts1 = [[s + 32 * HALF[n % 2] for n, s in enumerate(row)] for row in starts1]
    base0 = dst_p[starts0]
    arrays = {
        "xb": x_p.reshape(NB, P, D).transpose(1, 0, 2).reshape(P, NB * D),
        "src0": np.concatenate([src_p, np.zeros(P * ATILES - EPAD, i32)]).reshape(ATILES, P).T,
        "dst0": np.concatenate([dst_p[:-1], np.full(P * ATILES - EPAD, NO_DST, i32)]).reshape(ATILES, P).T,
        "srcs": src_p.reshape(4, Q),
        "srcq": src_p.reshape(4, TILES, 32).transpose(0, 2, 1).reshape(P, TILES),
        "dstq": np.stack([np.concatenate([np.full(1, -1, i32) if q == 0 else dst_p[Q * q - 1:Q * q], dst_p[Q * q:Q * q + Q]]) for q in range(4)]),
        "eat": ea_p.reshape(4, Q, D).transpose(0, 2, 1).reshape(P, Q),
        "base0": base0, "base0c": np.concatenate([base0, np.full(CHUNK * CHUNKS - GROUPS, NO_DST, i32)]).reshape(CHUNKS, CHUNK).T,
        "last0": dst_p[ends0], "base1": dst_p[starts1], "last1": dst_p[ends1], "next1": dst_p[nexts1],
        "slast": dst_p[[Q * q + Q - 1 for q in range(3)]],
        "dstp": dst_p[:-1], "src": src, "dst": dst, "ea": ea,
        "beta": a["L0_gnn_beta"], "w01": a["L0_gnn_W1"], "b01": a["L0_gnn_b1"], "w02": a["L0_gnn_W2"], "b02": a["L0_gnn_b2"],
        "w11": a["L1_gnn_W1"], "b11": a["L1_gnn_b1"], "w12": a["L1_gnn_W2"], "b12": a["L1_gnn_b2"],
    }
    nc = bacc.Bacc("TRN2", target_bir_lowering=False, num_devices=1)
    feeds, aps = {}, {}
    for name, v in arrays.items():
        v = np.ascontiguousarray(v)
        feeds[f"in_{name}"] = v
        aps[name] = nc.dram_tensor(f"in_{name}", v.shape, mb.dt.from_np(v.dtype), kind="ExternalInput").ap()
    out = nc.dram_tensor("out_0", (P, NB * D), mb.dt.float32, kind="ExternalOutput").ap()
    build(nc, **aps, out=out)
    got = launch(nc, [feeds], core_ids=[0]).results[0]["out_0"]
    return got.reshape(P, NB, D).transpose(1, 0, 2).reshape(NP, D)[:N]
```
